# Optimizing a Trainium2 kernel written in Bass

```python
import numpy as np
import jax
import jax.numpy as jnp

def _softmax(x, axis=-1):
    return jax.nn.softmax(x, axis=axis)

def _gelu(x):
    return jax.nn.gelu(x, approximate=True)

def _silu(x):
    return jax.nn.silu(x)

def _sigmoid(x):
    return jax.nn.sigmoid(x)

def _layernorm(x, axis=-1, eps=1e-05):
    m = jnp.mean(x, axis=axis, keepdims=True)
    v = jnp.var(x, axis=axis, keepdims=True)
    return (x - m) / jnp.sqrt(v + eps)

def _scatter_add(tgt, idx, src, axis=0):
    return tgt.at[idx].add(src)

def _segment_sum(src, seg, n):
    return jax.ops.segment_sum(src, seg, n)
kernel_name = 'mk_decoder_postln_d1_seqx_r8_4e3a69'

def setup_inputs(seed: int=0):
    np.random.seed(seed)
    _w = jnp.asarray

    def _rec_inputs():
        import jax
        import jax.numpy as jnp
        _rk = jax.random.key(seed)
        x = -0.0003929 + 0.9999 * jax.random.normal(jax.random.fold_in(_rk, 1), (64, 128, 128), jnp.float32)
        _lenS = 128 - jax.random.randint(jax.random.fold_in(_rk, 7), (64,), 0, max(1, 128 // 4) + 1, jnp.int32)
        _lenS2 = 77 - jax.random.randint(jax.random.fold_in(_rk, 8), (64,), 0, max(1, 77 // 4) + 1, jnp.int32)
        _ctx_768P = jax.random.normal(jax.random.fold_in(_rk, 11), (64, 16, 96), jnp.float32)
        _ctx_768c = jax.random.dirichlet(jax.random.fold_in(_rk, 511), 0.3 * jnp.ones((16,), jnp.float32), (64, 77))
        _ctx_768t = jnp.einsum('bsk,bkd->bsd', _ctx_768c, _ctx_768P)
        _ctx_768t = _ctx_768t * jax.lax.rsqrt(jnp.mean(jnp.square(_ctx_768t)) + 1e-12) * 0.953939
        ctx_768 = -7.36909e-05 + 0.999899 * (_ctx_768t + 0.3 * jax.random.normal(jax.random.fold_in(_rk, 611), (64, 77, 96), jnp.float32))
        return (x, ctx_768)
    x, ctx_768 = _rec_inputs()

    def _L0_attn_setup():
        import jax, jax.numpy as jnp
        import numpy as np
        D_MODEL = 128
        NUM_HEADS = 16
        HEAD_DIM = D_MODEL // NUM_HEADS
        WINDOW = 16
        DILATION = 3
        SCALE = HEAD_DIM ** (-0.5)

        def _linear(x, W, b):
            return x @ W.T + b

        def _chunk_attention(x, Wq, bq, Wk, bk, Wv, bv, chunk):
            B, L, D = x.shape
            pad = -L % chunk
            if pad:
                x = jnp.pad(x, ((0, 0), (0, pad), (0, 0)))
            Lp = L + pad
            nC = Lp // chunk
            xr = x.reshape(B * nC, chunk, D)

            def heads(t):
                return t.reshape(B * nC, chunk, NUM_HEADS, HEAD_DIM).transpose(0, 2, 1, 3)
            q = heads(_linear(xr, Wq, bq))
            k = heads(_linear(xr, Wk, bk))
            v = heads(_linear(xr, Wv, bv))
            attn = jax.nn.softmax(jnp.einsum('bhqd,bhkd->bhqk', q, k) * SCALE, axis=-1)
            out = jnp.einsum('bhqk,bhkd->bhqd', attn, v)
            out = out.transpose(0, 2, 1, 3).reshape(B, Lp, D)
            return out[:, :L, :]
        key = jax.random.key(seed)
        ks = jax.random.split(key, 9)
        s = 1.0 / np.sqrt(D_MODEL)
        x = jax.random.normal(ks[0], (4, 512, D_MODEL), dtype=jnp.float32)

        def lin(kw, kb):
            W = jax.random.uniform(kw, (D_MODEL, D_MODEL), minval=-s, maxval=s, dtype=jnp.float32)
            b = jax.random.uniform(kb, (D_MODEL,), minval=-s, maxval=s, dtype=jnp.float32)
            return (W, b)
        Wq, bq = lin(ks[1], ks[2])
        Wk, bk = lin(ks[3], ks[4])
        Wv, bv = lin(ks[5], ks[6])
        Wo, bo = lin(ks[7], ks[8])
        return {'x': x, 'Wq': Wq, 'bq': bq, 'Wk': Wk, 'bk': bk, 'Wv': Wv, 'bv': bv, 'Wo': Wo, 'bo': bo}
    _L0_attn_all = _L0_attn_setup()
    _L0_attn_in = {k: v for k, v in _L0_attn_all.items() if k in ('Wq', 'bq', 'Wk', 'bk', 'Wv', 'bv', 'Wo', 'bo')}
    del _L0_attn_all

    def _L0_xattn_setup():
        import jax, jax.numpy as jnp
        import numpy as np
        IMG_DIM, TXT_DIM, HID = (128, 96, 128)
        B, LQ, LK = (8, 256, 256)
        key = jax.random.key(seed)
        ks = jax.random.split(key, 8)
        s_img = 1.0 / np.sqrt(IMG_DIM)
        s_txt = 1.0 / np.sqrt(TXT_DIM)
        return {'image_features': jax.random.normal(ks[0], (B, LQ, IMG_DIM), jnp.float32), 'text_features': jax.random.normal(ks[1], (B, LK, TXT_DIM), jnp.float32), 'Wq': jax.random.uniform(ks[2], (IMG_DIM, HID), jnp.float32, -s_img, s_img), 'bq': jax.random.uniform(ks[3], (HID,), jnp.float32, -s_img, s_img), 'Wk': jax.random.uniform(ks[4], (TXT_DIM, HID), jnp.float32, -s_txt, s_txt), 'bk': jax.random.uniform(ks[5], (HID,), jnp.float32, -s_txt, s_txt), 'Wv': jax.random.uniform(ks[6], (TXT_DIM, HID), jnp.float32, -s_txt, s_txt), 'bv': jax.random.uniform(ks[7], (HID,), jnp.float32, -s_txt, s_txt)}
    _L0_xattn_all = _L0_xattn_setup()
    _L0_xattn_in = {k: v for k, v in _L0_xattn_all.items() if k in ('Wq', 'bq', 'Wk', 'bk', 'Wv', 'bv')}
    del _L0_xattn_all

    def _L0_ffn_setup():
        import jax, jax.numpy as jnp
        import numpy as np
        B, S, H = (2, 128, 128)
        E, F = (8, 512)
        GATE_TEMP = 0.1
        key = jax.random.key(seed)
        ks = jax.random.split(key, 6)
        s_h = 1.0 / np.sqrt(H)
        s_f = 1.0 / np.sqrt(F)
        return {'hidden_states': jax.random.normal(ks[0], (B, S, H), dtype=jnp.float32), 'w_router': jax.random.normal(ks[1], (H, E), dtype=jnp.float32) * s_h, 'w_gating': jax.random.normal(ks[2], (H, E), dtype=jnp.float32) * s_h, 'w_gate': jax.random.normal(ks[3], (E, H, F), dtype=jnp.float32) * s_h, 'w_up': jax.random.normal(ks[4], (E, H, F), dtype=jnp.float32) * s_h, 'w_down': jax.random.normal(ks[5], (E, F, H), dtype=jnp.float32) * s_f}
    _L0_ffn_all = _L0_ffn_setup()
    _L0_ffn_in = {k: v for k, v in _L0_ffn_all.items() if k in ('w_router', 'w_gating', 'w_gate', 'w_up', 'w_down')}
    del _L0_ffn_all
    return {'x': x, 'ctx_768': ctx_768, 'L0_attn_Wq': _L0_attn_in['Wq'], 'L0_attn_bq': _L0_attn_in['bq'], 'L0_attn_Wk': _L0_attn_in['Wk'], 'L0_attn_bk': _L0_attn_in['bk'], 'L0_attn_Wv': _L0_attn_in['Wv'], 'L0_attn_bv': _L0_attn_in['bv'], 'L0_attn_Wo': _L0_attn_in['Wo'], 'L0_attn_bo': _L0_attn_in['bo'], 'L0_xattn_Wq': _L0_xattn_in['Wq'], 'L0_xattn_bq': _L0_xattn_in['bq'], 'L0_xattn_Wk': _L0_xattn_in['Wk'], 'L0_xattn_bk': _L0_xattn_in['bk'], 'L0_xattn_Wv': _L0_xattn_in['Wv'], 'L0_xattn_bv': _L0_xattn_in['bv'], 'L0_ffn_w_router': _L0_ffn_in['w_router'], 'L0_ffn_w_gating': _L0_ffn_in['w_gating'], 'L0_ffn_w_gate': _L0_ffn_in['w_gate'], 'L0_ffn_w_up': _L0_ffn_in['w_up'], 'L0_ffn_w_down': _L0_ffn_in['w_down']}

def reference(x, ctx_768, L0_attn_Wq, L0_attn_bq, L0_attn_Wk, L0_attn_bk, L0_attn_Wv, L0_attn_bv, L0_attn_Wo, L0_attn_bo, L0_xattn_Wq, L0_xattn_bq, L0_xattn_Wk, L0_xattn_bk, L0_xattn_Wv, L0_xattn_bv, L0_ffn_w_router, L0_ffn_w_gating, L0_ffn_w_gate, L0_ffn_w_up, L0_ffn_w_down):
    import jax
    import jax.numpy as jnp

    def _L0_attn_ref(x, Wq, bq, Wk, bk, Wv, bv, Wo, bo):
        import jax, jax.numpy as jnp
        import numpy as np
        D_MODEL = 128
        NUM_HEADS = 16
        HEAD_DIM = D_MODEL // NUM_HEADS
        WINDOW = 16
        DILATION = 3
        SCALE = HEAD_DIM ** (-0.5)

        def _linear(x, W, b):
            return x @ W.T + b

        def _chunk_attention(x, Wq, bq, Wk, bk, Wv, bv, chunk):
            B, L, D = x.shape
            pad = -L % chunk
            if pad:
                x = jnp.pad(x, ((0, 0), (0, pad), (0, 0)))
            Lp = L + pad
            nC = Lp // chunk
            xr = x.reshape(B * nC, chunk, D)

            def heads(t):
                return t.reshape(B * nC, chunk, NUM_HEADS, HEAD_DIM).transpose(0, 2, 1, 3)
            q = heads(_linear(xr, Wq, bq))
            k = heads(_linear(xr, Wk, bk))
            v = heads(_linear(xr, Wv, bv))
            attn = jax.nn.softmax(jnp.einsum('bhqd,bhkd->bhqk', q, k) * SCALE, axis=-1)
            out = jnp.einsum('bhqk,bhkd->bhqd', attn, v)
            out = out.transpose(0, 2, 1, 3).reshape(B, Lp, D)
            return out[:, :L, :]
        B, L, D = x.shape
        local_out = _chunk_attention(x, Wq, bq, Wk, bk, Wv, bv, WINDOW)
        pad = -L % DILATION
        x_pad = jnp.pad(x, ((0, 0), (0, pad), (0, 0))) if pad else x
        Lp = L + pad
        xv = x_pad.reshape(B, Lp // DILATION, DILATION, D).transpose(0, 2, 1, 3)
        x_atrous = xv.reshape(B * DILATION, Lp // DILATION, D)
        a = _chunk_attention(x_atrous, Wq, bq, Wk, bk, Wv, bv, WINDOW)
        a = a.reshape(B, DILATION, Lp // DILATION, D).transpose(0, 2, 1, 3).reshape(B, Lp, D)
        atrous_out = a[:, :L, :]
        return _linear(local_out + atrous_out, Wo, bo)

    def _L0_xattn_ref(image_features, text_features, Wq, bq, Wk, bk, Wv, bv):
        import jax, jax.numpy as jnp
        import numpy as np
        IMG_DIM, TXT_DIM, HID = (128, 96, 128)
        B, LQ, LK = (8, 256, 256)
        query = jnp.einsum('bqi,ih->bqh', image_features, Wq) + bq
        key = jnp.einsum('bkt,th->bkh', text_features, Wk) + bk
        value = jnp.einsum('bkt,th->bkh', text_features, Wv) + bv
        scale = 1.0 / jnp.sqrt(jnp.asarray(HID, query.dtype))
        scores = jnp.einsum('bqh,bkh->bqk', query, key) * scale
        weights = jax.nn.softmax(scores, axis=-1)
        attended = jnp.einsum('bqk,bkh->bqh', weights, value)
        return attended

    def _L0_ffn_ref(hidden_states, w_router, w_gating, w_gate, w_up, w_down):
        import jax, jax.numpy as jnp
        import numpy as np
        B, S, H = (2, 128, 128)
        E, F = (8, 512)
        GATE_TEMP = 0.1
        x = hidden_states
        router_probs = jax.nn.softmax(jnp.einsum('bsh,he->bse', x, w_router), axis=-1)
        gate_weights = jax.nn.softmax(jnp.einsum('bsh,he->bse', x, w_gating) / GATE_TEMP, axis=-1)
        g = jnp.einsum('bsh,ehf->ebsf', x, w_gate)
        u = jnp.einsum('bsh,ehf->ebsf', x, w_up)
        h = jax.nn.silu(g) * u
        expert_out = jnp.einsum('ebsf,efh->ebsh', h, w_down)
        cw = router_probs * gate_weights
        cw = cw / (jnp.sum(cw, axis=-1, keepdims=True) + 1e-09)
        out = jnp.einsum('ebsh,bse->bsh', expert_out, cw)
        return out
    x = _layernorm(x + _L0_attn_ref(x, L0_attn_Wq, L0_attn_bq, L0_attn_Wk, L0_attn_bk, L0_attn_Wv, L0_attn_bv, L0_attn_Wo, L0_attn_bo), axis=-1)
    x = _layernorm(x + _L0_xattn_ref(x, ctx_768, L0_xattn_Wq, L0_xattn_bq, L0_xattn_Wk, L0_xattn_bk, L0_xattn_Wv, L0_xattn_bv), axis=-1)
    x = _layernorm(x + _L0_ffn_ref(x, L0_ffn_w_router, L0_ffn_w_gating, L0_ffn_w_gate, L0_ffn_w_up, L0_ffn_w_down), axis=-1)
    return x

_drawn_inputs = setup_inputs


def setup_inputs(seed=0):
    import zlib

    import numpy as np

    out = dict(_drawn_inputs(seed))
    spreads = {}
    factors = {'L0_attn_bq': 8.0, 'L0_attn_bk': 8.0, 'L0_xattn_bq': 8.0, 'L0_xattn_bk': 8.0}
    for name, (base, spread) in spreads.items():
        noise = np.random.default_rng([zlib.crc32(name.encode()), seed]).standard_normal(out[name].shape)
        drawn = base * np.exp(spread * noise) if base else spread * noise
        out[name] = jnp.asarray(drawn.astype(out[name].dtype))
    for name, factor in factors.items():
        out[name] = (out[name] * factor).astype(out[name].dtype)
    return out
```

```python
from contextlib import ExitStack

import numpy as np
import concourse.bass as bass
from concourse import mybir

ALU = mybir.AluOpType
ACT = mybir.ActivationFunctionType
F32 = mybir.dt.float32
F32R = mybir.dt.float32r
BF16 = mybir.dt.bfloat16
AX = mybir.AxisListType.X

P = 128
HEADS, HD = 16, 8
CHUNK, DIL = 16, 3
QUAD = 4
NQ = HEADS // QUAD
BLK = 2 * CHUNK
PADT = 144
NLOC, NATR = 4, 5
NBLK = NLOC + NATR
T = 4
EPS = 1e-5
MASKED = -1e30
VW = NLOC * HD + 1

C_ID = 0
C_HEADV = C_ID + P
C_HEADQ = C_HEADV + HEADS
C_KEEP = C_HEADQ + QUAD
C_MROW = C_KEEP
C_MCOL = C_MROW + P
C_SEL = C_MCOL + NBLK * BLK
C_ALL = C_SEL + NBLK * P


def block_tokens(j):
    if j < NLOC:
        return [BLK * j + k for k in range(BLK)]
    if j < NLOC + DIL:
        return [(j - NLOC) + DIL * k for k in range(BLK)]
    r0 = j - NLOC - DIL
    return [DIL * (BLK + k % CHUNK) + r0 + k // CHUNK for k in range(BLK)]


def constants():
    c = np.zeros((P, C_ALL), np.float32)
    p = np.arange(P)
    c[:, C_ID:C_ID + P] = np.eye(P)
    c[:, C_HEADV:C_HEADV + HEADS] = (np.arange(HEADS)[None] % QUAD) == (p[:, None] // 32)
    c[:, C_HEADQ:C_HEADQ + QUAD] = np.arange(QUAD)[None] == (p[:, None] % 32) // HD
    half = (np.arange(P) % BLK) // CHUNK
    khalf = (np.arange(NBLK * BLK) % BLK) // CHUNK
    for g in range(NQ):
        for s in range(2):
            c[32 * g + s, C_MROW:C_MROW + P] = half == s
            c[32 * g + s, C_MCOL:C_MCOL + NBLK * BLK] = np.where(khalf == s, 0.0, MASKED)
    for j in range(NBLK):
        for k, t in enumerate(block_tokens(j)):
            if t < P:
                for h in range(QUAD):
                    c[t, C_SEL + j * P + h * BLK + k] = 1.0
    return c


JOBS = [("xt", 1), ("qk", 2), ("vn", 1)]
JOBS += [(f"sc{b}{j}", 1) for b in range(T) for j in range(2)]
JOBS += [("vr0", 1), ("v5", 1)]
for _b in range(T):
    JOBS += [(f"av{_b}L", 1), (f"av{_b}A", 1), (f"av{_b}5", 1)]
    if _b + 1 < T:
        JOBS += [(f"vr{_b + 1}", 1)]
JOBS += [("ot", 1), ("ot5", 1), ("kx", 1), ("vx", 1), ("wo", 1), ("x1t", 1), ("qx", 1), ("sx", 1), ("pt", 1),
         ("ax", 1), ("x2t", 1), ("rt", 1)]
assert len(JOBS) % 2 == 0
PAIR, DONE_AT, FREED_BEFORE = {}, {}, {}
_done, _freed = [0, 0], [0, 0]
for _n, (_name, _k) in enumerate(JOBS):
    PAIR[_name] = _n % 2
    FREED_BEFORE[_name] = _freed[_n % 2]
    _done[_n % 2] += 1
    _freed[_n % 2] += _k
    DONE_AT[_name] = _done[_n % 2]
DONE_PER, FREED_PER = tuple(_done), tuple(_freed)

STEPS = {
    0: [("xt",)], 1: [("qk",), ("qe", 0), ("vn",)],
    2: [("sc", 0, 0), ("qe", 1)], 3: [("sc", 0, 1)], 4: [("sc", 1, 0), ("qe", 2)], 5: [("sc", 1, 1)],
    6: [("sc", 2, 0), ("qe", 3)], 7: [("sc", 2, 1)], 8: [("sc", 3, 0)], 9: [("sc", 3, 1)],
    10: [("exps",), ("vr", 0)], 11: [("v5",), ("tr", 0)],
    12: [("av", 0, "L"), ("av", 0, "A")], 13: [("av5", 0), ("vr", 1), ("tr", 1)],
    14: [("av", 1, "L"), ("av", 1, "A")], 15: [("av5", 1), ("vr", 2), ("tr", 2)],
    16: [("av", 2, "L"), ("av", 2, "A")], 17: [("av5", 2), ("vr", 3), ("tr", 3)],
    18: [("av", 3, "L"), ("av", 3, "A")], 19: [("av5", 3), ("ot",)],
    20: [("ot5",), ("kx",), ("vx",)], 21: [("wo",)], 22: [("ln1",)], 23: [("x1t",)], 24: [("qx",)],
    25: [("sx",)], 26: [("ex",)], 27: [("pt",)], 28: [("ax",)], 29: [("ln2",)], 30: [("x2t",)],
    31: [("rt",), ("cw",)],
}
DVE_ATT_LINKS = 90
DVE_FFN_LINKS = 3


def build_decoder(nc, x, ctx, cst, WqT, WkT, WvT, WoT, bq, bk, bv, bo, Wxq, Wxk, Wxv, bxq, bxk, bxv,
                  w_router, w_gating, w_gate, w_up, w_down, out):
    B, L, D = x.shape
    _, LC, DC = ctx.shape
    E, _, F = w_gate.shape
    G = B // T
    FC = F // P
    NCH = E * FC
    TOK = T * P
    SELF_SCALE = float(HD) ** -0.5
    CROSS_SCALE = float(D) ** -0.5
    PIECES = 3 * E
    assert L == P and D == P and F == 4 * P and NCH == 32 and G * T == B

    with ExitStack() as stack:
        def sb(name, shape, dt=F32):
            return stack.enter_context(nc.sbuf_tensor(name, shape, dt))

        def ps(name, shape):
            return stack.enter_context(nc.psum_tensor(name, shape, F32))

        def sem(name):
            return stack.enter_context(nc.semaphore(name))

        pair = [ps("pair0", [P, 2, 512]), ps("pair1", [P, 2, 512])]
        gate_ps, up_ps, y_ps, xs_ps = (ps(n, [P, 512]) for n in ("gate_ps", "up_ps", "y_ps", "xs_ps"))

        cs = sb("cs", [P, C_KEEP])
        ident = cs[:, C_ID:C_ID + P]
        headv = cs[:, C_HEADV:C_HEADV + HEADS]
        headq = cs[:, C_HEADQ:C_HEADQ + QUAD]
        wqT, wkT, wvT, woT, wxq = (sb(n, [P, P]) for n in ("wqT", "wkT", "wvT", "woT", "wxq"))
        wxk, wxv = sb("wxk", [DC, P]), sb("wxv", [DC, P])
        wrg = sb("wrg", [P, 2 * E])
        cols = sb("cols", [P, 5])
        rows = sb("rows", [1, 2 * P])
        mrow = sb("mrow", [P, P], BF16)
        mcol = sb("mcol", [P, NBLK * BLK], BF16)
        sel = sb("sel", [P, NBLK, P], F32R)
        ones = sb("ones", [1, P])
        bv2 = sb("bv2", [P, 1])
        bias_o = sb("bias_o", [P, P])
        bias_x = sb("bias_x", [P, P])
        minus_half = sb("minus_half", [P, T])
        wH = sb("wH", [P, 3, E, 512], F32R)
        wL = sb("wL", [P, 3, E, 512], F32R)
        sh = sb("sh", [P, 4, 512])
        hH, hL = sb("hH", [P, 2, 512], F32R), sb("hL", [P, 2, 512], F32R)
        xs = sb("xs", [P, T, P])
        xsH, xsL = sb("xsH", [P, 2, 512], F32R), sb("xsL", [P, 2, 512], F32R)
        x2H, x2L = sb("x2H", [P, 512], F32R), sb("x2L", [P, 512], F32R)
        x2r = sb("x2r", [P, T, P])
        yo = sb("yo", [P, T, P])
        x_in = sb("x_in", [P, T, P])
        xb = sb("xb", [P, T, P])
        ctx_in = sb("ctx_in", [LC, T, DC])
        xT = sb("xT", [P, T, PADT])
        Kt = sb("Kt", [P, T, PADT])
        Qr = sb("Qr", [P, T, NBLK, BLK])
        vH, vL = sb("vH", [P, TOK], F32R), sb("vL", [P, TOK], F32R)
        qo = sb("qo", [P, 2 * NBLK * P])
        Qbd = qo[:, :].rearrange("p (b j h k) -> p b j h k", b=2, j=NBLK, h=QUAD)
        oL = qo[:, 0:TOK].rearrange("p (b c) -> p b c", b=T)
        oA = qo[:, TOK:2 * TOK].rearrange("p (b c) -> p b c", b=T)
        o5 = qo[:, 2 * TOK:3 * TOK].rearrange("p (b c) -> p b c", b=T)
        big = sb("big", [P, T * NQ * NBLK * BLK])
        S = big[:, :].rearrange("p (b g j k) -> p b g j k", b=T, g=NQ, j=NBLK)
        Pt = sb("Pt", [P, NQ, NBLK, BLK])
        Vbd = sb("Vbd", [P, 2, HEADS, VW])
        V5 = sb("V5", [P, T, HEADS, HD + 1])
        oT = sb("oT", [P, T, PADT])
        ctxT = sb("ctxT", [DC, T * LC])
        KxT = sb("KxT", [P, T, LC])
        at = 0
        views = []
        for width in (TOK, TOK, T * LC, TOK, TOK, TOK, TOK, TOK, TOK):
            views.append(big[:, at:at + width])
            at += width + width % 2
        assert at <= T * NQ * NBLK * BLK
        x1T, QxT = views[0], views[1].rearrange("p (b t) -> p b t", b=T)
        Px = views[2].rearrange("p (b k) -> p b k", b=T)
        PxT = views[3][0:LC, :].rearrange("p (b t) -> p b t", b=T)
        r1, r2, x1 = (views[n].rearrange("p (b d) -> p b d", b=T) for n in (4, 5, 6))
        x2T = views[7]
        Vx = views[8][0:LC, :].rearrange("p (b d) -> p b d", b=T)
        x2 = sb("x2", [P, T, P])
        cst_in = big[:, 0:C_ALL - C_KEEP]
        smax = sb("smax", [P, 2 * NBLK])
        rsum = sb("rsum", [P, HEADS])
        bst = sb("bst", [P, T, 6])
        pause = sb("pause", [P, 1])
        mv = sb("mv", [P, T, 2])
        vareps = sb("vareps", [P, T])
        rstd = sb("rstd", [P, T])
        bst3, mv3 = sb("bst3", [P, T, 6]), sb("mv3", [P, T, 2])
        vareps3, rstd3 = sb("vareps3", [P, T]), sb("rstd3", [P, T])
        xmax, xsum, xrec = sb("xmax", [P, T]), sb("xsum", [P, T]), sb("xrec", [P, T])
        lg = sb("lg", [P, 2 * T, E])
        lmax, lsum, lrec = (sb(n, [P, 2 * T]) for n in ("lmax", "lsum", "lrec"))
        cw = sb("cw", [P, T, E])
        csum, crec = sb("csum", [P, T]), sb("crec", [P, T])

        params_in = sem("params_in")
        piece_in = [sem(f"piece_in{n}") for n in range(4)]
        x_loaded, ctx_loaded, out_stored = sem("x_loaded"), sem("ctx_loaded"), sem("out_stored")
        dve_setup, pe_bias, bias_ready, act_setup = sem("dve_setup"), sem("pe_bias"), sem("bias_ready"), sem("act_setup")
        piece_hi, piece_lo = sem("piece_hi"), sem("piece_lo")
        pair_done = [sem("pair_done0"), sem("pair_done1")]
        pair_free = [sem("pair_free0"), sem("pair_free1")]
        xT_ready, q_ready, k_ready, xb_ready = sem("xT_ready"), sem("q_ready"), sem("k_ready"), sem("xb_ready")
        qbd_ready, vH_ready, vL_ready = sem("qbd_ready"), sem("vH_ready"), sem("vL_ready")
        ctxT_ready, kx_ready, vx_ready = sem("ctxT_ready"), sem("kx_ready"), sem("vx_ready")
        s_ready, p_ready, pt_ready = sem("s_ready"), sem("p_ready"), sem("pt_ready")
        v_ready, v5_ready, o_ready = sem("v_ready"), sem("v5_ready"), sem("o_ready")
        oTl_ready, oT_ready = sem("oTl_ready"), sem("oT_ready")
        var_ready, rstd_ready = sem("var_ready"), sem("rstd_ready")
        x1_ready, x1b_ready, x1T_ready, qx_ready = sem("x1_ready"), sem("x1b_ready"), sem("x1T_ready"), sem("qx_ready")
        sx_ready, ex_ready, pxT_ready = sem("sx_ready"), sem("ex_ready"), sem("pxT_ready")
        x2_ready, x2T_ready, lg_ready, elg_ready, cw_ready = (sem(n) for n in (
            "x2_ready", "x2T_ready", "lg_ready", "elg_ready", "cw_ready"))
        x2H_ready, x2L_ready, x2r_ready = sem("x2H_ready"), sem("x2L_ready"), sem("x2r_ready")
        xs_ready, xsT_done, xsH_ready, xsL_ready = sem("xs_ready"), sem("xsT_done"), sem("xsH_ready"), sem("xsL_ready")
        gate_done, up_done, down_done = sem("gate_done"), sem("up_done"), sem("down_done")
        silu_ready, h_ready, hH_ready, hL_ready = sem("silu_ready"), sem("h_ready"), sem("hH_ready"), sem("hL_ready")
        yT_ready, yt_done, r3_ready, var3_ready, rstd3_ready, out_ready = (sem(n) for n in (
            "yT_ready", "yt_done", "r3_ready", "var3_ready", "rstd3_ready", "out_ready"))
        att_link, ffn_link, setup_link = sem("att_link"), sem("ffn_link"), sem("setup_link")

        def done_at(name, g):
            return g * DONE_PER[PAIR[name]] + DONE_AT[name]

        def freed_at(name, g):
            return g * FREED_PER[PAIR[name]] + FREED_BEFORE[name]

        def walk(run_ffn, run_att, tail, ffn, att):
            for n in range(NCH):
                if ffn:
                    run_ffn(n)
                if att:
                    for name, *args in STEPS[n]:
                        run_att(name, args)
                if not ffn and att and n < PIECES:
                    run_att("piece", (n,))
            tail(ffn, att)

        def tokens(view, j):
            if j < NLOC:
                return view[..., BLK * j:BLK * (j + 1)]
            v = view.rearrange("p b (i r) -> p b r i", r=DIL) if len(view.shape) == 3 else \
                view.rearrange("p (i r) -> p r i", r=DIL)
            if j < NLOC + DIL:
                return v[..., j - NLOC, 0:BLK]
            r = j - NLOC - DIL
            return v[..., r:r + 2, BLK:BLK + CHUNK]

        block = stack.enter_context(nc.Block())

        @block.sync
        def _(sp):
            n_params = 0
            for dst, src in ((cs[:, :], cst[:, 0:C_KEEP]), (cst_in, cst[:, C_KEEP:C_ALL]), (wqT[:, :], WqT), (wkT[:, :], WkT), (wvT[:, :], WvT),
                             (woT[:, :], WoT), (wxq[:, :], Wxq), (wxk[:, :], Wxk), (wxv[:, :], Wxv),
                             (wrg[:, 0:E], w_router), (wrg[:, E:2 * E], w_gating),
                             (cols[:, 0:1], bq), (cols[:, 1:2], bk), (cols[:, 2:3], bv),
                             (cols[:, 3:4], bxq), (cols[:, 4:5], bxk)):
                if len(src.shape) == 1:
                    src = src.rearrange("(p a) -> p a", a=1)
                sp.dma_start(dst, src).then_inc(params_in, 16)
            for n, src in enumerate((bo, bxv)):
                sp.dma_start(rows[:, n * P:(n + 1) * P], src.rearrange("(a n) -> a n", a=1)).then_inc(params_in, 16)

            def load(g, first=False):
                if not first:
                    sp.wait_ge(pair_done[PAIR["xt"]], done_at("xt", g - 1))
                    sp.wait_ge(xb_ready, 2 * (g - 1) + 1)
                sp.dma_start(x_in[:, :, :], x[bass.ds(g * T, T)].rearrange("b t d -> t b d")).then_inc(x_loaded, 16)
                sp.dma_start(ctx_in[:, :, :], ctx[bass.ds(g * T, T)].rearrange("b t d -> t b d")).then_inc(ctx_loaded, 16)

            def store(f):
                sp.wait_ge(out_ready, f + 1)
                sp.dma_start(out[bass.ds(f * T, T)].rearrange("b t d -> t b d"), yo[:, :, :]).then_inc(out_stored, 16)

            sp.sem_inc(out_stored, 16)
            load(0, first=True)
            for n in range(PIECES):
                if n >= 4:
                    sp.wait_ge(piece_lo, n - 3)
                m, e = n // E, n % E
                src = w_gate[e] if m == 0 else w_up[e] if m == 1 else w_down[e].rearrange("(c p) n -> p c n", p=P)
                dst = sh[:, n % 4, :] if m < 2 else sh[:, n % 4, :].rearrange("p (c n) -> p c n", c=FC)
                sp.dma_start(dst, src).then_inc(piece_in[n % 4], 16)
            load(1)
            with sp.Fori(1, G - 1) as i:
                load(i + 1)
                store(i - 1)
            store(G - 2)
            store(G - 1)
            sp.wait_ge(out_stored, 16 * (G + 1))

        @block.tensor
        def _(pe):
            nc_pe = nc.tensor
            pe.wait_ge(params_in, 16 * 18)
            pe.wait_ge(dve_setup, 1)
            nc_pe.matmul(xs_ps[:, 0:P], bv2[:, 0:1].broadcast_to([P, P]), woT[:, :], start=True, stop=False)
            nc_pe.matmul(xs_ps[:, 0:P], ones[:, :], rows[:, 0:P], start=False, stop=True)
            nc_pe.matmul(xs_ps[:, P:2 * P], ones[:, :], rows[:, P:2 * P], start=True, stop=True).then_inc(pe_bias, 1)
            pe.wait_ge(bias_ready, 1)

            def run_att(g, first=False):
                def transposes(t, src, n_out):
                    for b in range(T):
                        s = src[:, b, :]
                        k = s.shape[0]
                        ins = nc_pe.transpose(t[0:n_out, 0, b * k:(b + 1) * k], s, ident[0:k, 0:k])
                    return ins

                def step(name, args):
                    if name == "xt":
                        pe.wait_ge(x_loaded, 16 * g + 16)
                        pe.wait_ge(ctx_loaded, 16 * g + 16)
                        pe.wait_ge(pair_free[PAIR["xt"]], freed_at("xt", g))
                        t = pair[PAIR["xt"]]
                        for b in range(T):
                            nc_pe.transpose(t[:, 0, b * P:(b + 1) * P], x_in[:, b, :], ident)
                        for b in range(T):
                            ins = nc_pe.transpose(t[0:DC, 1, b * LC:(b + 1) * LC], ctx_in[:, b, :],
                                                  ident[0:LC, 0:LC])
                        ins.then_inc(pair_done[PAIR["xt"]], 1)
                    elif name == "qk":
                        pe.wait_ge(xT_ready, g + 1)
                        pe.wait_ge(pair_free[PAIR["qk"]], freed_at("qk", g))
                        t = pair[PAIR["qk"]]
                        src = xT[:, :, 0:P]
                        nc_pe.matmul(t[:, 0, :], wqT[:, :], src, start=True, stop=True)
                        nc_pe.matmul(t[:, 1, :], wkT[:, :], src, start=True, stop=True).then_inc(pair_done[PAIR["qk"]], 1)
                    elif name == "sc":
                        b, j = args
                        if j == 0:
                            pe.wait_ge(qbd_ready, T * g + b + 1)
                        if (b, j) == (0, 0):
                            pe.wait_ge(k_ready, g + 1)
                        pe.wait_ge(pair_free[PAIR[f"sc{b}{j}"]], freed_at(f"sc{b}{j}", g))
                        t = pair[PAIR[f"sc{b}{j}"]]
                        for gl in range(2):
                            q0 = 32 * (2 * j + gl)
                            nc_pe.matmul(t[:, gl, 0:NBLK * BLK], mrow[q0:q0 + 2, :], mcol[q0:q0 + 2, :],
                                         start=True, stop=False)
                            for k in range(NBLK):
                                ins = nc_pe.matmul(t[:, gl, k * BLK:(k + 1) * BLK],
                                                   Qbd[q0:q0 + 32, b % 2, k], tokens(Kt[q0:q0 + 32, b, :], k),
                                                   start=False, stop=(k == NBLK - 1))
                        ins.then_inc(pair_done[PAIR[f"sc{b}{j}"]], 1)
                    elif name == "vn":
                        pe.wait_ge(pair_free[PAIR["vn"]], freed_at("vn", g))
                        t = pair[PAIR["vn"]]
                        for b in range(T):
                            ins = nc_pe.matmul(t[:, 0, b * P:(b + 1) * P], xT[:, b, 0:P], wvT[:, :],
                                               start=True, stop=True)
                        ins.then_inc(pair_done[PAIR["vn"]], 1)
                    elif name == "vr":
                        b, = args
                        pe.wait_ge(vH_ready, g + 1)
                        pe.wait_ge(vL_ready, g + 1)
                        pe.wait_ge(pair_free[PAIR[f"vr{b}"]], freed_at(f"vr{b}", g))
                        t = pair[PAIR[f"vr{b}"]]
                        for k in range(2 * NLOC):
                            dst = t[:, k // NLOC, (k % NLOC) * P:(k % NLOC + 1) * P]
                            nc_pe.matmul(dst, sel[:, k, :], vH[:, b * P:(b + 1) * P], start=True, stop=False)
                            ins = nc_pe.matmul(dst, sel[:, k, :], vL[:, b * P:(b + 1) * P], start=False, stop=True)
                        ins.then_inc(pair_done[PAIR[f"vr{b}"]], 1)
                    elif name == "v5":
                        pe.wait_ge(pair_free[PAIR["v5"]], freed_at("v5", g))
                        t = pair[PAIR["v5"]]
                        nc_pe.matmul(t[:, 0, :], sel[:, NBLK - 1, :], vH[:, :], start=True, stop=False)
                        nc_pe.matmul(t[:, 0, :], sel[:, NBLK - 1, :], vL[:, :], start=False, stop=True).then_inc(pair_done[PAIR["v5"]], 1)
                    elif name == "av":
                        b, which = args
                        pe.wait_ge(pt_ready, T * g + b + 1)
                        pe.wait_ge(v_ready, T * g + b + 1)
                        pe.wait_ge(pair_free[PAIR[f"av{b}{which}"]], freed_at(f"av{b}{which}", g))
                        t = pair[PAIR[f"av{b}{which}"]]
                        s = "LA".index(which)
                        for q in range(NQ):
                            ins = nc_pe.matmul(t[:, q // 2, (q % 2) * QUAD * VW:(q % 2 + 1) * QUAD * VW],
                                               Pt[:, q, NLOC * s:NLOC * (s + 1), :],
                                               Vbd[:, s, QUAD * q:QUAD * (q + 1), :], start=True, stop=True)
                        ins.then_inc(pair_done[PAIR[f"av{b}{which}"]], 1)
                    elif name == "av5":
                        b, = args
                        if b == 0:
                            pe.wait_ge(v5_ready, g + 1)
                        pe.wait_ge(pair_free[PAIR[f"av{b}5"]], freed_at(f"av{b}5", g))
                        t = pair[PAIR[f"av{b}5"]]
                        w = QUAD * (HD + 1)
                        for q in range(NQ):
                            ins = nc_pe.matmul(t[0:BLK, 0, q * w:(q + 1) * w], Pt[:, q, NBLK - 1, :],
                                               V5[:, b, QUAD * q:QUAD * (q + 1), :], start=True, stop=True)
                        ins.then_inc(pair_done[PAIR[f"av{b}5"]], 1)
                    elif name == "ot":
                        pe.wait_ge(o_ready, g + 1)
                        pe.wait_ge(pair_free[PAIR["ot"]], freed_at("ot", g))
                        t = pair[PAIR["ot"]]
                        for s, o in enumerate((oL, oA)):
                            for b in range(T):
                                ins = nc_pe.transpose(t[:, s, b * P:(b + 1) * P], o[:, b, :], ident)
                        ins.then_inc(pair_done[PAIR["ot"]], 1)
                    elif name == "ot5":
                        pe.wait_ge(pair_free[PAIR["ot5"]], freed_at("ot5", g))
                        t = pair[PAIR["ot5"]]
                        for b in range(T):
                            ins = nc_pe.transpose(t[:, 0, b * P:(b + 1) * P], o5[:, b, :], ident)
                        ins.then_inc(pair_done[PAIR["ot5"]], 1)
                    elif name == "kx":
                        pe.wait_ge(ctxT_ready, g + 1)
                        pe.wait_ge(pair_free[PAIR["kx"]], freed_at("kx", g))
                        t = pair[PAIR["kx"]]
                        nc_pe.matmul(t[:, 0, 0:T * LC], wxk[:, :], ctxT[:, :], start=True, stop=True).then_inc(pair_done[PAIR["kx"]], 1)
                    elif name == "vx":
                        pe.wait_ge(pair_free[PAIR["vx"]], freed_at("vx", g))
                        t = pair[PAIR["vx"]]
                        for b in range(T):
                            ins = nc_pe.matmul(t[0:LC, 0, b * P:(b + 1) * P], ctxT[:, b * LC:(b + 1) * LC],
                                               wxv[:, :], start=True, stop=True)
                        ins.then_inc(pair_done[PAIR["vx"]], 1)
                    elif name == "wo":
                        pe.wait_ge(oT_ready, g + 1)
                        pe.wait_ge(pair_free[PAIR["wo"]], freed_at("wo", g))
                        t = pair[PAIR["wo"]]
                        for b in range(T):
                            ins = nc_pe.matmul(t[:, 0, b * P:(b + 1) * P], oT[:, b, 0:P], woT[:, :],
                                               start=True, stop=True)
                        ins.then_inc(pair_done[PAIR["wo"]], 1)
                    elif name == "x1t":
                        pe.wait_ge(x1_ready, g + 1)
                        pe.wait_ge(pair_free[PAIR["x1t"]], freed_at("x1t", g))
                        t = pair[PAIR["x1t"]]
                        transposes(t, x1, P).then_inc(pair_done[PAIR["x1t"]], 1)
                    elif name == "qx":
                        pe.wait_ge(x1T_ready, g + 1)
                        pe.wait_ge(pair_free[PAIR["qx"]], freed_at("qx", g))
                        t = pair[PAIR["qx"]]
                        nc_pe.matmul(t[:, 0, :], wxq[:, :], x1T, start=True, stop=True).then_inc(pair_done[PAIR["qx"]], 1)
                    elif name == "sx":
                        pe.wait_ge(qx_ready, g + 1)
                        pe.wait_ge(kx_ready, g + 1)
                        pe.wait_ge(pair_free[PAIR["sx"]], freed_at("sx", g))
                        t = pair[PAIR["sx"]]
                        for b in range(T):
                            ins = nc_pe.matmul(t[:, 0, b * LC:(b + 1) * LC], QxT[:, b, :], KxT[:, b, :],
                                               start=True, stop=True)
                        ins.then_inc(pair_done[PAIR["sx"]], 1)
                    elif name == "pt":
                        pe.wait_ge(ex_ready, g + 1)
                        pe.wait_ge(pair_free[PAIR["pt"]], freed_at("pt", g))
                        t = pair[PAIR["pt"]]
                        transposes(t, Px, LC).then_inc(pair_done[PAIR["pt"]], 1)
                    elif name == "ax":
                        pe.wait_ge(pxT_ready, g + 1)
                        pe.wait_ge(vx_ready, g + 1)
                        pe.wait_ge(pair_free[PAIR["ax"]], freed_at("ax", g))
                        t = pair[PAIR["ax"]]
                        for b in range(T):
                            ins = nc_pe.matmul(t[:, 0, b * P:(b + 1) * P], PxT[:, b, :], Vx[:, b, :],
                                               start=True, stop=True)
                        ins.then_inc(pair_done[PAIR["ax"]], 1)
                    elif name == "x2t":
                        pe.wait_ge(x2_ready, g + 1)
                        pe.wait_ge(pair_free[PAIR["x2t"]], freed_at("x2t", g))
                        t = pair[PAIR["x2t"]]
                        transposes(t, x2, P).then_inc(pair_done[PAIR["x2t"]], 1)
                    elif name == "rt":
                        pe.wait_ge(x2T_ready, g + 1)
                        pe.wait_ge(pair_free[PAIR["rt"]], freed_at("rt", g))
                        t = pair[PAIR["rt"]]
                        for b in range(T):
                            ins = nc_pe.matmul(t[:, 0, b * 2 * E:(b + 1) * 2 * E], x2T[:, b * P:(b + 1) * P],
                                               wrg[:, :], start=True, stop=True)
                        ins.then_inc(pair_done[PAIR["rt"]], 1)
                return step

            def scaled_tokens(f, e):
                pe.wait_ge(xs_ready, E * f + e + 1)
                pe.wait_ge(xsH_ready, E * f + e)
                pe.wait_ge(xsL_ready, E * f + e)
                for b in range(T):
                    ins = nc_pe.transpose(xs_ps[:, b * P:(b + 1) * P], xs[:, b, :], ident)
                ins.then_inc(xsT_done, 1)

            def three(dst, w, a, rh, rl, start, stop):
                nc_pe.matmul(dst, wH[(slice(None), *w)][:, a:a + P], rh, start=start, stop=False)
                nc_pe.matmul(dst, wH[(slice(None), *w)][:, a:a + P], rl, start=False, stop=False)
                return nc_pe.matmul(dst, wL[(slice(None), *w)][:, a:a + P], rh, start=False, stop=stop)

            def down(f, n):
                pe.wait_ge(hH_ready, NCH * f + n + 1)
                pe.wait_ge(hL_ready, NCH * f + n + 1)
                if n == 0:
                    pe.wait_ge(x2r_ready, f + 1)
                e, c = n // FC, n % FC
                three(y_ps[:, :], (2, e), c * P, hH[:, n % 2, :], hL[:, n % 2, :],
                      n == 0, n == NCH - 1).then_inc(down_done, 1)

            def run_ffn(f):
                def chunk(n):
                    e, c = n // FC, n % FC
                    if n == 0:
                        pe.wait_ge(x2H_ready, f + 1)
                        pe.wait_ge(x2L_ready, f + 1)
                    if n >= 1:
                        pe.wait_ge(silu_ready, NCH * f + n)
                    three(gate_ps[:, :], (0, e), c * P, x2H[:, :], x2L[:, :], True, True).then_inc(gate_done, 1)
                    if c == 0:
                        pe.wait_ge(xsH_ready, E * f + e + 1)
                        pe.wait_ge(xsL_ready, E * f + e + 1)
                    if n >= 1:
                        pe.wait_ge(h_ready, NCH * f + n)
                    three(up_ps[:, :], (1, e), c * P, xsH[:, e % 2, :], xsL[:, e % 2, :], True, True)\
                        .then_inc(up_done, 1)
                    if n >= 2:
                        down(f, n - 2)
                    if c == 2 and e + 1 < E:
                        scaled_tokens(f, e + 1)
                return chunk

            def tail(f, g):
                def run(ffn, att):
                    if ffn:
                        down(f, NCH - 2)
                    if att:
                        scaled_tokens(g, 0)
                    if ffn:
                        down(f, NCH - 1)
                        pe.wait_ge(yT_ready, f + 1)
                        for b in range(T):
                            ins = nc_pe.transpose(y_ps[:, b * P:(b + 1) * P], yo[:, b, :], ident)
                        ins.then_inc(yt_done, 1)
                return run

            walk(None, run_att(0, first=True), tail(0, 0), False, True)
            pe.wait_ge(piece_lo, PIECES)
            with pe.Fori(1, G) as i:
                walk(run_ffn(i - 1), run_att(i), tail(i - 1, i), True, True)
            walk(run_ffn(G - 1), None, tail(G - 1, 0), True, False)

        @block.scalar
        def _(act):
            sc = nc.scalar
            act.wait_ge(params_in, 16 * 18)
            act.wait_ge(dve_setup, 1)

            def run_att(g, first=False):
                def step(name, args):
                    if name == "xt":
                        act.wait_ge(pair_done[PAIR["xt"]], done_at("xt", g))
                        if not first:
                            act.wait_ge(pair_done[PAIR["vn"]], done_at("vn", g - 1))
                        t = pair[PAIR["xt"]]
                        sc.copy(xT[:, :, 0:P], t[:, 0, :].rearrange("p (b t) -> p b t", b=T)).then_inc(xT_ready, 1)
                        if not first:
                            act.wait_ge(pair_done[PAIR["vx"]], done_at("vx", g - 1))
                        ins = sc.copy(ctxT[:, :], t[0:DC, 1, 0:T * LC])
                        ins.then_inc(ctxT_ready, 1)
                        act.wait_ge(ctxT_ready, g + 1)
                        act.sem_inc(pair_free[PAIR["xt"]], 1)
                    elif name == "qk":
                        act.wait_ge(pair_done[PAIR["qk"]], done_at("qk", g))
                        act.wait_ge(qbd_ready, T * g)
                        src = pair[PAIR["qk"]][:, 0, :].rearrange("p (b t) -> p b t", b=T)
                        sc.activation(Qr[:, :, 0:NLOC, :].rearrange("p b j k -> p b (j k)"), src,
                                      ACT.Identity, bias=cols[:, 0:1])
                        sc.activation(Qr[:, :, NLOC:NLOC + DIL, :],
                                      src[:, :, 0:DIL * BLK].rearrange("p b (k r) -> p b r k", r=DIL),
                                      ACT.Identity, bias=cols[:, 0:1])
                        for j in (NBLK - 2, NBLK - 1):
                            for half in range(2):
                                own = [t for t in block_tokens(j)[half * CHUNK:(half + 1) * CHUNK] if t < P]
                                ins = sc.activation(Qr[:, :, j, half * CHUNK:half * CHUNK + len(own)],
                                                    src[:, :, own[0]:own[-1] + 1:DIL], ACT.Identity,
                                                    bias=cols[:, 0:1])
                        ins.then_inc(q_ready, 1)
                        act.wait_ge(q_ready, g + 1)
                        act.sem_inc(pair_free[PAIR["qk"]], 1)
                    elif name == "vn":
                        act.wait_ge(pair_done[PAIR["vn"]], done_at("vn", g))
                        if not first:
                            act.wait_ge(pair_done[PAIR["vr3"]], done_at("vr3", g - 1))
                        sc.copy(vH[:, :], pair[PAIR["vn"]][:, 0, :]).then_inc(vH_ready, 1)
                    elif name == "exps":
                        for b in range(T):
                            act.wait_ge(s_ready, 2 * T * g + 2 * b + 2)
                            v = S[:, b].rearrange("p g j k -> p (g j k)")
                            sc.activation(v, v, ACT.Exp, scale=SELF_SCALE).then_inc(p_ready, 1)
                    elif name == "ot":
                        act.wait_ge(pair_done[PAIR["ot"]], done_at("ot", g))
                        if not first:
                            act.wait_ge(pair_done[PAIR["wo"]], done_at("wo", g - 1))
                        sc.copy(oT[:, :, 0:P], pair[PAIR["ot"]][:, 0, :].rearrange("p (b t) -> p b t", b=T))\
                            .then_inc(oTl_ready, 1)
                    elif name == "kx":
                        act.wait_ge(pair_done[PAIR["kx"]], done_at("kx", g))
                        if not first:
                            act.wait_ge(pair_done[PAIR["sx"]], done_at("sx", g - 1))
                        sc.activation(KxT[:, :, :], pair[PAIR["kx"]][:, 0, 0:T * LC].rearrange("p (b k) -> p b k", b=T),
                                      ACT.Identity, bias=cols[:, 4:5]).then_inc(kx_ready, 1)
                        act.wait_ge(kx_ready, g + 1)
                        act.sem_inc(pair_free[PAIR["kx"]], 1)
                    elif name == "vx":
                        act.wait_ge(pair_done[PAIR["vx"]], done_at("vx", g))
                        act.wait_ge(pt_ready, T * g + T)
                        sc.copy(Vx, pair[PAIR["vx"]][0:LC, 0, :].rearrange("p (b d) -> p b d", b=T))\
                            .then_inc(vx_ready, 1)
                        act.wait_ge(vx_ready, g + 1)
                        act.sem_inc(pair_free[PAIR["vx"]], 1)
                    elif name == "x1t":
                        act.wait_ge(pair_done[PAIR["x1t"]], done_at("x1t", g))
                        act.wait_ge(pt_ready, T * g + T)
                        sc.copy(x1T, pair[PAIR["x1t"]][:, 0, :]).then_inc(x1T_ready, 1)
                        act.wait_ge(x1T_ready, g + 1)
                        act.sem_inc(pair_free[PAIR["x1t"]], 1)
                    elif name == "qx":
                        act.wait_ge(pair_done[PAIR["qx"]], done_at("qx", g))
                        sc.activation(QxT, pair[PAIR["qx"]][:, 0, :].rearrange("p (b t) -> p b t", b=T),
                                      ACT.Identity, bias=cols[:, 3:4]).then_inc(qx_ready, 1)
                        act.wait_ge(qx_ready, g + 1)
                        act.sem_inc(pair_free[PAIR["qx"]], 1)
                    elif name == "ex":
                        act.wait_ge(sx_ready, g + 1)
                        sc.activation(Px, Px, ACT.Exp, scale=CROSS_SCALE).then_inc(ex_ready, 1)
                    elif name == "pt":
                        act.wait_ge(pair_done[PAIR["pt"]], done_at("pt", g))
                        sc.copy(PxT, pair[PAIR["pt"]][0:LC, 0, :].rearrange("p (b t) -> p b t", b=T))\
                            .then_inc(pxT_ready, 1)
                        act.wait_ge(pxT_ready, g + 1)
                        act.sem_inc(pair_free[PAIR["pt"]], 1)
                    elif name == "x2t":
                        act.wait_ge(pair_done[PAIR["x2t"]], done_at("x2t", g))
                        sc.copy(x2T, pair[PAIR["x2t"]][:, 0, :]).then_inc(x2T_ready, 1)
                        act.wait_ge(x2T_ready, g + 1)
                        act.sem_inc(pair_free[PAIR["x2t"]], 1)
                    elif name == "cw":
                        act.wait_ge(lg_ready, g + 1)
                        v = lg[:, :, :].rearrange("p (b s) e -> p b s e", s=2)
                        sc.activation(v[:, :, 0, :], v[:, :, 0, :], ACT.Exp)
                        sc.activation(v[:, :, 1, :], v[:, :, 1, :], ACT.Exp, scale=10.0).then_inc(elg_ready, 1)
                    elif name == "piece":
                        n, = args
                        act.wait_ge(piece_in[n % 4], 16 * (n // 4 + 1))
                        sc.copy(wH[:, n // E, n % E, :], sh[:, n % 4, :]).then_inc(piece_hi, 1)
                return step

            def high(f, n):
                act.wait_ge(h_ready, NCH * f + n + 1)
                if n >= 2:
                    act.wait_ge(down_done, NCH * f + n - 1)
                sc.copy(hH[:, n % 2, :], sh[:, n % 4, :]).then_inc(hH_ready, 1)

            def scaled_high(f, e, first=False):
                act.wait_ge(xsT_done, E * f + e + 1)
                if not first:
                    act.wait_ge(up_done, NCH * f + FC * (e - 1))
                sc.copy(xsH[:, e % 2, :], xs_ps[:, :]).then_inc(xsH_ready, 1)

            def run_ffn(f):
                def chunk(n):
                    act.wait_ge(gate_done, NCH * f + n + 1)
                    if n >= 4:
                        act.wait_ge(hL_ready, NCH * f + n - 3)
                    sc.activation(sh[:, n % 4, :], gate_ps[:, :], ACT.Silu).then_inc(silu_ready, 1)
                    if n >= 1:
                        high(f, n - 1)
                    if n % FC == 3 and n // FC + 1 < E:
                        scaled_high(f, n // FC + 1)
                return chunk

            def tail(f, g):
                def run(ffn, att):
                    if ffn:
                        high(f, NCH - 1)
                    if att:
                        act.wait_ge(gate_done, NCH * g)
                        act.wait_ge(x2T_ready, g + 1)
                        sc.copy(x2H[:, :], x2T).then_inc(x2H_ready, 1)
                        scaled_high(g, 0, first=not ffn)
                    if ffn:
                        act.wait_ge(down_done, NCH * f + NCH)
                        act.wait_ge(out_stored, 16 * (f + 1))
                        sc.copy(yo[:, :, :].rearrange("p b d -> p (b d)"), y_ps[:, :]).then_inc(yT_ready, 1)
                    if att:
                        act.wait_ge(r3_ready, g)
                        act.wait_ge(x2_ready, g + 1)
                        sc.copy(x2r[:, :, :], x2[:, :, :]).then_inc(x2r_ready, 1)
                return run

            act.wait_ge(pe_bias, 1)
            sc.copy(bias_o[:, :], xs_ps[:, 0:P])
            sc.copy(bias_x[:, :], xs_ps[:, P:2 * P]).then_inc(bias_ready, 1)
            walk(None, run_att(0, first=True), tail(0, 0), False, True)
            with act.Fori(1, G) as i:
                walk(run_ffn(i - 1), run_att(i), tail(i - 1, i), True, True)
            walk(run_ffn(G - 1), None, tail(G - 1, 0), True, False)

        @block.vector
        def _(dve):
            ve = nc.vector
            links = [0]

            def link(ins, s, base):
                links[0] += 1
                ins.then_inc(s, 1)
                dve.wait_ge(s, base + links[0])

            dve.wait_ge(params_in, 16 * 18)
            ve.memset(xT[:, :, P:PADT], 0.0)
            ve.memset(Qr[:, :, :, :], 0.0)
            ve.memset(ones[:, :], 1.0)
            ve.memset(minus_half[:, :], -0.5)
            ve.tensor_copy(mrow[:, :], cst_in[:, C_MROW - C_KEEP:C_MROW - C_KEEP + P])
            ve.tensor_copy(mcol[:, :], cst_in[:, C_MCOL - C_KEEP:C_MCOL - C_KEEP + NBLK * BLK])
            ve.tensor_copy(sel[:, :, :], cst_in[:, C_SEL - C_KEEP:].rearrange("p (j m) -> p j m", j=NBLK))
            ve.tensor_scalar(bv2[:, :], cols[:, 2:3], 2.0, None, ALU.mult)
            link(ve.memset(Kt[:, :, P:PADT], 0.0), setup_link, 0)
            ve.tensor_scalar(Kt[:, :, P:PADT], Kt[:, :, P:PADT], cols[:, 1:2], None, ALU.add)
            for s in range(2):
                ve.tensor_copy(Vbd[:, s, :, VW - 1], headv)
            ve.tensor_copy(V5[:, :, :, HD], headv.unsqueeze(1).broadcast_to([P, T, HEADS])).then_inc(dve_setup, 1)

            def stats(r, st, m, ve_out, do_link, base, s):
                for b in range(T):
                    ins = ve.bn_stats(st[:, b, :], r[:, b, :])
                do_link(ins, s, base)
                ve.memset(pause[:, :], 0.0)
                for b in range(T):
                    ins = ve.bn_aggr(m[:, b, :], st[:, b, :])
                do_link(ins, s, base)
                return ve.tensor_scalar(ve_out[:, :], m[:, :, 1], EPS, None, ALU.add)

            def normalise(dst, r, m, rs):
                for b in range(T):
                    ins = ve.tensor_scalar(dst[:, b, :], r[:, b, :], m[:, b, 0:1], rs[:, b:b + 1],
                                           ALU.subtract, ALU.mult)
                return ins

            def run_att(g, first=False):
                base = g * DVE_ATT_LINKS

                def lk(ins):
                    link(ins, att_link, base)

                def step(name, args):
                    if name == "qk":
                        dve.wait_ge(pair_done[PAIR["qk"]], done_at("qk", g))
                        if not first:
                            dve.wait_ge(pair_done[PAIR["sc31"]], done_at("sc31", g - 1))
                        lk(ve.tensor_scalar(Kt[:, :, 0:P],
                                            pair[PAIR["qk"]][:, 1, :].rearrange("p (b t) -> p b t", b=T),
                                            cols[:, 1:2], None, ALU.add))
                        dve.sem_inc(k_ready, 1)
                        dve.sem_inc(pair_free[PAIR["qk"]], 1)
                    elif name == "vn":
                        dve.wait_ge(vH_ready, g + 1)
                        ve.tensor_tensor(vL[:, :], pair[PAIR["vn"]][:, 0, :], vH[:, :].bitcast(F32), ALU.subtract)\
                            .then_inc(vL_ready, 1)
                        dve.wait_ge(vL_ready, g + 1)
                        dve.sem_inc(pair_free[PAIR["vn"]], 1)
                    elif name == "sc":
                        b, j = args
                        nm = f"sc{b}{j}"
                        dve.wait_ge(pair_done[PAIR[nm]], done_at(nm, g))
                        v = pair[PAIR[nm]][:, :, 0:NBLK * BLK].rearrange("p a (j k) -> p a j k", j=NBLK)
                        m = smax[:, :].rearrange("p (a j) -> p a j", a=2)
                        lk(ve.tensor_reduce(m, v, AX, ALU.max))
                        if (b, j) == (0, 0):
                            dve.wait_ge(x2L_ready, g)
                        for gl in range(2):
                            ins = ve.tensor_tensor(S[:, b, 2 * j + gl], v[:, gl],
                                                   m[:, gl].unsqueeze(2).broadcast_to([P, NBLK, BLK]), ALU.subtract)
                            if gl == 0:
                                ins.then_inc(att_link, 1)
                                links[0] += 1
                        ins.then_inc(s_ready, 1)
                        dve.wait_ge(s_ready, 2 * T * g + 2 * b + j + 1)
                        dve.sem_inc(pair_free[PAIR[nm]], 1)
                    elif name == "vr":
                        b, = args
                        nm = f"vr{b}"
                        dve.wait_ge(pair_done[PAIR[nm]], done_at(nm, g))
                        if b:
                            dve.wait_ge(pair_done[PAIR[f"av{b - 1}A"]], done_at(f"av{b - 1}A", g))
                        else:
                            if not first:
                                dve.wait_ge(pair_done[PAIR["av3A"]], done_at("av3A", g - 1))
                        hv = headv.unsqueeze(1).unsqueeze(3).broadcast_to([P, NLOC, HEADS, HD])
                        for s in range(2):
                            src = pair[PAIR[nm]][:, s, :].rearrange("p (k h d) -> p k h d", k=NLOC, h=HEADS)
                            dst = Vbd[:, s, :, 0:VW - 1].rearrange("p h (k d) -> p k h d", k=NLOC)
                            ins = ve.tensor_tensor(dst, src, hv, ALU.mult)
                        ins.then_inc(v_ready, 1)
                        dve.wait_ge(v_ready, T * g + b + 1)
                        dve.sem_inc(pair_free[PAIR[nm]], 1)
                    elif name == "v5":
                        dve.wait_ge(pair_done[PAIR["v5"]], done_at("v5", g))
                        if not first:
                            dve.wait_ge(pair_done[PAIR["av35"]], done_at("av35", g - 1))
                        src = pair[PAIR["v5"]][:, 0, :].rearrange("p (b h d) -> p b h d", b=T, h=HEADS)
                        ve.tensor_tensor(V5[:, :, :, 0:HD], src,
                                         headv.unsqueeze(1).unsqueeze(3).broadcast_to([P, T, HEADS, HD]),
                                         ALU.mult).then_inc(v5_ready, 1)
                        dve.wait_ge(v5_ready, g + 1)
                        dve.sem_inc(pair_free[PAIR["v5"]], 1)
                    elif name == "tr":
                        b, = args
                        dve.wait_ge(p_ready, T * g + b + 1)
                        if b:
                            dve.wait_ge(pair_done[PAIR[f"av{b - 1}5"]], done_at(f"av{b - 1}5", g))
                        else:
                            if not first:
                                dve.wait_ge(pair_done[PAIR["av35"]], done_at("av35", g - 1))
                        ve.transpose(Pt[:, :, :, :].rearrange("p g j k -> p (g j k)"),
                                     S[:, b].rearrange("p g j k -> p (g j k)")).then_inc(pt_ready, 1)
                    elif name == "av":
                        b, which = args
                        nm = f"av{b}{which}"
                        dve.wait_ge(pair_done[PAIR[nm]], done_at(nm, g))
                        v = pair[PAIR[nm]][:, :, 0:2 * QUAD * VW].rearrange("p a (h c) -> p a h c", c=VW)
                        rs = rsum[:, :].rearrange("p (a h) -> p a h", a=2)
                        lk(ve.reciprocal(rs, v[:, :, :, VW - 1]))
                        o = (oL if which == "L" else oA)[:, b, :].rearrange("p (a h d) -> p a h d", a=2, d=HD)
                        for k in range(NLOC):
                            q = slice(BLK * k, BLK * (k + 1))
                            ins = ve.tensor_tensor(o[q], v[q, :, :, HD * k:HD * (k + 1)],
                                                   rs[q].unsqueeze(3).broadcast_to([BLK, 2, HEADS // 2, HD]), ALU.mult)
                            if k < NLOC - 1:
                                ins.then_inc(att_link, 1)
                                links[0] += 1
                        lk(ins)
                        dve.sem_inc(pair_free[PAIR[nm]], 1)
                    elif name == "av5":
                        b, = args
                        nm = f"av{b}5"
                        dve.wait_ge(pair_done[PAIR[nm]], done_at(nm, g))
                        v = pair[PAIR[nm]][0:BLK, 0, 0:HEADS * (HD + 1)].rearrange("p (h c) -> p h c", c=HD + 1)
                        lk(ve.reciprocal(rsum[0:BLK, :], v[:, :, HD]))
                        lk(ve.tensor_tensor(o5[0:BLK, b, :].rearrange("p (h d) -> p h d", d=HD), v[:, :, 0:HD],
                                            rsum[0:BLK, :].unsqueeze(2).broadcast_to([BLK, HEADS, HD]), ALU.mult))
                        dve.sem_inc(pair_free[PAIR[nm]], 1)
                        if b == T - 1:
                            dve.sem_inc(o_ready, 1)
                    elif name == "ot":
                        dve.wait_ge(oTl_ready, g + 1)
                        src = pair[PAIR["ot"]][:, 1, :].rearrange("p (b t) -> p b t", b=T)
                        dst = oT[:, :, :].rearrange("p b (i r) -> p b r i", r=DIL)
                        for r in range(DIL):
                            d = dst[:, :, r, 0:BLK]
                            ins = ve.tensor_tensor(d, d, src[:, :, r * BLK:(r + 1) * BLK], ALU.add)
                            ins.then_inc(att_link, 1)
                            links[0] += 1
                        n_last = -(-(P - DIL * BLK - 1) // DIL)
                        for r in range(2):
                            d = dst[:, :, r, BLK:BLK + n_last]
                            ins = ve.tensor_tensor(d, d, src[:, :, DIL * BLK + r * CHUNK:DIL * BLK + r * CHUNK + n_last],
                                                   ALU.add)
                            if r == 0:
                                ins.then_inc(att_link, 1)
                                links[0] += 1
                        lk(ins)
                        dve.sem_inc(pair_free[PAIR["ot"]], 1)
                    elif name == "ot5":
                        dve.wait_ge(pair_done[PAIR["ot5"]], done_at("ot5", g))
                        src = pair[PAIR["ot5"]][:, 0, :].rearrange("p (b t) -> p b t", b=T)
                        n_last = (P - DIL * BLK - 2 + DIL - 1) // DIL
                        d = oT[:, :, :].rearrange("p b (i r) -> p b r i", r=DIL)[:, :, 2, BLK:BLK + n_last]
                        lk(ve.tensor_tensor(d, d, src[:, :, CHUNK:CHUNK + n_last], ALU.add))
                        dve.sem_inc(oT_ready, 1)
                        dve.sem_inc(pair_free[PAIR["ot5"]], 1)
                    elif name == "wo":
                        dve.wait_ge(pair_done[PAIR["wo"]], done_at("wo", g))
                        dve.wait_ge(xb_ready, 2 * g + 1)
                        lk(ve.tensor_tensor(r1, pair[PAIR["wo"]][:, 0, :].rearrange("p (b d) -> p b d", b=T),
                                            xb[:, :, :], ALU.add))
                        dve.sem_inc(pair_free[PAIR["wo"]], 1)
                        stats(r1, bst, mv, vareps, link, base, att_link).then_inc(var_ready, 1)
                    elif name == "ln1":
                        dve.wait_ge(rstd_ready, 2 * g + 1)
                        normalise(x1, r1, mv, rstd).then_inc(x1_ready, 1)
                    elif name == "sx":
                        dve.wait_ge(pair_done[PAIR["sx"]], done_at("sx", g))
                        v = pair[PAIR["sx"]][:, 0, 0:T * LC].rearrange("p (b k) -> p b k", b=T)
                        lk(ve.tensor_reduce(xmax[:, :], v, AX, ALU.max))
                        lk(ve.tensor_tensor(Px, v, xmax[:, :].unsqueeze(2).broadcast_to([P, T, LC]), ALU.subtract))
                        dve.sem_inc(sx_ready, 1)
                        dve.sem_inc(pair_free[PAIR["sx"]], 1)
                    elif name == "ex":
                        dve.wait_ge(ex_ready, g + 1)
                        lk(ve.tensor_reduce(xsum[:, :], Px, AX, ALU.add))
                        lk(ve.reciprocal(xrec[:, :], xsum[:, :]))
                    elif name == "ax":
                        dve.wait_ge(pair_done[PAIR["ax"]], done_at("ax", g))
                        dve.wait_ge(x1b_ready, g + 1)
                        for b in range(T):
                            ins = ve.scalar_tensor_tensor(r2[:, b, :], pair[PAIR["ax"]][:, 0, b * P:(b + 1) * P],
                                                          xrec[:, b:b + 1], xb[:, b, :], ALU.mult, ALU.add)
                        lk(ins)
                        dve.sem_inc(pair_free[PAIR["ax"]], 1)
                        stats(r2, bst, mv, vareps, link, base, att_link).then_inc(var_ready, 1)
                    elif name == "ln2":
                        dve.wait_ge(rstd_ready, 2 * g + 2)
                        if not first:
                            dve.wait_ge(pair_done[PAIR["x2t"]], done_at("x2t", g - 1))
                        dve.wait_ge(xs_ready, E * g)
                        dve.wait_ge(x2r_ready, g)
                        normalise(x2, r2, mv, rstd).then_inc(x2_ready, 1)
                    elif name == "rt":
                        dve.wait_ge(pair_done[PAIR["rt"]], done_at("rt", g))
                        v = pair[PAIR["rt"]][:, 0, 0:T * 2 * E].rearrange("p (s e) -> p s e", e=E)
                        lk(ve.tensor_reduce(lmax[:, :], v, AX, ALU.max))
                        lk(ve.tensor_tensor(lg[:, :, :], v, lmax[:, :].unsqueeze(2).broadcast_to([P, 2 * T, E]),
                                            ALU.subtract))
                        dve.sem_inc(lg_ready, 1)
                        dve.sem_inc(pair_free[PAIR["rt"]], 1)
                    elif name == "cw":
                        dve.wait_ge(elg_ready, g + 1)
                        lk(ve.tensor_reduce(lsum[:, :], lg[:, :, :], AX, ALU.add))
                        lk(ve.reciprocal(lrec[:, :], lsum[:, :]))
                        lk(ve.tensor_tensor(lg[:, :, :], lg[:, :, :],
                                            lrec[:, :].unsqueeze(2).broadcast_to([P, 2 * T, E]), ALU.mult))
                        v = lg[:, :, :].rearrange("p (b s) e -> p b s e", s=2)
                        lk(ve.tensor_tensor(v[:, :, 0, :], v[:, :, 0, :], v[:, :, 1, :], ALU.mult))
                        lk(ve.tensor_reduce(csum[:, :], v[:, :, 0, :], AX, ALU.add))
                        lk(ve.tensor_scalar(csum[:, :], csum[:, :], 1e-9, None, ALU.add))
                        lk(ve.reciprocal(crec[:, :], csum[:, :]))
                        ve.tensor_tensor(cw[:, :, :], v[:, :, 0, :],
                                         crec[:, :].unsqueeze(2).broadcast_to([P, T, E]), ALU.mult).then_inc(cw_ready, 1)
                return step

            def scaled_low(f, e):
                dve.wait_ge(xsH_ready, E * f + e + 1)
                ve.tensor_tensor(xsL[:, e % 2, :], xs_ps[:, :], xsH[:, e % 2, :].bitcast(F32), ALU.subtract)\
                    .then_inc(xsL_ready, 1)

            def run_ffn(f):
                def chunk(n):
                    dve.wait_ge(silu_ready, NCH * f + n + 1)
                    dve.wait_ge(up_done, NCH * f + n + 1)
                    ve.tensor_tensor(sh[:, n % 4, :], sh[:, n % 4, :], up_ps[:, :], ALU.mult).then_inc(h_ready, 1)
                    if n % FC == 3 and n // FC + 1 < E:
                        scaled_low(f, n // FC + 1)
                return chunk

            def tail(f, g):
                def run(ffn, att):
                    if att:
                        scaled_low(g, 0)
                    if ffn:
                        dve.wait_ge(yt_done, f + 1)
                        dve.wait_ge(x2r_ready, f + 1)
                        n0 = links[0]
                        links[0] = 0
                        fb = f * DVE_FFN_LINKS
                        link(ve.tensor_tensor(yo[:, :, :], y_ps[:, :].rearrange("p (b d) -> p b d", b=T),
                                              x2r[:, :, :], ALU.add), ffn_link, fb)
                        dve.sem_inc(r3_ready, 1)
                        stats(yo, bst3, mv3, vareps3, link, fb, ffn_link).then_inc(var3_ready, 1)
                        dve.wait_ge(rstd3_ready, f + 1)
                        normalise(yo, yo, mv3, rstd3).then_inc(out_ready, 1)
                        assert links[0] == DVE_FFN_LINKS, links
                        links[0] = n0
                    assert not att or links[0] == DVE_ATT_LINKS, links
                    links[0] = 0
                return run

            links[0] = 0
            walk(None, run_att(0, first=True), tail(0, 0), False, True)
            with dve.Fori(1, G) as i:
                walk(run_ffn(i - 1), run_att(i), tail(i - 1, i), True, True)
            walk(run_ffn(G - 1), None, tail(G - 1, 0), True, False)

        @block.gpsimd
        def _(pool):
            po = nc.gpsimd
            pool.wait_ge(bias_ready, 1)

            def run_att(g, first=False):
                def step(name, args):
                    if name == "xt":
                        pool.wait_ge(x_loaded, 16 * g + 16)
                        pool.wait_ge(x2_ready, g)
                        po.tensor_tensor(xb[:, :, :], x_in[:, :, :],
                                         bias_o[:, :].unsqueeze(1).broadcast_to([P, T, P]), ALU.add)\
                            .then_inc(xb_ready, 1)
                    elif name == "qe":
                        b, = args
                        pool.wait_ge(q_ready, g + 1)
                        if b >= 2:
                            pool.wait_ge(pair_done[PAIR[f"sc{b - 2}1"]], done_at(f"sc{b - 2}1", g))
                        else:
                            if not first:
                                pool.wait_ge(pair_done[PAIR["ot5"]], done_at("ot5", g - 1))
                        po.tensor_tensor(Qbd[:, b % 2], Qr[:, b].unsqueeze(2).broadcast_to([P, NBLK, QUAD, BLK]),
                                         headq.unsqueeze(1).unsqueeze(3).broadcast_to([P, NBLK, QUAD, BLK]),
                                         ALU.mult).then_inc(qbd_ready, 1)
                    elif name == "wo":
                        pool.wait_ge(var_ready, 2 * g + 1)
                        po.tensor_tensor(rstd[:, :], vareps[:, :], minus_half[:, :], ALU.pow).then_inc(rstd_ready, 1)
                    elif name == "x1t":
                        pool.wait_ge(x1_ready, g + 1)
                        po.tensor_tensor(xb[:, :, :], x1, bias_x[:, :].unsqueeze(1).broadcast_to([P, T, P]), ALU.add)\
                            .then_inc(x1b_ready, 1)
                        pool.wait_ge(x1b_ready, g + 1)
                        pool.sem_inc(xb_ready, 1)
                    elif name == "ax":
                        pool.wait_ge(var_ready, 2 * g + 2)
                        po.tensor_tensor(rstd[:, :], vareps[:, :], minus_half[:, :], ALU.pow).then_inc(rstd_ready, 1)
                    elif name == "piece":
                        n, = args
                        pool.wait_ge(piece_hi, n + 1)
                        po.tensor_tensor(wL[:, n // E, n % E, :], sh[:, n % 4, :],
                                         wH[:, n // E, n % E, :].bitcast(F32), ALU.subtract).then_inc(piece_lo, 1)
                return step

            def scaled(f, e):
                pool.wait_ge(xsT_done, E * f + e)
                po.tensor_tensor(xs[:, :, :], x2[:, :, :], cw[:, :, e:e + 1].broadcast_to([P, T, P]), ALU.mult)\
                    .then_inc(xs_ready, 1)

            def low(f, n):
                pool.wait_ge(hH_ready, NCH * f + n + 1)
                po.tensor_tensor(hL[:, n % 2, :], sh[:, n % 4, :], hH[:, n % 2, :].bitcast(F32), ALU.subtract)\
                    .then_inc(hL_ready, 1)

            def run_ffn(f):
                def chunk(n):
                    if n % FC == 0 and n // FC + 1 < E:
                        scaled(f, n // FC + 1)
                    if n >= 1:
                        low(f, n - 1)
                return chunk

            def tail(f, g):
                def run(ffn, att):
                    if ffn:
                        low(f, NCH - 1)
                    if att:
                        pool.wait_ge(cw_ready, g + 1)
                        scaled(g, 0)
                        pool.wait_ge(x2H_ready, g + 1)
                        po.tensor_tensor(x2L[:, :], x2T, x2H[:, :].bitcast(F32), ALU.subtract).then_inc(x2L_ready, 1)
                    if ffn:
                        pool.wait_ge(var3_ready, f + 1)
                        po.tensor_tensor(rstd3[:, :], vareps3[:, :], minus_half[:, :], ALU.pow).then_inc(rstd3_ready, 1)
                return run

            walk(None, run_att(0, first=True), tail(0, 0), False, True)
            with pool.Fori(1, G) as i:
                walk(run_ffn(i - 1), run_att(i), tail(i - 1, i), True, True)
            walk(run_ffn(G - 1), None, tail(G - 1, 0), True, False)


def kernel(**inputs):
    import concourse.bacc as bacc
    from concourse.bass_utils import run_bass_kernel_spmd

    names = {"x": "x", "ctx": "ctx_768", "bq": "L0_attn_bq", "bk": "L0_attn_bk", "bv": "L0_attn_bv",
             "bo": "L0_attn_bo", "Wxq": "L0_xattn_Wq", "Wxk": "L0_xattn_Wk", "Wxv": "L0_xattn_Wv",
             "bxq": "L0_xattn_bq", "bxk": "L0_xattn_bk", "bxv": "L0_xattn_bv",
             "w_router": "L0_ffn_w_router", "w_gating": "L0_ffn_w_gating", "w_gate": "L0_ffn_w_gate",
             "w_up": "L0_ffn_w_up", "w_down": "L0_ffn_w_down"}
    arrays = {k: np.ascontiguousarray(inputs[v]) for k, v in names.items()}
    for k in ("q", "k", "v", "o"):
        arrays[f"W{k}T"] = np.ascontiguousarray(np.asarray(inputs[f"L0_attn_W{k}"]).T)
    arrays["cst"] = constants()

    nc = bacc.Bacc("TRN2", target_bir_lowering=False, num_devices=1)
    aps = {k: nc.dram_tensor(f"in_{k}", a.shape, mybir.dt.from_np(a.dtype), kind="ExternalInput").ap()
           for k, a in arrays.items()}
    out = nc.dram_tensor("out", arrays["x"].shape, F32, kind="ExternalOutput").ap()
    build_decoder(nc, out=out, **aps)
    r = run_bass_kernel_spmd(nc, [{f"in_{k}": a for k, a in arrays.items()}], core_ids=[0])
    return r.results[0]["out"]
```

```python
from contextlib import ExitStack

import numpy as np
import concourse.bass as bass
from concourse import mybir

ALU = mybir.AluOpType
ACT = mybir.ActivationFunctionType
F32 = mybir.dt.float32
F32R = mybir.dt.float32r
BF16 = mybir.dt.bfloat16
AX = mybir.AxisListType.X

P = 128
HEADS, HD = 16, 8
CHUNK, DIL = 16, 3
QUAD = 4
NQ = HEADS // QUAD
BLK = 2 * CHUNK
PADT = 144
NLOC, NATR = 4, 5
NBLK = NLOC + NATR
T = 4
EPS = 1e-5
MASKED = -1e30
BANK = 512
SBLK = 8
VW = NLOC * HD + 1

C_ID = 0
C_HEADV = C_ID + P
C_HEADQ = C_HEADV + HEADS
C_KEEP = C_HEADQ + QUAD
C_MROW = C_KEEP
C_MCOL = C_MROW + P
C_SEL = C_MCOL + BANK
C_ALL = C_SEL + NBLK * P


def block_tokens(j):
    if j < NLOC:
        return [BLK * j + k for k in range(BLK)]
    if j < NLOC + DIL:
        return [(j - NLOC) + DIL * k for k in range(BLK)]
    r0 = j - NLOC - DIL
    return [DIL * (BLK + k % CHUNK) + r0 + k // CHUNK for k in range(BLK)]


def constants():
    c = np.zeros((P, C_ALL), np.float32)
    p = np.arange(P)
    c[:, C_ID:C_ID + P] = np.eye(P)
    c[:, C_HEADV:C_HEADV + HEADS] = (np.arange(HEADS)[None] % QUAD) == (p[:, None] // 32)
    c[:, C_HEADQ:C_HEADQ + QUAD] = np.arange(QUAD)[None] == (p[:, None] % 32) // HD
    half = (np.arange(P) % BLK) // CHUNK
    khalf = (np.arange(BANK) % BLK) // CHUNK
    for s in range(2):
        c[s, C_MROW:C_MROW + P] = half == s
        c[s, C_MCOL:C_MCOL + BANK] = np.where(khalf == s, 0.0, MASKED)
    for j in range(NBLK):
        for k, t in enumerate(block_tokens(j)):
            if t < P:
                for h in range(QUAD):
                    c[t, C_SEL + j * P + h * BLK + k] = 1.0
    return c


JOBS = [("xt", 1), ("qk", 2), ("vn", 1)]
JOBS += [(f"sc{b}", 1) for b in range(T)] + [("sc_last", 1)]
JOBS += [("vr0", 1), ("v5", 1)]
for _b in range(T):
    JOBS += [(f"av{_b}L", 1), (f"av{_b}A", 1), (f"av{_b}5", 1)]
    if _b + 1 < T:
        JOBS += [(f"vr{_b + 1}", 1)]
JOBS += [("ot", 1), ("ot5", 1), ("kv", 1), ("wo", 1), ("x1t", 1), ("qx", 1), ("sx", 1), ("pt", 1),
         ("ax", 1), ("x2t", 1), ("rt", 1)]
assert len(JOBS) % 2 == 0
PAIR, DONE_AT, FREED_BEFORE = {}, {}, {}
_done, _freed = [0, 0], [0, 0]
for _n, (_name, _k) in enumerate(JOBS):
    PAIR[_name] = _n % 2
    FREED_BEFORE[_name] = _freed[_n % 2]
    _done[_n % 2] += 1
    _freed[_n % 2] += _k
    DONE_AT[_name] = _done[_n % 2]
DONE_PER, FREED_PER = tuple(_done), tuple(_freed)

STEPS = [[[], [], []] for _ in range(32)]
STEPS[0] = [("xt",)], [], []
STEPS[1] = [("qk",), ("qe", 0)], [("vn",)], [("qe", 1)]
STEPS[3] = [("sc", 0, 0)], [("sc", 0, 1)], [("qe", 2)]
STEPS[4] = [("sc", 1, 0)], [("sc", 1, 1)], [("qe", 3)]
STEPS[5] = [("sc", 2, 0)], [("sc", 2, 1)], [("qe_last",)]
STEPS[6] = [("sc", 3, 0)], [("sc", 3, 1)], []
STEPS[7] = [("sc_last",), ("exps",)], [("vr", 0)], [("v5",)]
STEPS[8] = [], [], [("tr", 0)]
for _b in range(T):
    STEPS[9 + 2 * _b] = [("av", _b, "L")], [("av", _b, "A")], []
    STEPS[10 + 2 * _b] = [("av5", _b)], [("vr", _b + 1), ("tr", _b + 1)] if _b < 3 else [("ot",)], []
STEPS[17] = [("ot5",)], [("kv",)], []
STEPS[18] = [("wo",)], [], []
STEPS[19] = [("ln1",)], [], []
STEPS[20] = [("x1t",)], [], []
STEPS[21] = [("qx",)], [], []
STEPS[22] = [("sx",)], [], []
STEPS[23] = [("ex",)], [], []
STEPS[24] = [("pt",)], [], []
STEPS[25] = [("ax",)], [], []
STEPS[26] = [], [("ln2",)], []
STEPS[27] = [], [("x2t",)], []
STEPS[28] = [("rt",)], [], []
STEPS[29] = [("cw",)], [], []
DVE_ATT_LINKS = 79
DVE_FFN_LINKS = 3


def build_decoder(nc, x, ctx, cst, WqT, WkT, WvT, WoT, bq, bk, bv, bo, Wxq, Wxk, Wxv, bxq, bxk, bxv,
                  w_router, w_gating, w_gate, w_up, w_down, out):
    B, L, D = x.shape
    _, LC, DC = ctx.shape
    E, _, F = w_gate.shape
    G = B // T
    FC = F // P
    NCH = E * FC
    TOK = T * P
    SELF_SCALE = float(HD) ** -0.5
    CROSS_SCALE = float(D) ** -0.5
    PIECES = 3 * E
    assert L == P and D == P and F == 4 * P and NCH == 32 and G * T == B

    with ExitStack() as stack:
        def sb(name, shape, dt=F32):
            return stack.enter_context(nc.sbuf_tensor(name, shape, dt))

        def ps(name, shape):
            return stack.enter_context(nc.psum_tensor(name, shape, F32))

        def sem(name):
            return stack.enter_context(nc.semaphore(name))

        pair = [ps("pair0", [P, 2, 512]), ps("pair1", [P, 2, 512])]
        gate_ps, up_ps, y_ps, xs_ps = (ps(n, [P, 512]) for n in ("gate_ps", "up_ps", "y_ps", "xs_ps"))

        cs = sb("cs", [P, C_KEEP])
        ident = cs[:, C_ID:C_ID + P]
        headv = cs[:, C_HEADV:C_HEADV + HEADS]
        headq = cs[:, C_HEADQ:C_HEADQ + QUAD]
        wqT, wkT, wvT, woT, wxq = (sb(n, [P, P]) for n in ("wqT", "wkT", "wvT", "woT", "wxq"))
        wxk, wxv = sb("wxk", [DC, P]), sb("wxv", [DC, P])
        wrg = sb("wrg", [P, 2 * E])
        cols = sb("cols", [P, 5])
        rows = sb("rows", [1, 2 * P])
        mrow = sb("mrow", [P, P], BF16)
        mcol = sb("mcol", [P, BANK], BF16)
        sel = sb("sel", [P, NBLK, P], F32R)
        ones = sb("ones", [1, P])
        bv2 = sb("bv2", [P, 1])
        bkq = sb("bkq", [P, NQ])
        bias_o = sb("bias_o", [P, P])
        bias_x = sb("bias_x", [P, P])
        minus_half = sb("minus_half", [P, T])
        wH = sb("wH", [P, 3, E, 512], F32R)
        wL = sb("wL", [P, 3, E, 512], F32R)
        sh = sb("sh", [P, 4, 512])
        hH, hL = sb("hH", [P, 2, 512], F32R), sb("hL", [P, 2, 512], F32R)
        xs = sb("xs", [P, T, P])
        xsH, xsL = sb("xsH", [P, 2, 512], F32R), sb("xsL", [P, 2, 512], F32R)
        x2H, x2L = sb("x2H", [P, 512], F32R), sb("x2L", [P, 512], F32R)
        x2r = sb("x2r", [P, T, P])
        yo = sb("yo", [P, T, P])
        x_in = sb("x_in", [P, T, P])
        xb = sb("xb", [P, T, P])
        ctx_in = sb("ctx_in", [LC, T, DC])
        xT = sb("xT", [P, T, PADT])
        late = sb("late", [P, NQ * T * PADT])
        Kq = late[:, :].rearrange("p (g b t) -> p g b t", g=NQ, b=T)
        Pt = late[:, 0:NQ * NBLK * BLK].rearrange("p (g j k) -> p g j k", g=NQ, j=NBLK)
        oT = late[:, NQ * NBLK * BLK:NQ * NBLK * BLK + T * PADT].rearrange("p (b t) -> p b t", b=T)
        Qr = sb("Qr", [P, T, NBLK, BLK])
        vH, vL = sb("vH", [P, TOK], F32R), sb("vL", [P, TOK], F32R)
        qo = sb("qo", [P, (2 * SBLK + T) * P])
        Qbd = qo[:, 0:2 * SBLK * P].rearrange("p (b j h k) -> p b j h k", b=2, j=SBLK, h=QUAD)
        Qbd_last = qo[:, 2 * SBLK * P:].rearrange("p (b h k) -> p b h k", b=T, h=QUAD)
        oL = qo[:, 0:TOK].rearrange("p (b c) -> p b c", b=T)
        oA = qo[:, TOK:2 * TOK].rearrange("p (b c) -> p b c", b=T)
        o5 = qo[:, 2 * TOK:3 * TOK].rearrange("p (b c) -> p b c", b=T)
        big = sb("big", [P, T * NQ * NBLK * BLK])
        S = big[:, :].rearrange("p (b g j k) -> p b g j k", b=T, g=NQ, j=NBLK)
        Vbd = sb("Vbd", [P, 2, HEADS, VW])
        V5 = sb("V5", [P, T, HEADS, HD + 1])
        ctxT = sb("ctxT", [DC, T * LC])
        KxT = sb("KxT", [P, T, LC])
        at = 0
        views = []
        for width in (TOK, TOK, T * LC, TOK, TOK, TOK, TOK, TOK, TOK):
            views.append(big[:, at:at + width])
            at += width + width % 2
        assert at <= T * NQ * NBLK * BLK
        x1T, QxT = views[0], views[1].rearrange("p (b t) -> p b t", b=T)
        Px = views[2].rearrange("p (b k) -> p b k", b=T)
        PxT = views[3][0:LC, :].rearrange("p (b t) -> p b t", b=T)
        r1, r2, x1 = (views[n].rearrange("p (b d) -> p b d", b=T) for n in (4, 5, 6))
        x2T = views[7]
        Vx = views[8][0:LC, :].rearrange("p (b d) -> p b d", b=T)
        x2 = sb("x2", [P, T, P])
        cst_in = big[:, 0:C_ALL - C_KEEP]
        smax = sb("smax", [P, SBLK * NQ])
        rsum = sb("rsum", [P, HEADS])
        bst = sb("bst", [P, T, 6])
        pause = sb("pause", [P, 1])
        mv = sb("mv", [P, T, 2])
        vareps = sb("vareps", [P, T])
        rstd = sb("rstd", [P, T])
        bst3, mv3 = sb("bst3", [P, T, 6]), sb("mv3", [P, T, 2])
        vareps3, rstd3 = sb("vareps3", [P, T]), sb("rstd3", [P, T])
        xmax, xsum, xrec = sb("xmax", [P, T]), sb("xsum", [P, T]), sb("xrec", [P, T])
        lg = sb("lg", [P, 2 * T, E])
        lmax, lsum, lrec = (sb(n, [P, 2 * T]) for n in ("lmax", "lsum", "lrec"))
        cw = sb("cw", [P, T, E])
        csum, crec = sb("csum", [P, T]), sb("crec", [P, T])

        params_in = sem("params_in")
        piece_in = [sem(f"piece_in{n}") for n in range(4)]
        x_loaded, ctx_loaded, out_stored = sem("x_loaded"), sem("ctx_loaded"), sem("out_stored")
        dve_setup, pe_bias, bias_ready, act_setup = sem("dve_setup"), sem("pe_bias"), sem("bias_ready"), sem("act_setup")
        piece_hi, piece_lo = sem("piece_hi"), sem("piece_lo")
        pair_done = [sem("pair_done0"), sem("pair_done1")]
        pair_free = [sem("pair_free0"), sem("pair_free1")]
        xT_ready, q_ready, k_ready, xb_ready = sem("xT_ready"), sem("q_ready"), sem("k_ready"), sem("xb_ready")
        qbd_ready, qlast_ready, vH_ready, vL_ready = sem("qbd_ready"), sem("qlast_ready"), sem("vH_ready"), sem("vL_ready")
        ctxT_ready, kx_ready, vx_ready = sem("ctxT_ready"), sem("kx_ready"), sem("vx_ready")
        s_ready, p_ready, pt_ready = sem("s_ready"), sem("p_ready"), sem("pt_ready")
        v_ready, v5_ready, o_ready = sem("v_ready"), sem("v5_ready"), sem("o_ready")
        oTl_ready, oT_ready = sem("oTl_ready"), sem("oT_ready")
        var_ready, rstd_ready = sem("var_ready"), sem("rstd_ready")
        x1_ready, x1b_ready, x1T_ready, qx_ready = sem("x1_ready"), sem("x1b_ready"), sem("x1T_ready"), sem("qx_ready")
        sx_ready, ex_ready, pxT_ready = sem("sx_ready"), sem("ex_ready"), sem("pxT_ready")
        x2_ready, x2T_ready, lg_ready, elg_ready, cw_ready = (sem(n) for n in (
            "x2_ready", "x2T_ready", "lg_ready", "elg_ready", "cw_ready"))
        x2H_ready, x2L_ready, x2r_ready = sem("x2H_ready"), sem("x2L_ready"), sem("x2r_ready")
        xs_ready, xsT_done, xsH_ready, xsL_ready = sem("xs_ready"), sem("xsT_done"), sem("xsH_ready"), sem("xsL_ready")
        gate_done, up_done, down_done = sem("gate_done"), sem("up_done"), sem("down_done")
        silu_ready, h_ready, hH_ready, hL_ready = sem("silu_ready"), sem("h_ready"), sem("hH_ready"), sem("hL_ready")
        yT_ready, yt_done, r3_ready, var3_ready, rstd3_ready, out_ready = (sem(n) for n in (
            "yT_ready", "yt_done", "r3_ready", "var3_ready", "rstd3_ready", "out_ready"))
        att_link, ffn_link, setup_link = sem("att_link"), sem("ffn_link"), sem("setup_link")

        def done_at(name, g):
            return g * DONE_PER[PAIR[name]] + DONE_AT[name]

        def freed_at(name, g):
            return g * FREED_PER[PAIR[name]] + FREED_BEFORE[name]

        def walk(run_ffn, run_att, tail, ffn, att):
            for n in range(NCH):
                for place in range(3):
                    if ffn:
                        run_ffn(n, place)
                    if att:
                        for name, *args in STEPS[n][place]:
                            run_att(name, args)
                if not ffn and att and n < PIECES:
                    run_att("piece", (n,))
            tail(ffn, att)

        def tokens(view, j):
            if j < NLOC:
                return view[..., BLK * j:BLK * (j + 1)]
            v = view.rearrange("p b (i r) -> p b r i", r=DIL) if len(view.shape) == 3 else \
                view.rearrange("p (i r) -> p r i", r=DIL)
            if j < NLOC + DIL:
                return v[..., j - NLOC, 0:BLK]
            r = j - NLOC - DIL
            return v[..., r:r + 2, BLK:BLK + CHUNK]

        block = stack.enter_context(nc.Block())

        @block.sync
        def _(sp):
            n_params = 0
            for dst, src in ((cs[:, :], cst[:, 0:C_KEEP]), (cst_in, cst[:, C_KEEP:C_ALL]), (wqT[:, :], WqT), (wkT[:, :], WkT), (wvT[:, :], WvT),
                             (woT[:, :], WoT), (wxq[:, :], Wxq), (wxk[:, :], Wxk), (wxv[:, :], Wxv),
                             (wrg[:, 0:E], w_router), (wrg[:, E:2 * E], w_gating),
                             (cols[:, 0:1], bq), (cols[:, 1:2], bk), (cols[:, 2:3], bv),
                             (cols[:, 3:4], bxq), (cols[:, 4:5], bxk)):
                if len(src.shape) == 1:
                    src = src.rearrange("(p a) -> p a", a=1)
                sp.dma_start(dst, src).then_inc(params_in, 16)
            for n, src in enumerate((bo, bxv)):
                sp.dma_start(rows[:, n * P:(n + 1) * P], src.rearrange("(a n) -> a n", a=1)).then_inc(params_in, 16)

            def load(g, first=False):
                if not first:
                    sp.wait_ge(pair_done[PAIR["xt"]], done_at("xt", g - 1))
                    sp.wait_ge(xb_ready, 2 * (g - 1) + 1)
                sp.dma_start(x_in[:, :, :], x[bass.ds(g * T, T)].rearrange("b t d -> t b d")).then_inc(x_loaded, 16)
                sp.dma_start(ctx_in[:, :, :], ctx[bass.ds(g * T, T)].rearrange("b t d -> t b d")).then_inc(ctx_loaded, 16)

            def store(f):
                sp.wait_ge(out_ready, f + 1)
                sp.dma_start(out[bass.ds(f * T, T)].rearrange("b t d -> t b d"), yo[:, :, :]).then_inc(out_stored, 16)

            sp.sem_inc(out_stored, 16)
            load(0, first=True)
            for n in range(PIECES):
                if n >= 4:
                    sp.wait_ge(piece_lo, n - 3)
                m, e = n // E, n % E
                src = w_gate[e] if m == 0 else w_up[e] if m == 1 else w_down[e].rearrange("(c p) n -> p c n", p=P)
                dst = sh[:, n % 4, :] if m < 2 else sh[:, n % 4, :].rearrange("p (c n) -> p c n", c=FC)
                sp.dma_start(dst, src).then_inc(piece_in[n % 4], 16)
            load(1)
            with sp.Fori(1, G - 1) as i:
                load(i + 1)
                store(i - 1)
            store(G - 2)
            store(G - 1)
            sp.wait_ge(out_stored, 16 * (G + 1))

        @block.tensor
        def _(pe):
            nc_pe = nc.tensor
            pe.wait_ge(params_in, 16 * 18)
            pe.wait_ge(dve_setup, 1)
            nc_pe.matmul(xs_ps[:, 0:P], bv2[:, 0:1].broadcast_to([P, P]), woT[:, :], start=True, stop=False)
            nc_pe.matmul(xs_ps[:, 0:P], ones[:, :], rows[:, 0:P], start=False, stop=True)
            nc_pe.matmul(xs_ps[:, P:2 * P], ones[:, :], rows[:, P:2 * P], start=True, stop=True).then_inc(pe_bias, 1)
            pe.wait_ge(bias_ready, 1)

            def run_att(g, first=False):
                def scores(bank, operands):
                    nc_pe.matmul(bank, mrow[0:2, :], mcol[0:2, :], start=True, stop=False)
                    for n, (q, k) in enumerate(operands):
                        ins = nc_pe.matmul(bank[:, n * P:(n + 1) * P], q, k, start=False, stop=(n == len(operands) - 1))
                    return ins

                def transposes(t, src, n_out):
                    for b in range(T):
                        s = src[:, b, :]
                        k = s.shape[0]
                        ins = nc_pe.transpose(t[0:n_out, 0, b * k:(b + 1) * k], s, ident[0:k, 0:k])
                    return ins

                def step(name, args):
                    if name == "xt":
                        pe.wait_ge(x_loaded, 16 * g + 16)
                        pe.wait_ge(ctx_loaded, 16 * g + 16)
                        pe.wait_ge(pair_free[PAIR["xt"]], freed_at("xt", g))
                        t = pair[PAIR["xt"]]
                        for b in range(T):
                            nc_pe.transpose(t[:, 0, b * P:(b + 1) * P], x_in[:, b, :], ident)
                        for b in range(T):
                            ins = nc_pe.transpose(t[0:DC, 1, b * LC:(b + 1) * LC], ctx_in[:, b, :],
                                                  ident[0:LC, 0:LC])
                        ins.then_inc(pair_done[PAIR["xt"]], 1)
                    elif name == "qk":
                        pe.wait_ge(xT_ready, g + 1)
                        pe.wait_ge(pair_free[PAIR["qk"]], freed_at("qk", g))
                        t = pair[PAIR["qk"]]
                        src = xT[:, :, 0:P]
                        nc_pe.matmul(t[:, 0, :], wqT[:, :], src, start=True, stop=True)
                        nc_pe.matmul(t[:, 1, :], wkT[:, :], src, start=True, stop=True).then_inc(pair_done[PAIR["qk"]], 1)
                    elif name == "sc":
                        b, half = args
                        nm = f"sc{b}"
                        if half == 0:
                            pe.wait_ge(qbd_ready, T * g + b + 1)
                            if b == 0:
                                pe.wait_ge(k_ready, g + 1)
                            pe.wait_ge(pair_free[PAIR[nm]], freed_at(nm, g))
                        ins = scores(pair[PAIR[nm]][:, half, :],
                                     [(Qbd[:, b % 2, k], tokens(Kq[:, :, b, :], k))
                                      for k in range(NLOC * half, NLOC * (half + 1))])
                        if half == 1:
                            ins.then_inc(pair_done[PAIR[nm]], 1)
                    elif name == "sc_last":
                        pe.wait_ge(qlast_ready, g + 1)
                        pe.wait_ge(pair_free[PAIR["sc_last"]], freed_at("sc_last", g))
                        scores(pair[PAIR["sc_last"]][:, 0, :],
                               [(Qbd_last[:, b], tokens(Kq[:, :, b, :], NBLK - 1)) for b in range(T)])\
                            .then_inc(pair_done[PAIR["sc_last"]], 1)
                    elif name == "vn":
                        pe.wait_ge(pair_free[PAIR["vn"]], freed_at("vn", g))
                        t = pair[PAIR["vn"]]
                        for b in range(T):
                            ins = nc_pe.matmul(t[:, 0, b * P:(b + 1) * P], xT[:, b, 0:P], wvT[:, :],
                                               start=True, stop=True)
                        ins.then_inc(pair_done[PAIR["vn"]], 1)
                    elif name == "vr":
                        b, = args
                        pe.wait_ge(vH_ready, g + 1)
                        pe.wait_ge(vL_ready, g + 1)
                        pe.wait_ge(pair_free[PAIR[f"vr{b}"]], freed_at(f"vr{b}", g))
                        t = pair[PAIR[f"vr{b}"]]
                        for k in range(2 * NLOC):
                            dst = t[:, k // NLOC, (k % NLOC) * P:(k % NLOC + 1) * P]
                            nc_pe.matmul(dst, sel[:, k, :], vH[:, b * P:(b + 1) * P], start=True, stop=False)
                            ins = nc_pe.matmul(dst, sel[:, k, :], vL[:, b * P:(b + 1) * P], start=False, stop=True)
                        ins.then_inc(pair_done[PAIR[f"vr{b}"]], 1)
                    elif name == "v5":
                        pe.wait_ge(pair_free[PAIR["v5"]], freed_at("v5", g))
                        t = pair[PAIR["v5"]]
                        nc_pe.matmul(t[:, 0, :], sel[:, NBLK - 1, :], vH[:, :], start=True, stop=False)
                        nc_pe.matmul(t[:, 0, :], sel[:, NBLK - 1, :], vL[:, :], start=False, stop=True).then_inc(pair_done[PAIR["v5"]], 1)
                    elif name == "av":
                        b, which = args
                        pe.wait_ge(pt_ready, T * g + b + 1)
                        pe.wait_ge(v_ready, T * g + b + 1)
                        pe.wait_ge(pair_free[PAIR[f"av{b}{which}"]], freed_at(f"av{b}{which}", g))
                        t = pair[PAIR[f"av{b}{which}"]]
                        s = "LA".index(which)
                        for q in range(NQ):
                            ins = nc_pe.matmul(t[:, q // 2, (q % 2) * QUAD * VW:(q % 2 + 1) * QUAD * VW],
                                               Pt[:, q, NLOC * s:NLOC * (s + 1), :],
                                               Vbd[:, s, QUAD * q:QUAD * (q + 1), :], start=True, stop=True)
                        ins.then_inc(pair_done[PAIR[f"av{b}{which}"]], 1)
                    elif name == "av5":
                        b, = args
                        if b == 0:
                            pe.wait_ge(v5_ready, g + 1)
                        pe.wait_ge(pair_free[PAIR[f"av{b}5"]], freed_at(f"av{b}5", g))
                        t = pair[PAIR[f"av{b}5"]]
                        w = QUAD * (HD + 1)
                        for q in range(NQ):
                            ins = nc_pe.matmul(t[0:BLK, 0, q * w:(q + 1) * w], Pt[:, q, NBLK - 1, :],
                                               V5[:, b, QUAD * q:QUAD * (q + 1), :], start=True, stop=True)
                        ins.then_inc(pair_done[PAIR[f"av{b}5"]], 1)
                    elif name == "ot":
                        pe.wait_ge(o_ready, g + 1)
                        pe.wait_ge(pair_free[PAIR["ot"]], freed_at("ot", g))
                        t = pair[PAIR["ot"]]
                        for s, o in enumerate((oL, oA)):
                            for b in range(T):
                                ins = nc_pe.transpose(t[:, s, b * P:(b + 1) * P], o[:, b, :], ident)
                        ins.then_inc(pair_done[PAIR["ot"]], 1)
                    elif name == "ot5":
                        pe.wait_ge(pair_free[PAIR["ot5"]], freed_at("ot5", g))
                        t = pair[PAIR["ot5"]]
                        for b in range(T):
                            ins = nc_pe.transpose(t[:, 0, b * P:(b + 1) * P], o5[:, b, :], ident)
                        ins.then_inc(pair_done[PAIR["ot5"]], 1)
                    elif name == "kv":
                        pe.wait_ge(ctxT_ready, g + 1)
                        pe.wait_ge(pair_free[PAIR["kv"]], freed_at("kv", g))
                        t = pair[PAIR["kv"]]
                        nc_pe.matmul(t[:, 0, 0:T * LC], wxk[:, :], ctxT[:, :], start=True, stop=True)
                        for b in range(T):
                            ins = nc_pe.matmul(t[0:LC, 1, b * P:(b + 1) * P], ctxT[:, b * LC:(b + 1) * LC],
                                               wxv[:, :], start=True, stop=True)
                        ins.then_inc(pair_done[PAIR["kv"]], 1)
                    elif name == "wo":
                        pe.wait_ge(oT_ready, g + 1)
                        pe.wait_ge(pair_free[PAIR["wo"]], freed_at("wo", g))
                        t = pair[PAIR["wo"]]
                        for b in range(T):
                            ins = nc_pe.matmul(t[:, 0, b * P:(b + 1) * P], oT[:, b, 0:P], woT[:, :],
                                               start=True, stop=True)
                        ins.then_inc(pair_done[PAIR["wo"]], 1)
                    elif name == "x1t":
                        pe.wait_ge(x1_ready, g + 1)
                        pe.wait_ge(pair_free[PAIR["x1t"]], freed_at("x1t", g))
                        t = pair[PAIR["x1t"]]
                        transposes(t, x1, P).then_inc(pair_done[PAIR["x1t"]], 1)
                    elif name == "qx":
                        pe.wait_ge(x1T_ready, g + 1)
                        pe.wait_ge(pair_free[PAIR["qx"]], freed_at("qx", g))
                        t = pair[PAIR["qx"]]
                        nc_pe.matmul(t[:, 0, :], wxq[:, :], x1T, start=True, stop=True).then_inc(pair_done[PAIR["qx"]], 1)
                    elif name == "sx":
                        pe.wait_ge(qx_ready, g + 1)
                        pe.wait_ge(kx_ready, g + 1)
                        pe.wait_ge(pair_free[PAIR["sx"]], freed_at("sx", g))
                        t = pair[PAIR["sx"]]
                        for b in range(T):
                            ins = nc_pe.matmul(t[:, 0, b * LC:(b + 1) * LC], QxT[:, b, :], KxT[:, b, :],
                                               start=True, stop=True)
                        ins.then_inc(pair_done[PAIR["sx"]], 1)
                    elif name == "pt":
                        pe.wait_ge(ex_ready, g + 1)
                        pe.wait_ge(pair_free[PAIR["pt"]], freed_at("pt", g))
                        t = pair[PAIR["pt"]]
                        transposes(t, Px, LC).then_inc(pair_done[PAIR["pt"]], 1)
                    elif name == "ax":
                        pe.wait_ge(pxT_ready, g + 1)
                        pe.wait_ge(vx_ready, g + 1)
                        pe.wait_ge(pair_free[PAIR["ax"]], freed_at("ax", g))
                        t = pair[PAIR["ax"]]
                        for b in range(T):
                            ins = nc_pe.matmul(t[:, 0, b * P:(b + 1) * P], PxT[:, b, :], Vx[:, b, :],
                                               start=True, stop=True)
                        ins.then_inc(pair_done[PAIR["ax"]], 1)
                    elif name == "x2t":
                        pe.wait_ge(x2_ready, g + 1)
                        pe.wait_ge(pair_free[PAIR["x2t"]], freed_at("x2t", g))
                        t = pair[PAIR["x2t"]]
                        transposes(t, x2, P).then_inc(pair_done[PAIR["x2t"]], 1)
                    elif name == "rt":
                        pe.wait_ge(x2T_ready, g + 1)
                        pe.wait_ge(pair_free[PAIR["rt"]], freed_at("rt", g))
                        t = pair[PAIR["rt"]]
                        for b in range(T):
                            ins = nc_pe.matmul(t[:, 0, b * 2 * E:(b + 1) * 2 * E], x2T[:, b * P:(b + 1) * P],
                                               wrg[:, :], start=True, stop=True)
                        ins.then_inc(pair_done[PAIR["rt"]], 1)
                return step

            def scaled_tokens(f, e):
                pe.wait_ge(xs_ready, E * f + e + 1)
                pe.wait_ge(xsH_ready, E * f + e)
                pe.wait_ge(xsL_ready, E * f + e)
                for b in range(T):
                    ins = nc_pe.transpose(xs_ps[:, b * P:(b + 1) * P], xs[:, b, :], ident)
                ins.then_inc(xsT_done, 1)

            def three(dst, w, a, rh, rl, start, stop):
                nc_pe.matmul(dst, wH[(slice(None), *w)][:, a:a + P], rh, start=start, stop=False)
                nc_pe.matmul(dst, wH[(slice(None), *w)][:, a:a + P], rl, start=False, stop=False)
                return nc_pe.matmul(dst, wL[(slice(None), *w)][:, a:a + P], rh, start=False, stop=stop)

            def down(f, n):
                pe.wait_ge(hH_ready, NCH * f + n + 1)
                pe.wait_ge(hL_ready, NCH * f + n + 1)
                if n == 0:
                    pe.wait_ge(x2r_ready, f + 1)
                e, c = n // FC, n % FC
                three(y_ps[:, :], (2, e), c * P, hH[:, n % 2, :], hL[:, n % 2, :],
                      n == 0, n == NCH - 1).then_inc(down_done, 1)

            def run_ffn(f):
                def chunk(n, place):
                    e, c = n // FC, n % FC
                    if place == 0:
                        if n == 0:
                            pe.wait_ge(x2H_ready, f + 1)
                            pe.wait_ge(x2L_ready, f + 1)
                        if n >= 1:
                            pe.wait_ge(silu_ready, NCH * f + n)
                        three(gate_ps[:, :], (0, e), c * P, x2H[:, :], x2L[:, :], True, True).then_inc(gate_done, 1)
                    elif place == 1:
                        if c == 0:
                            pe.wait_ge(xsH_ready, E * f + e + 1)
                            pe.wait_ge(xsL_ready, E * f + e + 1)
                        if n >= 1:
                            pe.wait_ge(h_ready, NCH * f + n)
                        three(up_ps[:, :], (1, e), c * P, xsH[:, e % 2, :], xsL[:, e % 2, :], True, True)\
                            .then_inc(up_done, 1)
                    else:
                        if n >= 2:
                            down(f, n - 2)
                        if c == 2 and e + 1 < E:
                            scaled_tokens(f, e + 1)
                return chunk

            def tail(f, g):
                def run(ffn, att):
                    if ffn:
                        down(f, NCH - 2)
                    if att:
                        scaled_tokens(g, 0)
                    if ffn:
                        down(f, NCH - 1)
                        pe.wait_ge(yT_ready, f + 1)
                        for b in range(T):
                            ins = nc_pe.transpose(y_ps[:, b * P:(b + 1) * P], yo[:, b, :], ident)
                        ins.then_inc(yt_done, 1)
                return run

            walk(None, run_att(0, first=True), tail(0, 0), False, True)
            pe.wait_ge(piece_lo, PIECES)
            with pe.Fori(1, G) as i:
                walk(run_ffn(i - 1), run_att(i), tail(i - 1, i), True, True)
            walk(run_ffn(G - 1), None, tail(G - 1, 0), True, False)

        @block.scalar
        def _(act):
            sc = nc.scalar
            act.wait_ge(params_in, 16 * 18)
            act.wait_ge(dve_setup, 1)

            def run_att(g, first=False):
                def step(name, args):
                    if name == "xt":
                        act.wait_ge(pair_done[PAIR["xt"]], done_at("xt", g))
                        if not first:
                            act.wait_ge(pair_done[PAIR["vn"]], done_at("vn", g - 1))
                        t = pair[PAIR["xt"]]
                        sc.copy(xT[:, :, 0:P], t[:, 0, :].rearrange("p (b t) -> p b t", b=T)).then_inc(xT_ready, 1)
                        if not first:
                            act.wait_ge(pair_done[PAIR["kv"]], done_at("kv", g - 1))
                        ins = sc.copy(ctxT[:, :], t[0:DC, 1, 0:T * LC])
                        ins.then_inc(ctxT_ready, 1)
                        act.wait_ge(ctxT_ready, g + 1)
                        act.sem_inc(pair_free[PAIR["xt"]], 1)
                    elif name == "qk":
                        act.wait_ge(pair_done[PAIR["qk"]], done_at("qk", g))
                        act.wait_ge(qbd_ready, T * g)
                        act.wait_ge(qlast_ready, g)
                        src = pair[PAIR["qk"]][:, 0, :].rearrange("p (b t) -> p b t", b=T)
                        sc.activation(Qr[:, :, 0:NLOC, :].rearrange("p b j k -> p b (j k)"), src,
                                      ACT.Identity, bias=cols[:, 0:1])
                        sc.activation(Qr[:, :, NLOC:NLOC + DIL, :],
                                      src[:, :, 0:DIL * BLK].rearrange("p b (k r) -> p b r k", r=DIL),
                                      ACT.Identity, bias=cols[:, 0:1])
                        for j in (NBLK - 2, NBLK - 1):
                            for half in range(2):
                                own = [t for t in block_tokens(j)[half * CHUNK:(half + 1) * CHUNK] if t < P]
                                ins = sc.activation(Qr[:, :, j, half * CHUNK:half * CHUNK + len(own)],
                                                    src[:, :, own[0]:own[-1] + 1:DIL], ACT.Identity,
                                                    bias=cols[:, 0:1])
                        ins.then_inc(q_ready, 1)
                        act.wait_ge(q_ready, g + 1)
                        act.sem_inc(pair_free[PAIR["qk"]], 1)
                    elif name == "vn":
                        act.wait_ge(pair_done[PAIR["vn"]], done_at("vn", g))
                        if not first:
                            act.wait_ge(pair_done[PAIR["vr3"]], done_at("vr3", g - 1))
                        sc.copy(vH[:, :], pair[PAIR["vn"]][:, 0, :]).then_inc(vH_ready, 1)
                    elif name == "exps":
                        act.wait_ge(s_ready, (T + 1) * g + T + 1)
                        for b in range(T):
                            v = S[:, b].rearrange("p g j k -> p (g j k)")
                            sc.activation(v, v, ACT.Exp, scale=SELF_SCALE).then_inc(p_ready, 1)
                    elif name == "ot":
                        act.wait_ge(pair_done[PAIR["ot"]], done_at("ot", g))
                        if not first:
                            act.wait_ge(pair_done[PAIR["wo"]], done_at("wo", g - 1))
                        sc.copy(oT[:, :, 0:P], pair[PAIR["ot"]][:, 0, :].rearrange("p (b t) -> p b t", b=T))\
                            .then_inc(oTl_ready, 1)
                    elif name == "kv":
                        act.wait_ge(pair_done[PAIR["kv"]], done_at("kv", g))
                        if not first:
                            act.wait_ge(pair_done[PAIR["sx"]], done_at("sx", g - 1))
                        sc.activation(KxT[:, :, :], pair[PAIR["kv"]][:, 0, 0:T * LC].rearrange("p (b k) -> p b k", b=T),
                                      ACT.Identity, bias=cols[:, 4:5]).then_inc(kx_ready, 1)
                        act.wait_ge(pt_ready, T * g + T)
                        sc.copy(Vx, pair[PAIR["kv"]][0:LC, 1, :].rearrange("p (b d) -> p b d", b=T))\
                            .then_inc(vx_ready, 1)
                        act.wait_ge(kx_ready, g + 1)
                        act.wait_ge(vx_ready, g + 1)
                        act.sem_inc(pair_free[PAIR["kv"]], 1)
                    elif name == "x1t":
                        act.wait_ge(pair_done[PAIR["x1t"]], done_at("x1t", g))
                        act.wait_ge(pt_ready, T * g + T)
                        sc.copy(x1T, pair[PAIR["x1t"]][:, 0, :]).then_inc(x1T_ready, 1)
                        act.wait_ge(x1T_ready, g + 1)
                        act.sem_inc(pair_free[PAIR["x1t"]], 1)
                    elif name == "qx":
                        act.wait_ge(pair_done[PAIR["qx"]], done_at("qx", g))
                        sc.activation(QxT, pair[PAIR["qx"]][:, 0, :].rearrange("p (b t) -> p b t", b=T),
                                      ACT.Identity, bias=cols[:, 3:4]).then_inc(qx_ready, 1)
                        act.wait_ge(qx_ready, g + 1)
                        act.sem_inc(pair_free[PAIR["qx"]], 1)
                    elif name == "ex":
                        act.wait_ge(sx_ready, g + 1)
                        sc.activation(Px, Px, ACT.Exp, scale=CROSS_SCALE).then_inc(ex_ready, 1)
                    elif name == "pt":
                        act.wait_ge(pair_done[PAIR["pt"]], done_at("pt", g))
                        sc.copy(PxT, pair[PAIR["pt"]][0:LC, 0, :].rearrange("p (b t) -> p b t", b=T))\
                            .then_inc(pxT_ready, 1)
                        act.wait_ge(pxT_ready, g + 1)
                        act.sem_inc(pair_free[PAIR["pt"]], 1)
                    elif name == "x2t":
                        act.wait_ge(pair_done[PAIR["x2t"]], done_at("x2t", g))
                        sc.copy(x2T, pair[PAIR["x2t"]][:, 0, :]).then_inc(x2T_ready, 1)
                        act.wait_ge(x2T_ready, g + 1)
                        act.sem_inc(pair_free[PAIR["x2t"]], 1)
                    elif name == "cw":
                        act.wait_ge(lg_ready, g + 1)
                        v = lg[:, :, :].rearrange("p (b s) e -> p b s e", s=2)
                        sc.activation(v[:, :, 0, :], v[:, :, 0, :], ACT.Exp)
                        sc.activation(v[:, :, 1, :], v[:, :, 1, :], ACT.Exp, scale=10.0).then_inc(elg_ready, 1)
                    elif name == "piece":
                        n, = args
                        act.wait_ge(piece_in[n % 4], 16 * (n // 4 + 1))
                        sc.copy(wH[:, n // E, n % E, :], sh[:, n % 4, :]).then_inc(piece_hi, 1)
                return step

            def high(f, n):
                act.wait_ge(h_ready, NCH * f + n + 1)
                if n >= 2:
                    act.wait_ge(down_done, NCH * f + n - 1)
                sc.copy(hH[:, n % 2, :], sh[:, n % 4, :]).then_inc(hH_ready, 1)

            def scaled_high(f, e, first=False):
                act.wait_ge(xsT_done, E * f + e + 1)
                if not first:
                    act.wait_ge(up_done, NCH * f + FC * (e - 1))
                sc.copy(xsH[:, e % 2, :], xs_ps[:, :]).then_inc(xsH_ready, 1)

            def run_ffn(f):
                def chunk(n, place):
                    if place:
                        return
                    act.wait_ge(gate_done, NCH * f + n + 1)
                    if n >= 4:
                        act.wait_ge(hL_ready, NCH * f + n - 3)
                    sc.activation(sh[:, n % 4, :], gate_ps[:, :], ACT.Silu).then_inc(silu_ready, 1)
                    if n >= 1:
                        high(f, n - 1)
                    if n % FC == 3 and n // FC + 1 < E:
                        scaled_high(f, n // FC + 1)
                return chunk

            def tail(f, g):
                def run(ffn, att):
                    if ffn:
                        high(f, NCH - 1)
                    if att:
                        act.wait_ge(gate_done, NCH * g)
                        act.wait_ge(x2T_ready, g + 1)
                        sc.copy(x2H[:, :], x2T).then_inc(x2H_ready, 1)
                        scaled_high(g, 0, first=not ffn)
                    if ffn:
                        act.wait_ge(down_done, NCH * f + NCH)
                        act.wait_ge(out_stored, 16 * (f + 1))
                        sc.copy(yo[:, :, :].rearrange("p b d -> p (b d)"), y_ps[:, :]).then_inc(yT_ready, 1)
                    if att:
                        act.wait_ge(r3_ready, g)
                        act.wait_ge(x2_ready, g + 1)
                        sc.copy(x2r[:, :, :], x2[:, :, :]).then_inc(x2r_ready, 1)
                return run

            act.wait_ge(pe_bias, 1)
            sc.copy(bias_o[:, :], xs_ps[:, 0:P])
            sc.copy(bias_x[:, :], xs_ps[:, P:2 * P]).then_inc(bias_ready, 1)
            walk(None, run_att(0, first=True), tail(0, 0), False, True)
            with act.Fori(1, G) as i:
                walk(run_ffn(i - 1), run_att(i), tail(i - 1, i), True, True)
            walk(run_ffn(G - 1), None, tail(G - 1, 0), True, False)

        @block.vector
        def _(dve):
            ve = nc.vector
            links = [0]

            def link(ins, s, base):
                links[0] += 1
                ins.then_inc(s, 1)
                dve.wait_ge(s, base + links[0])

            dve.wait_ge(params_in, 16 * 18)
            ve.memset(xT[:, :, P:PADT], 0.0)
            ve.memset(Qr[:, :, :, :], 0.0)
            ve.memset(ones[:, :], 1.0)
            ve.memset(minus_half[:, :], -0.5)
            ve.tensor_copy(mrow[:, :], cst_in[:, C_MROW - C_KEEP:C_MROW - C_KEEP + P])
            ve.tensor_copy(mcol[:, :], cst_in[:, C_MCOL - C_KEEP:C_MCOL - C_KEEP + BANK])
            ve.tensor_copy(sel[:, :, :], cst_in[:, C_SEL - C_KEEP:].rearrange("p (j m) -> p j m", j=NBLK))
            ve.tensor_scalar(bv2[:, :], cols[:, 2:3], 2.0, None, ALU.mult)
            ve.tensor_scalar(bkq[:, :], headv[:, 0:NQ], cols[:, 1:2], None, ALU.mult)
            for s in range(2):
                ve.tensor_copy(Vbd[:, s, :, VW - 1], headv)
            ve.tensor_copy(V5[:, :, :, HD], headv.unsqueeze(1).broadcast_to([P, T, HEADS])).then_inc(dve_setup, 1)

            def stats(r, st, m, ve_out, do_link, base, s):
                for b in range(T):
                    ins = ve.bn_stats(st[:, b, :], r[:, b, :])
                do_link(ins, s, base)
                ve.memset(pause[:, :], 0.0)
                for b in range(T):
                    ins = ve.bn_aggr(m[:, b, :], st[:, b, :])
                do_link(ins, s, base)
                return ve.tensor_scalar(ve_out[:, :], m[:, :, 1], EPS, None, ALU.add)

            def normalise(dst, r, m, rs):
                for b in range(T):
                    ins = ve.tensor_scalar(dst[:, b, :], r[:, b, :], m[:, b, 0:1], rs[:, b:b + 1],
                                           ALU.subtract, ALU.mult)
                return ins

            def run_att(g, first=False):
                base = g * DVE_ATT_LINKS

                def lk(ins):
                    link(ins, att_link, base)

                def step(name, args):
                    if name == "qk":
                        dve.wait_ge(pair_done[PAIR["qk"]], done_at("qk", g))
                        if not first:
                            dve.wait_ge(pair_done[PAIR["wo"]], done_at("wo", g - 1))
                        for q in range(NQ):
                            ve.tensor_scalar(Kq[:, q, :, 0:P],
                                             pair[PAIR["qk"]][:, 1, :].rearrange("p (b t) -> p b t", b=T),
                                             headv[:, q:q + 1], bkq[:, q:q + 1], ALU.mult, ALU.add)
                        lk(ve.tensor_copy(Kq[:, :, :, P:PADT],
                                          bkq[:, :].unsqueeze(2).unsqueeze(3).broadcast_to([P, NQ, T, PADT - P])))
                        dve.sem_inc(k_ready, 1)
                        dve.sem_inc(pair_free[PAIR["qk"]], 1)
                    elif name == "vn":
                        dve.wait_ge(vH_ready, g + 1)
                        ve.tensor_tensor(vL[:, :], pair[PAIR["vn"]][:, 0, :], vH[:, :].bitcast(F32), ALU.subtract)\
                            .then_inc(vL_ready, 1)
                        dve.wait_ge(vL_ready, g + 1)
                        dve.sem_inc(pair_free[PAIR["vn"]], 1)
                    elif name == "sc" and args[1] == 1:
                        b, _ = args
                        nm = f"sc{b}"
                        dve.wait_ge(pair_done[PAIR[nm]], done_at(nm, g))
                        v = pair[PAIR[nm]][:, :, :].rearrange("p a (j q k) -> p (a j) q k", q=NQ, k=BLK)
                        m = smax[:, :].rearrange("p (j q) -> p j q", q=NQ)
                        lk(ve.tensor_reduce(m, v, AX, ALU.max))
                        if b == 0:
                            dve.wait_ge(x2L_ready, g)
                        ve.tensor_tensor(S[:, b].rearrange("p q j k -> p j q k")[:, 0:SBLK], v,
                                         m.unsqueeze(3).broadcast_to([P, SBLK, NQ, BLK]), ALU.subtract)\
                            .then_inc(s_ready, 1)
                        dve.wait_ge(s_ready, (T + 1) * g + b + 1)
                        dve.sem_inc(pair_free[PAIR[nm]], 1)
                    elif name == "sc_last":
                        dve.wait_ge(pair_done[PAIR["sc_last"]], done_at("sc_last", g))
                        v = pair[PAIR["sc_last"]][:, 0, :].rearrange("p (b q k) -> p b q k", b=T, q=NQ)
                        m = smax[:, 0:T * NQ].rearrange("p (b q) -> p b q", b=T)
                        lk(ve.tensor_reduce(m, v, AX, ALU.max))
                        ve.tensor_tensor(S[:, :, :, NBLK - 1, :], v, m.unsqueeze(3).broadcast_to([P, T, NQ, BLK]),
                                         ALU.subtract).then_inc(s_ready, 1)
                        dve.wait_ge(s_ready, (T + 1) * g + T + 1)
                        dve.sem_inc(pair_free[PAIR["sc_last"]], 1)
                    elif name == "vr":
                        b, = args
                        nm = f"vr{b}"
                        dve.wait_ge(pair_done[PAIR[nm]], done_at(nm, g))
                        if b:
                            dve.wait_ge(pair_done[PAIR[f"av{b - 1}A"]], done_at(f"av{b - 1}A", g))
                        else:
                            if not first:
                                dve.wait_ge(pair_done[PAIR["av3A"]], done_at("av3A", g - 1))
                        hv = headv.unsqueeze(1).unsqueeze(3).broadcast_to([P, NLOC, HEADS, HD])
                        for s in range(2):
                            src = pair[PAIR[nm]][:, s, :].rearrange("p (k h d) -> p k h d", k=NLOC, h=HEADS)
                            dst = Vbd[:, s, :, 0:VW - 1].rearrange("p h (k d) -> p k h d", k=NLOC)
                            ins = ve.tensor_tensor(dst, src, hv, ALU.mult)
                        ins.then_inc(v_ready, 1)
                        dve.wait_ge(v_ready, T * g + b + 1)
                        dve.sem_inc(pair_free[PAIR[nm]], 1)
                    elif name == "v5":
                        dve.wait_ge(pair_done[PAIR["v5"]], done_at("v5", g))
                        if not first:
                            dve.wait_ge(pair_done[PAIR["av35"]], done_at("av35", g - 1))
                        src = pair[PAIR["v5"]][:, 0, :].rearrange("p (b h d) -> p b h d", b=T, h=HEADS)
                        ve.tensor_tensor(V5[:, :, :, 0:HD], src,
                                         headv.unsqueeze(1).unsqueeze(3).broadcast_to([P, T, HEADS, HD]),
                                         ALU.mult).then_inc(v5_ready, 1)
                        dve.wait_ge(v5_ready, g + 1)
                        dve.sem_inc(pair_free[PAIR["v5"]], 1)
                    elif name == "tr":
                        b, = args
                        dve.wait_ge(p_ready, T * g + b + 1)
                        if b:
                            dve.wait_ge(pair_done[PAIR[f"av{b - 1}5"]], done_at(f"av{b - 1}5", g))
                        else:
                            if not first:
                                dve.wait_ge(pair_done[PAIR["av35"]], done_at("av35", g - 1))
                        ve.transpose(Pt[:, :, :, :].rearrange("p g j k -> p (g j k)"),
                                     S[:, b].rearrange("p g j k -> p (g j k)")).then_inc(pt_ready, 1)
                    elif name == "av":
                        b, which = args
                        nm = f"av{b}{which}"
                        dve.wait_ge(pair_done[PAIR[nm]], done_at(nm, g))
                        v = pair[PAIR[nm]][:, :, 0:2 * QUAD * VW].rearrange("p a (h c) -> p a h c", c=VW)
                        rs = rsum[:, :].rearrange("p (a h) -> p a h", a=2)
                        lk(ve.reciprocal(rs, v[:, :, :, VW - 1]))
                        o = (oL if which == "L" else oA)[:, b, :].rearrange("p (a h d) -> p a h d", a=2, d=HD)
                        for k in range(NLOC):
                            q = slice(BLK * k, BLK * (k + 1))
                            ins = ve.tensor_tensor(o[q], v[q, :, :, HD * k:HD * (k + 1)],
                                                   rs[q].unsqueeze(3).broadcast_to([BLK, 2, HEADS // 2, HD]), ALU.mult)
                            if k < NLOC - 1:
                                ins.then_inc(att_link, 1)
                                links[0] += 1
                        lk(ins)
                        dve.sem_inc(pair_free[PAIR[nm]], 1)
                    elif name == "av5":
                        b, = args
                        nm = f"av{b}5"
                        dve.wait_ge(pair_done[PAIR[nm]], done_at(nm, g))
                        v = pair[PAIR[nm]][0:BLK, 0, 0:HEADS * (HD + 1)].rearrange("p (h c) -> p h c", c=HD + 1)
                        lk(ve.reciprocal(rsum[0:BLK, :], v[:, :, HD]))
                        lk(ve.tensor_tensor(o5[0:BLK, b, :].rearrange("p (h d) -> p h d", d=HD), v[:, :, 0:HD],
                                            rsum[0:BLK, :].unsqueeze(2).broadcast_to([BLK, HEADS, HD]), ALU.mult))
                        dve.sem_inc(pair_free[PAIR[nm]], 1)
                        if b == T - 1:
                            dve.sem_inc(o_ready, 1)
                    elif name == "ot":
                        dve.wait_ge(oTl_ready, g + 1)
                        src = pair[PAIR["ot"]][:, 1, :].rearrange("p (b t) -> p b t", b=T)
                        dst = oT[:, :, :].rearrange("p b (i r) -> p b r i", r=DIL)
                        for r in range(DIL):
                            d = dst[:, :, r, 0:BLK]
                            ins = ve.tensor_tensor(d, d, src[:, :, r * BLK:(r + 1) * BLK], ALU.add)
                            ins.then_inc(att_link, 1)
                            links[0] += 1
                        n_last = -(-(P - DIL * BLK - 1) // DIL)
                        for r in range(2):
                            d = dst[:, :, r, BLK:BLK + n_last]
                            ins = ve.tensor_tensor(d, d, src[:, :, DIL * BLK + r * CHUNK:DIL * BLK + r * CHUNK + n_last],
                                                   ALU.add)
                            if r == 0:
                                ins.then_inc(att_link, 1)
                                links[0] += 1
                        lk(ins)
                        dve.sem_inc(pair_free[PAIR["ot"]], 1)
                    elif name == "ot5":
                        dve.wait_ge(pair_done[PAIR["ot5"]], done_at("ot5", g))
                        src = pair[PAIR["ot5"]][:, 0, :].rearrange("p (b t) -> p b t", b=T)
                        n_last = (P - DIL * BLK - 2 + DIL - 1) // DIL
                        d = oT[:, :, :].rearrange("p b (i r) -> p b r i", r=DIL)[:, :, 2, BLK:BLK + n_last]
                        lk(ve.tensor_tensor(d, d, src[:, :, CHUNK:CHUNK + n_last], ALU.add))
                        dve.sem_inc(oT_ready, 1)
                        dve.sem_inc(pair_free[PAIR["ot5"]], 1)
                    elif name == "wo":
                        dve.wait_ge(pair_done[PAIR["wo"]], done_at("wo", g))
                        dve.wait_ge(xb_ready, 2 * g + 1)
                        lk(ve.tensor_tensor(r1, pair[PAIR["wo"]][:, 0, :].rearrange("p (b d) -> p b d", b=T),
                                            xb[:, :, :], ALU.add))
                        dve.sem_inc(pair_free[PAIR["wo"]], 1)
                        stats(r1, bst, mv, vareps, link, base, att_link).then_inc(var_ready, 1)
                    elif name == "ln1":
                        dve.wait_ge(rstd_ready, 2 * g + 1)
                        normalise(x1, r1, mv, rstd).then_inc(x1_ready, 1)
                    elif name == "sx":
                        dve.wait_ge(pair_done[PAIR["sx"]], done_at("sx", g))
                        v = pair[PAIR["sx"]][:, 0, 0:T * LC].rearrange("p (b k) -> p b k", b=T)
                        lk(ve.tensor_reduce(xmax[:, :], v, AX, ALU.max))
                        lk(ve.tensor_tensor(Px, v, xmax[:, :].unsqueeze(2).broadcast_to([P, T, LC]), ALU.subtract))
                        dve.sem_inc(sx_ready, 1)
                        dve.sem_inc(pair_free[PAIR["sx"]], 1)
                    elif name == "ex":
                        dve.wait_ge(ex_ready, g + 1)
                        lk(ve.tensor_reduce(xsum[:, :], Px, AX, ALU.add))
                        lk(ve.reciprocal(xrec[:, :], xsum[:, :]))
                    elif name == "ax":
                        dve.wait_ge(pair_done[PAIR["ax"]], done_at("ax", g))
                        dve.wait_ge(x1b_ready, g + 1)
                        for b in range(T):
                            ins = ve.scalar_tensor_tensor(r2[:, b, :], pair[PAIR["ax"]][:, 0, b * P:(b + 1) * P],
                                                          xrec[:, b:b + 1], xb[:, b, :], ALU.mult, ALU.add)
                        lk(ins)
                        dve.sem_inc(pair_free[PAIR["ax"]], 1)
                        stats(r2, bst, mv, vareps, link, base, att_link).then_inc(var_ready, 1)
                    elif name == "ln2":
                        dve.wait_ge(rstd_ready, 2 * g + 2)
                        if not first:
                            dve.wait_ge(pair_done[PAIR["x2t"]], done_at("x2t", g - 1))
                        dve.wait_ge(xs_ready, E * g)
                        dve.wait_ge(x2r_ready, g)
                        normalise(x2, r2, mv, rstd).then_inc(x2_ready, 1)
                    elif name == "rt":
                        dve.wait_ge(pair_done[PAIR["rt"]], done_at("rt", g))
                        v = pair[PAIR["rt"]][:, 0, 0:T * 2 * E].rearrange("p (s e) -> p s e", e=E)
                        lk(ve.tensor_reduce(lmax[:, :], v, AX, ALU.max))
                        lk(ve.tensor_tensor(lg[:, :, :], v, lmax[:, :].unsqueeze(2).broadcast_to([P, 2 * T, E]),
                                            ALU.subtract))
                        dve.sem_inc(lg_ready, 1)
                        dve.sem_inc(pair_free[PAIR["rt"]], 1)
                    elif name == "cw":
                        dve.wait_ge(elg_ready, g + 1)
                        lk(ve.tensor_reduce(lsum[:, :], lg[:, :, :], AX, ALU.add))
                        lk(ve.reciprocal(lrec[:, :], lsum[:, :]))
                        lk(ve.tensor_tensor(lg[:, :, :], lg[:, :, :],
                                            lrec[:, :].unsqueeze(2).broadcast_to([P, 2 * T, E]), ALU.mult))
                        v = lg[:, :, :].rearrange("p (b s) e -> p b s e", s=2)
                        lk(ve.tensor_tensor(v[:, :, 0, :], v[:, :, 0, :], v[:, :, 1, :], ALU.mult))
                        lk(ve.tensor_reduce(csum[:, :], v[:, :, 0, :], AX, ALU.add))
                        lk(ve.tensor_scalar(csum[:, :], csum[:, :], 1e-9, None, ALU.add))
                        lk(ve.reciprocal(crec[:, :], csum[:, :]))
                        ve.tensor_tensor(cw[:, :, :], v[:, :, 0, :],
                                         crec[:, :].unsqueeze(2).broadcast_to([P, T, E]), ALU.mult).then_inc(cw_ready, 1)
                return step

            def scaled_low(f, e):
                dve.wait_ge(xsH_ready, E * f + e + 1)
                ve.tensor_tensor(xsL[:, e % 2, :], xs_ps[:, :], xsH[:, e % 2, :].bitcast(F32), ALU.subtract)\
                    .then_inc(xsL_ready, 1)

            def run_ffn(f):
                def chunk(n, place):
                    if place:
                        return
                    dve.wait_ge(silu_ready, NCH * f + n + 1)
                    dve.wait_ge(up_done, NCH * f + n + 1)
                    ve.tensor_tensor(sh[:, n % 4, :], sh[:, n % 4, :], up_ps[:, :], ALU.mult).then_inc(h_ready, 1)
                    if n % FC == 3 and n // FC + 1 < E:
                        scaled_low(f, n // FC + 1)
                return chunk

            def tail(f, g):
                def run(ffn, att):
                    if att:
                        scaled_low(g, 0)
                    if ffn:
                        dve.wait_ge(yt_done, f + 1)
                        dve.wait_ge(x2r_ready, f + 1)
                        n0 = links[0]
                        links[0] = 0
                        fb = f * DVE_FFN_LINKS
                        link(ve.tensor_tensor(yo[:, :, :], y_ps[:, :].rearrange("p (b d) -> p b d", b=T),
                                              x2r[:, :, :], ALU.add), ffn_link, fb)
                        dve.sem_inc(r3_ready, 1)
                        stats(yo, bst3, mv3, vareps3, link, fb, ffn_link).then_inc(var3_ready, 1)
                        dve.wait_ge(rstd3_ready, f + 1)
                        normalise(yo, yo, mv3, rstd3).then_inc(out_ready, 1)
                        assert links[0] == DVE_FFN_LINKS, links
                        links[0] = n0
                    assert not att or links[0] == DVE_ATT_LINKS, links
                    links[0] = 0
                return run

            links[0] = 0
            walk(None, run_att(0, first=True), tail(0, 0), False, True)
            with dve.Fori(1, G) as i:
                walk(run_ffn(i - 1), run_att(i), tail(i - 1, i), True, True)
            walk(run_ffn(G - 1), None, tail(G - 1, 0), True, False)

        @block.gpsimd
        def _(pool):
            po = nc.gpsimd
            pool.wait_ge(bias_ready, 1)

            def run_att(g, first=False):
                def step(name, args):
                    if name == "xt":
                        pool.wait_ge(x_loaded, 16 * g + 16)
                        pool.wait_ge(x2_ready, g)
                        po.tensor_tensor(xb[:, :, :], x_in[:, :, :],
                                         bias_o[:, :].unsqueeze(1).broadcast_to([P, T, P]), ALU.add)\
                            .then_inc(xb_ready, 1)
                    elif name == "qe":
                        b, = args
                        pool.wait_ge(q_ready, g + 1)
                        if b >= 2:
                            pool.wait_ge(pair_done[PAIR[f"sc{b - 2}"]], done_at(f"sc{b - 2}", g))
                        else:
                            if not first:
                                pool.wait_ge(pair_done[PAIR["ot5"]], done_at("ot5", g - 1))
                        po.tensor_tensor(Qbd[:, b % 2], Qr[:, b, 0:SBLK].unsqueeze(2).broadcast_to([P, SBLK, QUAD, BLK]),
                                         headq.unsqueeze(1).unsqueeze(3).broadcast_to([P, SBLK, QUAD, BLK]),
                                         ALU.mult).then_inc(qbd_ready, 1)
                    elif name == "qe_last":
                        po.tensor_tensor(Qbd_last, Qr[:, :, NBLK - 1].unsqueeze(2).broadcast_to([P, T, QUAD, BLK]),
                                         headq.unsqueeze(1).unsqueeze(3).broadcast_to([P, T, QUAD, BLK]),
                                         ALU.mult).then_inc(qlast_ready, 1)
                    elif name == "wo":
                        pool.wait_ge(var_ready, 2 * g + 1)
                        po.tensor_tensor(rstd[:, :], vareps[:, :], minus_half[:, :], ALU.pow).then_inc(rstd_ready, 1)
                    elif name == "x1t":
                        pool.wait_ge(x1_ready, g + 1)
                        po.tensor_tensor(xb[:, :, :], x1, bias_x[:, :].unsqueeze(1).broadcast_to([P, T, P]), ALU.add)\
                            .then_inc(x1b_ready, 1)
                        pool.wait_ge(x1b_ready, g + 1)
                        pool.sem_inc(xb_ready, 1)
                    elif name == "ax":
                        pool.wait_ge(var_ready, 2 * g + 2)
                        po.tensor_tensor(rstd[:, :], vareps[:, :], minus_half[:, :], ALU.pow).then_inc(rstd_ready, 1)
                    elif name == "piece":
                        n, = args
                        pool.wait_ge(piece_hi, n + 1)
                        po.tensor_tensor(wL[:, n // E, n % E, :], sh[:, n % 4, :],
                                         wH[:, n // E, n % E, :].bitcast(F32), ALU.subtract).then_inc(piece_lo, 1)
                return step

            def scaled(f, e):
                pool.wait_ge(xsT_done, E * f + e)
                po.tensor_tensor(xs[:, :, :], x2[:, :, :], cw[:, :, e:e + 1].broadcast_to([P, T, P]), ALU.mult)\
                    .then_inc(xs_ready, 1)

            def low(f, n):
                pool.wait_ge(hH_ready, NCH * f + n + 1)
                po.tensor_tensor(hL[:, n % 2, :], sh[:, n % 4, :], hH[:, n % 2, :].bitcast(F32), ALU.subtract)\
                    .then_inc(hL_ready, 1)

            def run_ffn(f):
                def chunk(n, place):
                    if place:
                        return
                    if n % FC == 0 and n // FC + 1 < E:
                        scaled(f, n // FC + 1)
                    if n >= 1:
                        low(f, n - 1)
                return chunk

            def tail(f, g):
                def run(ffn, att):
                    if ffn:
                        low(f, NCH - 1)
                    if att:
                        pool.wait_ge(cw_ready, g + 1)
                        scaled(g, 0)
                        pool.wait_ge(x2H_ready, g + 1)
                        po.tensor_tensor(x2L[:, :], x2T, x2H[:, :].bitcast(F32), ALU.subtract).then_inc(x2L_ready, 1)
                    if ffn:
                        pool.wait_ge(var3_ready, f + 1)
                        po.tensor_tensor(rstd3[:, :], vareps3[:, :], minus_half[:, :], ALU.pow).then_inc(rstd3_ready, 1)
                return run

            walk(None, run_att(0, first=True), tail(0, 0), False, True)
            with pool.Fori(1, G) as i:
                walk(run_ffn(i - 1), run_att(i), tail(i - 1, i), True, True)
            walk(run_ffn(G - 1), None, tail(G - 1, 0), True, False)


def kernel(**inputs):
    import concourse.bacc as bacc
    from concourse.bass_utils import run_bass_kernel_spmd

    names = {"x": "x", "ctx": "ctx_768", "bq": "L0_attn_bq", "bk": "L0_attn_bk", "bv": "L0_attn_bv",
             "bo": "L0_attn_bo", "Wxq": "L0_xattn_Wq", "Wxk": "L0_xattn_Wk", "Wxv": "L0_xattn_Wv",
             "bxq": "L0_xattn_bq", "bxk": "L0_xattn_bk", "bxv": "L0_xattn_bv",
             "w_router": "L0_ffn_w_router", "w_gating": "L0_ffn_w_gating", "w_gate": "L0_ffn_w_gate",
             "w_up": "L0_ffn_w_up", "w_down": "L0_ffn_w_down"}
    arrays = {k: np.ascontiguousarray(inputs[v]) for k, v in names.items()}
    for k in ("q", "k", "v", "o"):
        arrays[f"W{k}T"] = np.ascontiguousarray(np.asarray(inputs[f"L0_attn_W{k}"]).T)
    arrays["cst"] = constants()

    nc = bacc.Bacc("TRN2", target_bir_lowering=False, num_devices=1)
    aps = {k: nc.dram_tensor(f"in_{k}", a.shape, mybir.dt.from_np(a.dtype), kind="ExternalInput").ap()
           for k, a in arrays.items()}
    out = nc.dram_tensor("out", arrays["x"].shape, F32, kind="ExternalOutput").ap()
    build_decoder(nc, out=out, **aps)
    r = run_bass_kernel_spmd(nc, [{f"in_{k}": a for k, a in arrays.items()}], core_ids=[0])
    return r.results[0]["out"]
```

```python
from contextlib import ExitStack

import numpy as np
import concourse.bass as bass
from concourse import mybir

ALU = mybir.AluOpType
ACT = mybir.ActivationFunctionType
F32 = mybir.dt.float32
F32R = mybir.dt.float32r
BF16 = mybir.dt.bfloat16
AX = mybir.AxisListType.X

P = 128
HEADS, HD = 16, 8
CHUNK, DIL = 16, 3
QUAD = 4
NQ = HEADS // QUAD
BLK = 2 * CHUNK
PADT = 144
NLOC, NATR = 4, 5
NBLK = NLOC + NATR
T = 4
EPS = 1e-5
MASKED = -1e30
BANK = 512
SBLK = 8
VW = NLOC * HD + 1

C_ID = 0
C_HEADV = C_ID + P
C_HEADQ = C_HEADV + HEADS
C_KEEP = C_HEADQ + QUAD
C_MROW = C_KEEP
C_MCOL = C_MROW + P
C_SEL = C_MCOL + BANK
C_ALL = C_SEL + NBLK * P


def block_tokens(j):
    if j < NLOC:
        return [BLK * j + k for k in range(BLK)]
    if j < NLOC + DIL:
        return [(j - NLOC) + DIL * k for k in range(BLK)]
    r0 = j - NLOC - DIL
    return [DIL * (BLK + k % CHUNK) + r0 + k // CHUNK for k in range(BLK)]


def constants():
    c = np.zeros((P, C_ALL), np.float32)
    p = np.arange(P)
    c[:, C_ID:C_ID + P] = np.eye(P)
    c[:, C_HEADV:C_HEADV + HEADS] = (np.arange(HEADS)[None] % QUAD) == (p[:, None] // 32)
    c[:, C_HEADQ:C_HEADQ + QUAD] = np.arange(QUAD)[None] == (p[:, None] % 32) // HD
    half = (np.arange(P) % BLK) // CHUNK
    khalf = (np.arange(BANK) % BLK) // CHUNK
    for s in range(2):
        c[s, C_MROW:C_MROW + P] = half == s
        c[s, C_MCOL:C_MCOL + BANK] = np.where(khalf == s, 0.0, MASKED)
    for j in range(NBLK):
        for k, t in enumerate(block_tokens(j)):
            if t < P:
                for h in range(QUAD):
                    c[t, C_SEL + j * P + h * BLK + k] = 1.0
    return c


JOBS = ["xt", "qk", "vn", "sc_last"] + [f"sc{b}" for b in range(T)]
JOBS += ["vr0L", "vr0A", "v5", "av0L", "av0A", "av05", "av1L", "av1A"]
JOBS += ["vr2L", "vr2A", "av15", "av2L", "av2A", "av25", "av3L", "av3A", "av35"]
JOBS += ["kv", "ot", "ot5", "wo", "x1t", "qx", "sx", "pt", "ax", "x2t", "rt"]
assert len(JOBS) % 2 == 0
PAIR = {name: n % 2 for n, name in enumerate(JOBS)}
DONE_AT = {name: n // 2 + 1 for n, name in enumerate(JOBS)}
DONE_PER = len(JOBS) // 2
AV_PER = 3 * T

STEPS = [[[], [], []] for _ in range(32)]
for _at, _steps in {
        (0, 0): [("xt",)], (0, 2): [("qk",), ("qe_last",), ("qe", 0)], (1, 1): [("k2",)], (1, 2): [("vn",), ("qe", 1)],
        (2, 1): [("sc_last",)], (2, 2): [("sc", 0, 0)], (3, 0): [("sc", 0, 1)],
        (3, 1): [("sc", 1, 0)], (3, 2): [("sc", 1, 1), ("qe", 2)],
        (4, 1): [("sc", 2, 0)], (4, 2): [("sc", 2, 1), ("qe", 3)], (5, 0): [("exps", 0)],
        (5, 1): [("sc", 3, 0)], (5, 2): [("sc", 3, 1)],
        (6, 1): [("vr", 0, "L")], (6, 2): [("vr", 0, "A"), ("exps", 2), ("tr", 0)], (7, 0): [("v5",), ("tr", 1)],
        (7, 2): [("av", 0, "L")], (8, 0): [("av", 0, "A")], (8, 1): [("av5", 0)],
        (8, 2): [("av", 1, "L")], (9, 0): [("tr", 2)], (9, 1): [("av", 1, "A")],
        (9, 2): [("vr", 2, "L")], (10, 0): [("vr", 2, "A")], (10, 2): [("av5", 1)],
        (11, 1): [("av", 2, "L"), ("tr", 3)], (11, 2): [("av", 2, "A")], (12, 0): [("av5", 2)],
        (12, 2): [("av", 3, "L")], (13, 0): [("av", 3, "A")], (13, 2): [("av5", 3)],
        (14, 0): [("kv",)], (14, 2): [("ot",)], (15, 0): [("ot5",)], (16, 0): [("wo",)],
        (16, 2): [("pow1",)], (18, 0): [("ln1",)], (19, 0): [("x1t",)], (19, 2): [("qx",)], (20, 1): [("sx",)],
        (20, 2): [("ex",)], (21, 2): [("pt",)], (22, 1): [("ax",)], (23, 2): [("pow2",)], (24, 0): [("ln2",)],
        (25, 1): [("x2t",)], (26, 0): [("rt",)], (26, 1): [("cw",)], (27, 1): [("cw2",)]}.items():
    STEPS[_at[0]][_at[1]] += _steps
GATE_BANK, UP_BANK, XS_BANK = (0, 2, 2, 1), (1, 0, 0, 2), 1
DVE_ATT_LINKS = 34
DVE_FFN_LINKS = 3


def build_decoder(nc, x, ctx, cst, WqT, WkT, WvT, WoT, bq, bk, bv, bo, Wxq, Wxk, Wxv, bxq, bxk, bxv,
                  w_router, w_gating, w_gate, w_up, w_down, out):
    B, L, D = x.shape
    _, LC, DC = ctx.shape
    E, _, F = w_gate.shape
    G = B // T
    FC = F // P
    NCH = E * FC
    TOK = T * P
    SELF_SCALE = float(HD) ** -0.5
    CROSS_SCALE = float(D) ** -0.5
    PIECES = 3 * E
    assert L == P and D == P and F == 4 * P and NCH == 32 and G * T == B

    with ExitStack() as stack:
        def sb(name, shape, dt=F32):
            return stack.enter_context(nc.sbuf_tensor(name, shape, dt))

        def ps(name, shape):
            return stack.enter_context(nc.psum_tensor(name, shape, F32))

        def sem(name):
            return stack.enter_context(nc.semaphore(name))

        pair = [ps("pair0", [P, 2, 512]), ps("pair1", [P, 2, 512])]
        ring = [ps(f"ring{n}", [P, BANK]) for n in range(3)]
        y_ps = ps("y_ps", [P, BANK])
        xs_ps = ring[XS_BANK]

        cs = sb("cs", [P, C_KEEP])
        ident = cs[:, C_ID:C_ID + P]
        headv = cs[:, C_HEADV:C_HEADV + HEADS]
        headq = cs[:, C_HEADQ:C_HEADQ + QUAD]
        wqT, wkT, wvT, woT, wxq = (sb(n, [P, P]) for n in ("wqT", "wkT", "wvT", "woT", "wxq"))
        wxk, wxv = sb("wxk", [DC, P]), sb("wxv", [DC, P])
        wrg = sb("wrg", [P, 2 * E])
        cols = sb("cols", [P, 5])
        rows = sb("rows", [1, 2 * P])
        mrow = sb("mrow", [P, P], BF16)
        mcol = sb("mcol", [P, BANK], BF16)
        sel = sb("sel", [P, NBLK, P], F32R)
        ones = sb("ones", [1, P])
        bv2 = sb("bv2", [P, 1])
        bkq = sb("bkq", [P, NQ])
        bias_o = sb("bias_o", [P, P])
        bias_x = sb("bias_x", [P, P])
        minus_half = sb("minus_half", [P, T])
        wH = sb("wH", [P, 3, E, 512], F32R)
        wL = sb("wL", [P, 3, E, 512], F32R)
        sh = sb("sh", [P, 4, 512])
        hH, hL = sb("hH", [P, 2, 512], F32R), sb("hL", [P, 2, 512], F32R)
        xs = sb("xs", [P, T, P])
        xsH, xsL = sb("xsH", [P, 2, 512], F32R), sb("xsL", [P, 2, 512], F32R)
        x2H, x2L = sb("x2H", [P, 512], F32R), sb("x2L", [P, 512], F32R)
        x2r = sb("x2r", [P, T, P])
        yo = sb("yo", [P, T, P])
        x_in = sb("x_in", [P, T, P])
        xb = sb("xb", [P, T, P])
        ctx_in = sb("ctx_in", [LC, T, DC])
        xT = sb("xT", [P, T, PADT])
        late = sb("late", [P, NQ * T * PADT])
        Kq = late[:, :].rearrange("p (g b t) -> p g b t", g=NQ, b=T)
        Pt = late[:, :].rearrange("p (s g j k) -> p s g j k", s=2, g=NQ, j=NBLK)
        qv = sb("qv", [P, T * NBLK * BLK])
        Qr = qv[:, :].rearrange("p (b j k) -> p b j k", b=T, j=NBLK)
        vH, vL = sb("vH", [P, TOK], F32R), sb("vL", [P, TOK], F32R)
        qo = sb("qo", [P, (2 * SBLK + T) * P])
        Qbd = qo[:, 0:2 * SBLK * P].rearrange("p (b j h k) -> p b j h k", b=2, j=SBLK, h=QUAD)
        Qbd_last = qo[:, 2 * SBLK * P:].rearrange("p (b h k) -> p b h k", b=T, h=QUAD)
        oL = qo[:, 0:TOK].rearrange("p (b c) -> p b c", b=T)
        oA = qo[:, TOK:2 * TOK].rearrange("p (b c) -> p b c", b=T)
        o5 = qo[:, 2 * TOK:3 * TOK].rearrange("p (b c) -> p b c", b=T)
        oT = qo[:, 3 * TOK:3 * TOK + T * PADT].rearrange("p (b t) -> p b t", b=T)
        big = sb("big", [P, T * NQ * NBLK * BLK])
        S = big[:, :].rearrange("p (b g j k) -> p b g j k", b=T, g=NQ, j=NBLK)
        Vbd = [sb("Vbd", [P, 2, HEADS, VW])[:, :, :, :],
               qv[:, 0:2 * HEADS * VW].rearrange("p (s h w) -> p s h w", s=2, h=HEADS)]
        V5 = sb("V5", [P, T, HEADS, HD + 1])
        ctxT = sb("ctxT", [DC, T * LC])
        KxT = sb("KxT", [P, T, LC])
        at = 0
        views = []
        for width in (TOK, TOK, T * LC, TOK, TOK, TOK, TOK, TOK, TOK):
            views.append(big[:, at:at + width])
            at += width + width % 2
        assert at <= T * NQ * NBLK * BLK
        x1T, QxT = views[0], views[1].rearrange("p (b t) -> p b t", b=T)
        Px = views[2].rearrange("p (b k) -> p b k", b=T)
        PxT = views[3][0:LC, :].rearrange("p (b t) -> p b t", b=T)
        r1, r2, x1 = (views[n].rearrange("p (b d) -> p b d", b=T) for n in (4, 5, 6))
        x2T = views[7]
        Vx = views[8][0:LC, :].rearrange("p (b d) -> p b d", b=T)
        x2 = sb("x2", [P, T, P])
        cst_in = big[:, 0:C_ALL - C_KEEP]
        smax = sb("smax", [P, SBLK * NQ])
        rsum = smax[:, :].rearrange("p (s h) -> p s h", s=2)
        bst = sb("bst", [P, T, 6])
        pause = sb("pause", [P, 1])
        mv = sb("mv", [P, T, 2])
        vareps = sb("vareps", [P, T])
        rstd = sb("rstd", [P, T])
        bst3, mv3 = sb("bst3", [P, T, 6]), sb("mv3", [P, T, 2])
        vareps3, rstd3 = sb("vareps3", [P, T]), sb("rstd3", [P, T])
        xmax, xsum, xrec = sb("xmax", [P, T]), sb("xsum", [P, T]), sb("xrec", [P, T])
        lg = sb("lg", [P, 2 * T, E])
        lmax, lsum, lrec = (sb(n, [P, 2 * T]) for n in ("lmax", "lsum", "lrec"))
        cw = sb("cw", [P, T, E])
        csum, crec = sb("csum", [P, T]), sb("crec", [P, T])

        params_in = sem("params_in")
        piece_in = [sem(f"piece_in{n}") for n in range(4)]
        x_loaded, ctx_loaded, out_stored = sem("x_loaded"), sem("ctx_loaded"), sem("out_stored")
        dve_setup, pe_bias, bias_ready, act_setup = sem("dve_setup"), sem("pe_bias"), sem("bias_ready"), sem("act_setup")
        piece_hi, piece_lo = sem("piece_hi"), sem("piece_lo")
        pair_done = [sem("pair_done0"), sem("pair_done1")]
        xT_ready, q_ready, k_ready, xb_ready = sem("xT_ready"), sem("q_ready"), sem("k_ready"), sem("xb_ready")
        qbd_ready, qlast_ready, vH_ready, vL_ready = sem("qbd_ready"), sem("qlast_ready"), sem("vH_ready"), sem("vL_ready")
        ctxT_ready, kx_ready, vx_ready = sem("ctxT_ready"), sem("kx_ready"), sem("vx_ready")
        s_ready, p_ready, pt_ready = sem("s_ready"), sem("p_ready"), sem("pt_ready")
        v_ready, v5_ready, av_read = sem("v_ready"), sem("v5_ready"), sem("av_read")
        oTl_ready, oT_ready = sem("oTl_ready"), sem("oT_ready")
        var_ready, rstd_ready = sem("var_ready"), sem("rstd_ready")
        x1_ready, x1b_ready, x1T_ready, qx_ready = sem("x1_ready"), sem("x1b_ready"), sem("x1T_ready"), sem("qx_ready")
        sx_ready, ex_ready, pxT_ready = sem("sx_ready"), sem("ex_ready"), sem("pxT_ready")
        x2_ready, x2T_ready, lg_ready, elg_ready, cw_ready = (sem(n) for n in (
            "x2_ready", "x2T_ready", "lg_ready", "elg_ready", "cw_ready"))
        x2H_ready, x2L_ready, x2r_ready = sem("x2H_ready"), sem("x2L_ready"), sem("x2r_ready")
        xs_ready, xsT_done, xsH_ready, xsL_ready = sem("xs_ready"), sem("xsT_done"), sem("xsH_ready"), sem("xsL_ready")
        gate_done, up_done, down_done = sem("gate_done"), sem("up_done"), sem("down_done")
        silu_ready, h_ready, hH_ready, hL_ready = sem("silu_ready"), sem("h_ready"), sem("hH_ready"), sem("hL_ready")
        yT_ready, yt_done, r3_ready, var3_ready, rstd3_ready, out_ready = (sem(n) for n in (
            "yT_ready", "yt_done", "r3_ready", "var3_ready", "rstd3_ready", "out_ready"))
        att_link, ffn_link, setup_link = sem("att_link"), sem("ffn_link"), sem("setup_link")

        def done_at(name, g):
            return g * DONE_PER + DONE_AT[name]

        def walk(run_ffn, run_att):
            for n in range(NCH):
                for place in range(3):
                    if run_ffn:
                        run_ffn(n, place)
                    if run_att:
                        for name, *args in STEPS[n][place]:
                            run_att(name, args)
                if not run_ffn and n < PIECES:
                    run_att("piece", (n,))

        def tokens(view, j):
            if j < NLOC:
                return view[..., BLK * j:BLK * (j + 1)]
            v = view.rearrange("p b (i r) -> p b r i", r=DIL) if len(view.shape) == 3 else \
                view.rearrange("p (i r) -> p r i", r=DIL)
            if j < NLOC + DIL:
                return v[..., j - NLOC, 0:BLK]
            r = j - NLOC - DIL
            return v[..., r:r + 2, BLK:BLK + CHUNK]

        block = stack.enter_context(nc.Block())

        @block.sync
        def _(sp):
            for dst, src in ((cs[:, :], cst[:, 0:C_KEEP]), (cst_in, cst[:, C_KEEP:C_ALL]),
                             (cols[:, 0:1], bq), (cols[:, 1:2], bk), (cols[:, 2:3], bv),
                             (cols[:, 3:4], bxq), (cols[:, 4:5], bxk)):
                if len(src.shape) == 1:
                    src = src.rearrange("(p a) -> p a", a=1)
                sp.dma_start(dst, src).then_inc(params_in, 16)

            def load(g, first=False):
                if not first:
                    sp.wait_ge(pair_done[PAIR["xt"]], done_at("xt", g - 1))
                    sp.wait_ge(xb_ready, 2 * (g - 1) + 1)
                sp.dma_start(x_in[:, :, :], x[bass.ds(g * T, T)].rearrange("b t d -> t b d")).then_inc(x_loaded, 16)
                sp.dma_start(ctx_in[:, :, :], ctx[bass.ds(g * T, T)].rearrange("b t d -> t b d")).then_inc(ctx_loaded, 16)

            def store(f):
                sp.wait_ge(out_ready, f + 1)
                sp.dma_start(out[bass.ds(f * T, T)].rearrange("b t d -> t b d"), yo[:, :, :]).then_inc(out_stored, 16)

            sp.sem_inc(out_stored, 16)
            load(0, first=True)
            for n in range(PIECES):
                if n >= 4:
                    sp.wait_ge(piece_lo, n - 3)
                m, e = n // E, n % E
                src = w_gate[e] if m == 0 else w_up[e] if m == 1 else w_down[e].rearrange("(c p) n -> p c n", p=P)
                dst = sh[:, n % 4, :] if m < 2 else sh[:, n % 4, :].rearrange("p (c n) -> p c n", c=FC)
                sp.dma_start(dst, src).then_inc(piece_in[n % 4], 16)
            load(1)
            with sp.Fori(1, G - 1) as i:
                load(i + 1)
                store(i - 1)
            store(G - 2)
            store(G - 1)
            sp.wait_ge(out_stored, 16 * (G + 1))

        @block.tensor
        def _(pe):
            nc_pe = nc.tensor
            pe.wait_ge(params_in, 16 * 18)
            pe.wait_ge(dve_setup, 1)
            nc_pe.matmul(xs_ps[:, 0:P], bv2[:, 0:1].broadcast_to([P, P]), woT[:, :], start=True, stop=False)
            nc_pe.matmul(xs_ps[:, 0:P], ones[:, :], rows[:, 0:P], start=False, stop=True)
            nc_pe.matmul(xs_ps[:, P:2 * P], ones[:, :], rows[:, P:2 * P], start=True, stop=True).then_inc(pe_bias, 1)
            pe.wait_ge(bias_ready, 1)

            def run_att(g, first=False):
                def scores(bank, operands):
                    nc_pe.matmul(bank, mrow[0:2, :], mcol[0:2, :], start=True, stop=False)
                    for n, (q, k) in enumerate(operands):
                        ins = nc_pe.matmul(bank[:, n * P:(n + 1) * P], q, k, start=False, stop=(n == len(operands) - 1))
                    return ins

                def transposes(t, src, n_out):
                    for b in range(T):
                        s = src[:, b, :]
                        k = s.shape[0]
                        ins = nc_pe.transpose(t[0:n_out, 0, b * k:(b + 1) * k], s, ident[0:k, 0:k])
                    return ins

                def step(name, args):
                    if name == "xt":
                        pe.wait_ge(x_loaded, 16 * g + 16)
                        pe.wait_ge(ctx_loaded, 16 * g + 16)
                        t = pair[PAIR["xt"]]
                        for b in range(T):
                            nc_pe.transpose(t[:, 0, b * P:(b + 1) * P], x_in[:, b, :], ident)
                        for b in range(T):
                            ins = nc_pe.transpose(t[0:DC, 1, b * LC:(b + 1) * LC], ctx_in[:, b, :],
                                                  ident[0:LC, 0:LC])
                        ins.then_inc(pair_done[PAIR["xt"]], 1)
                    elif name == "qk":
                        pe.wait_ge(xT_ready, g + 1)
                        pe.wait_ge(lg_ready, g)
                        t = pair[PAIR["qk"]]
                        src = xT[:, :, 0:P]
                        nc_pe.matmul(t[:, 0, :], wqT[:, :], src, start=True, stop=True)
                        nc_pe.matmul(t[:, 1, :], wkT[:, :], src, start=True, stop=True).then_inc(pair_done[PAIR["qk"]], 1)
                    elif name == "sc":
                        b, half = args
                        nm = f"sc{b}"
                        if half == 0:
                            pe.wait_ge(qbd_ready, T * g + b + 1)
                            if b == 0:
                                pe.wait_ge(vL_ready, g + 1)
                                pe.wait_ge(ctxT_ready, g + 1)
                            pe.wait_ge(s_ready, (T + 1) * g + b)
                        ins = scores(pair[PAIR[nm]][:, half, :],
                                     [(Qbd[:, b % 2, k], tokens(Kq[:, :, b, :], k))
                                      for k in range(NLOC * half, NLOC * (half + 1))])
                        if half == 1:
                            ins.then_inc(pair_done[PAIR[nm]], 1)
                    elif name == "sc_last":
                        pe.wait_ge(qlast_ready, g + 1)
                        pe.wait_ge(k_ready, g + 1)
                        pe.wait_ge(q_ready, g + 1)
                        scores(pair[PAIR["sc_last"]][:, 0, :],
                               [(Qbd_last[:, b], tokens(Kq[:, :, b, :], NBLK - 1)) for b in range(T)])\
                            .then_inc(pair_done[PAIR["sc_last"]], 1)
                    elif name == "vn":
                        t = pair[PAIR["vn"]]
                        for b in range(T):
                            ins = nc_pe.matmul(t[:, 0, b * P:(b + 1) * P], xT[:, b, 0:P], wvT[:, :],
                                               start=True, stop=True)
                        ins.then_inc(pair_done[PAIR["vn"]], 1)
                    elif name == "vr":
                        b, which = args
                        nm = f"vr{b}{which}"
                        pe.wait_ge(vH_ready, g + 1)
                        pe.wait_ge(vL_ready, g + 1)
                        if b == 0:
                            pe.wait_ge(s_ready, (T + 1) * g + (T if which == "L" else T + 1))
                        else:
                            pe.wait_ge(av_read, AV_PER * g + (4 if which == "L" else 5))
                        t = pair[PAIR[nm]]
                        for k in range(NLOC):
                            w = sel[:, k + NLOC * "LA".index(which), :]
                            dst = t[:, k // 2, (k % 2) * 2 * P:(k % 2 + 1) * 2 * P]
                            nc_pe.matmul(dst, w, vH[:, b * P:(b + 2) * P], start=True, stop=False)
                            ins = nc_pe.matmul(dst, w, vL[:, b * P:(b + 2) * P], start=False, stop=True)
                        ins.then_inc(pair_done[PAIR[nm]], 1)
                    elif name == "v5":
                        pe.wait_ge(v_ready, T * g + 1)
                        t = pair[PAIR["v5"]]
                        nc_pe.matmul(t[:, 0, :], sel[:, NBLK - 1, :], vH[:, :], start=True, stop=False)
                        nc_pe.matmul(t[:, 0, :], sel[:, NBLK - 1, :], vL[:, :], start=False, stop=True)\
                            .then_inc(pair_done[PAIR["v5"]], 1)
                    elif name == "av":
                        b, which = args
                        pe.wait_ge(pt_ready, T * g + b + 1)
                        pe.wait_ge(v_ready, T * g + 2 * (b // 2) + 2)
                        if (b, which) == (0, "A"):
                            pe.wait_ge(v5_ready, g + 1)
                        elif which == "A" or b % 2:
                            pe.wait_ge(av_read, AV_PER * g + 3 * b + (-1 if which == "L" else 0))
                        t = pair[PAIR[f"av{b}{which}"]]
                        s = "LA".index(which)
                        for q in range(NQ):
                            ins = nc_pe.matmul(t[:, q // 2, (q % 2) * QUAD * VW:(q % 2 + 1) * QUAD * VW],
                                               Pt[:, b % 2, q, NLOC * s:NLOC * (s + 1), :],
                                               Vbd[b % 2][:, s, QUAD * q:QUAD * (q + 1), :], start=True, stop=True)
                        ins.then_inc(pair_done[PAIR[f"av{b}{which}"]], 1)
                    elif name == "av5":
                        b, = args
                        if b == 1:
                            pe.wait_ge(v_ready, T * g + 3)
                        else:
                            pe.wait_ge(av_read, AV_PER * g + 3 * b + 1)
                        t = pair[PAIR[f"av{b}5"]]
                        w = QUAD * (HD + 1)
                        for q in range(NQ):
                            ins = nc_pe.matmul(t[0:BLK, 0, q * w:(q + 1) * w], Pt[:, b % 2, q, NBLK - 1, :],
                                               V5[:, b, QUAD * q:QUAD * (q + 1), :], start=True, stop=True)
                        ins.then_inc(pair_done[PAIR[f"av{b}5"]], 1)
                    elif name == "ot":
                        pe.wait_ge(av_read, AV_PER * g + AV_PER)
                        t = pair[PAIR["ot"]]
                        for s, o in enumerate((oL, oA)):
                            for b in range(T):
                                ins = nc_pe.transpose(t[:, s, b * P:(b + 1) * P], o[:, b, :], ident)
                        ins.then_inc(pair_done[PAIR["ot"]], 1)
                    elif name == "ot5":
                        pe.wait_ge(kx_ready, g + 1)
                        pe.wait_ge(vx_ready, g + 1)
                        t = pair[PAIR["ot5"]]
                        for b in range(T):
                            ins = nc_pe.transpose(t[:, 0, b * P:(b + 1) * P], o5[:, b, :], ident)
                        ins.then_inc(pair_done[PAIR["ot5"]], 1)
                    elif name == "kv":
                        pe.wait_ge(ctxT_ready, g + 1)
                        pe.wait_ge(av_read, AV_PER * g + AV_PER - 1)
                        t = pair[PAIR["kv"]]
                        nc_pe.matmul(t[:, 0, 0:T * LC], wxk[:, :], ctxT[:, :], start=True, stop=True)
                        for b in range(T):
                            ins = nc_pe.matmul(t[0:LC, 1, b * P:(b + 1) * P], ctxT[:, b * LC:(b + 1) * LC],
                                               wxv[:, :], start=True, stop=True)
                        ins.then_inc(pair_done[PAIR["kv"]], 1)
                    elif name == "wo":
                        pe.wait_ge(oT_ready, g + 1)
                        t = pair[PAIR["wo"]]
                        for b in range(T):
                            ins = nc_pe.matmul(t[:, 0, b * P:(b + 1) * P], oT[:, b, 0:P], woT[:, :],
                                               start=True, stop=True)
                        ins.then_inc(pair_done[PAIR["wo"]], 1)
                    elif name == "x1t":
                        pe.wait_ge(x1_ready, g + 1)
                        t = pair[PAIR["x1t"]]
                        transposes(t, x1, P).then_inc(pair_done[PAIR["x1t"]], 1)
                    elif name == "qx":
                        pe.wait_ge(x1T_ready, g + 1)
                        t = pair[PAIR["qx"]]
                        nc_pe.matmul(t[:, 0, :], wxq[:, :], x1T, start=True, stop=True).then_inc(pair_done[PAIR["qx"]], 1)
                    elif name == "sx":
                        pe.wait_ge(qx_ready, g + 1)
                        pe.wait_ge(kx_ready, g + 1)
                        t = pair[PAIR["sx"]]
                        for b in range(T):
                            ins = nc_pe.matmul(t[:, 0, b * LC:(b + 1) * LC], QxT[:, b, :], KxT[:, b, :],
                                               start=True, stop=True)
                        ins.then_inc(pair_done[PAIR["sx"]], 1)
                    elif name == "pt":
                        pe.wait_ge(ex_ready, g + 1)
                        t = pair[PAIR["pt"]]
                        transposes(t, Px, LC).then_inc(pair_done[PAIR["pt"]], 1)
                    elif name == "ax":
                        pe.wait_ge(pxT_ready, g + 1)
                        pe.wait_ge(vx_ready, g + 1)
                        t = pair[PAIR["ax"]]
                        for b in range(T):
                            ins = nc_pe.matmul(t[:, 0, b * P:(b + 1) * P], PxT[:, b, :], Vx[:, b, :],
                                               start=True, stop=True)
                        ins.then_inc(pair_done[PAIR["ax"]], 1)
                    elif name == "x2t":
                        pe.wait_ge(x2_ready, g + 1)
                        t = pair[PAIR["x2t"]]
                        transposes(t, x2, P).then_inc(pair_done[PAIR["x2t"]], 1)
                    elif name == "rt":
                        pe.wait_ge(x2T_ready, g + 1)
                        t = pair[PAIR["rt"]]
                        for b in range(T):
                            ins = nc_pe.matmul(t[:, 0, b * 2 * E:(b + 1) * 2 * E], x2T[:, b * P:(b + 1) * P],
                                               wrg[:, :], start=True, stop=True)
                        ins.then_inc(pair_done[PAIR["rt"]], 1)
                return step

            def scaled_tokens(f, e):
                pe.wait_ge(xs_ready, E * f + e + 1)
                for b in range(T):
                    ins = nc_pe.transpose(xs_ps[:, b * P:(b + 1) * P], xs[:, b, :], ident)
                ins.then_inc(xsT_done, 1)

            def three(dst, w, a, rh, rl, start, stop):
                nc_pe.matmul(dst, wH[(slice(None), *w)][:, a:a + P], rh, start=start, stop=False)
                nc_pe.matmul(dst, wH[(slice(None), *w)][:, a:a + P], rl, start=False, stop=False)
                return nc_pe.matmul(dst, wL[(slice(None), *w)][:, a:a + P], rh, start=False, stop=stop)

            def down(f, n):
                pe.wait_ge(hH_ready, NCH * f + n + 1)
                pe.wait_ge(hL_ready, NCH * f + n + 1)
                e, c = n // FC, n % FC
                three(y_ps[:, :], (2, e), c * P, hH[:, n % 2, :], hL[:, n % 2, :],
                      n == 0, n == NCH - 1).then_inc(down_done, 1)

            def transpose_y(f):
                pe.wait_ge(yT_ready, f + 1)
                for b in range(T):
                    ins = nc_pe.transpose(y_ps[:, b * P:(b + 1) * P], yo[:, b, :], ident)
                ins.then_inc(yt_done, 1)

            def run_ffn(f, before, after):
                def chunk(n, place):
                    e, c = n // FC, n % FC
                    if place == 0:
                        if n == 0:
                            pe.wait_ge(x2H_ready, f + 1)
                            pe.wait_ge(x2L_ready, f + 1)
                        if c == 3:
                            pe.wait_ge(xsH_ready, E * f + e + (1 if e + 1 == E and after is None else 2))
                            pe.wait_ge(xsL_ready, E * f + e + (1 if e + 1 == E and after is None else 2))
                        elif c == 2:
                            pe.wait_ge(silu_ready, NCH * f + n)
                        elif n >= 1 or before is not None:
                            pe.wait_ge(h_ready, NCH * f + n - 1)
                        three(ring[GATE_BANK[c]][:, :], (0, e), c * P, x2H[:, :], x2L[:, :], True, True)\
                            .then_inc(gate_done, 1)
                    elif place == 1:
                        if c == 0:
                            pe.wait_ge(xsH_ready, E * f + e + 1)
                            pe.wait_ge(xsL_ready, E * f + e + 1)
                        if c == 2:
                            pe.wait_ge(h_ready, NCH * f + n)
                        else:
                            pe.wait_ge(silu_ready, NCH * f + n)
                        three(ring[UP_BANK[c]][:, :], (1, e), c * P, xsH[:, e % 2, :], xsL[:, e % 2, :], True, True)\
                            .then_inc(up_done, 1)
                        if n == 2 and before is not None:
                            transpose_y(before)
                        if n == 3:
                            pe.wait_ge(r3_ready, f)
                            down(f, 0)
                    else:
                        if n < 2 and before is not None:
                            down(before, NCH - 2 + n)
                        elif n >= 3:
                            down(f, n - 2)
                        if c == 1:
                            pe.wait_ge(h_ready, NCH * f + n)
                            if e + 1 < E:
                                scaled_tokens(f, e + 1)
                            elif after is not None:
                                scaled_tokens(after, 0)
                return chunk

            walk(None, run_att(0, first=True))
            scaled_tokens(0, 0)
            pe.wait_ge(piece_lo, PIECES)
            walk(run_ffn(0, None, 1), run_att(1))
            with pe.Fori(2, G) as i:
                walk(run_ffn(i - 1, i - 2, i), run_att(i))
            walk(run_ffn(G - 1, G - 2, None), None)
            down(G - 1, NCH - 2)
            down(G - 1, NCH - 1)
            transpose_y(G - 1)

        @block.scalar
        def _(act):
            sc = nc.scalar
            for dst, src in ((woT[:, :], WoT), (wqT[:, :], WqT), (wkT[:, :], WkT), (wvT[:, :], WvT),
                             (wxq[:, :], Wxq), (wxk[:, :], Wxk), (wxv[:, :], Wxv),
                             (wrg[:, 0:E], w_router), (wrg[:, E:2 * E], w_gating)):
                act.dma_start(dst, src).then_inc(params_in, 16)
            for n, src in enumerate((bo, bxv)):
                act.dma_start(rows[:, n * P:(n + 1) * P], src.rearrange("(a n) -> a n", a=1)).then_inc(params_in, 16)
            act.wait_ge(params_in, 16 * 18)
            act.wait_ge(dve_setup, 1)

            def run_att(g, first=False):
                def step(name, args):
                    if name == "xt":
                        act.wait_ge(pair_done[PAIR["xt"]], done_at("xt", g))
                        if not first:
                            act.wait_ge(pair_done[PAIR["vn"]], done_at("vn", g - 1))
                        t = pair[PAIR["xt"]]
                        sc.copy(xT[:, :, 0:P], t[:, 0, :].rearrange("p (b t) -> p b t", b=T)).then_inc(xT_ready, 1)
                        if not first:
                            act.wait_ge(pair_done[PAIR["kv"]], done_at("kv", g - 1))
                        ins = sc.copy(ctxT[:, :], t[0:DC, 1, 0:T * LC])
                        ins.then_inc(ctxT_ready, 1)
                    elif name == "qk":
                        act.wait_ge(pair_done[PAIR["qk"]], done_at("qk", g))
                        act.wait_ge(qbd_ready, T * g)
                        act.wait_ge(qlast_ready, g)
                        if not first:
                            act.wait_ge(pair_done[PAIR["av3A"]], done_at("av3A", g - 1))
                        src = pair[PAIR["qk"]][:, 0, :].rearrange("p (b t) -> p b t", b=T)
                        sc.activation(Qr[:, :, 0:NLOC, :].rearrange("p b j k -> p b (j k)"), src,
                                      ACT.Identity, bias=cols[:, 0:1])
                        sc.activation(Qr[:, :, NLOC:NLOC + DIL, :],
                                      src[:, :, 0:DIL * BLK].rearrange("p b (k r) -> p b r k", r=DIL),
                                      ACT.Identity, bias=cols[:, 0:1])
                        for j in (NBLK - 2, NBLK - 1):
                            for half in range(2):
                                own = [t for t in block_tokens(j)[half * CHUNK:(half + 1) * CHUNK] if t < P]
                                ins = sc.activation(Qr[:, :, j, half * CHUNK:half * CHUNK + len(own)],
                                                    src[:, :, own[0]:own[-1] + 1:DIL], ACT.Identity,
                                                    bias=cols[:, 0:1])
                        ins.then_inc(q_ready, 1)
                    elif name == "vn":
                        act.wait_ge(pair_done[PAIR["vn"]], done_at("vn", g))
                        if not first:
                            act.wait_ge(pair_done[PAIR["vr2A"]], done_at("vr2A", g - 1))
                        sc.copy(vH[:, :], pair[PAIR["vn"]][:, 0, :]).then_inc(vH_ready, 1)
                    elif name == "exps":
                        first_b, = args
                        for b in range(first_b, first_b + 2):
                            act.wait_ge(s_ready, (T + 1) * g + b + 2)
                            v = S[:, b].rearrange("p g j k -> p (g j k)")
                            sc.activation(v, v, ACT.Exp, scale=SELF_SCALE).then_inc(p_ready, 1)
                    elif name == "ot":
                        act.wait_ge(pair_done[PAIR["ot"]], done_at("ot", g))
                        if not first:
                            act.wait_ge(pair_done[PAIR["wo"]], done_at("wo", g - 1))
                        sc.copy(oT[:, :, 0:P], pair[PAIR["ot"]][:, 0, :].rearrange("p (b t) -> p b t", b=T))\
                            .then_inc(oTl_ready, 1)
                    elif name == "kv":
                        act.wait_ge(pair_done[PAIR["kv"]], done_at("kv", g))
                        if not first:
                            act.wait_ge(pair_done[PAIR["sx"]], done_at("sx", g - 1))
                        sc.activation(KxT[:, :, :], pair[PAIR["kv"]][:, 0, 0:T * LC].rearrange("p (b k) -> p b k", b=T),
                                      ACT.Identity, bias=cols[:, 4:5]).then_inc(kx_ready, 1)
                        act.wait_ge(pt_ready, T * g + T)
                        sc.copy(Vx, pair[PAIR["kv"]][0:LC, 1, :].rearrange("p (b d) -> p b d", b=T))\
                            .then_inc(vx_ready, 1)
                    elif name == "x1t":
                        act.wait_ge(pair_done[PAIR["x1t"]], done_at("x1t", g))
                        act.wait_ge(pt_ready, T * g + T)
                        sc.copy(x1T, pair[PAIR["x1t"]][:, 0, :]).then_inc(x1T_ready, 1)
                    elif name == "qx":
                        act.wait_ge(pair_done[PAIR["qx"]], done_at("qx", g))
                        sc.activation(QxT, pair[PAIR["qx"]][:, 0, :].rearrange("p (b t) -> p b t", b=T),
                                      ACT.Identity, bias=cols[:, 3:4]).then_inc(qx_ready, 1)
                    elif name == "ex":
                        act.wait_ge(sx_ready, g + 1)
                        sc.activation(Px, Px, ACT.Exp, scale=CROSS_SCALE).then_inc(ex_ready, 1)
                    elif name == "pt":
                        act.wait_ge(pair_done[PAIR["pt"]], done_at("pt", g))
                        sc.copy(PxT, pair[PAIR["pt"]][0:LC, 0, :].rearrange("p (b t) -> p b t", b=T))\
                            .then_inc(pxT_ready, 1)
                    elif name == "x2t":
                        act.wait_ge(pair_done[PAIR["x2t"]], done_at("x2t", g))
                        sc.copy(x2T, pair[PAIR["x2t"]][:, 0, :]).then_inc(x2T_ready, 1)
                    elif name == "cw":
                        act.wait_ge(lg_ready, g + 1)
                        v = lg[:, :, :].rearrange("p (b s) e -> p b s e", s=2)
                        sc.activation(v[:, :, 0, :], v[:, :, 0, :], ACT.Exp)
                        sc.activation(v[:, :, 1, :], v[:, :, 1, :], ACT.Exp, scale=10.0).then_inc(elg_ready, 1)
                    elif name == "piece":
                        n, = args
                        act.wait_ge(piece_in[n % 4], 16 * (n // 4 + 1))
                        sc.copy(wH[:, n // E, n % E, :], sh[:, n % 4, :]).then_inc(piece_hi, 1)
                return step

            def high(f, n, first=False):
                act.wait_ge(h_ready, NCH * f + n + 1)
                if n or not first:
                    act.wait_ge(down_done, NCH * f + n - 1)
                sc.copy(hH[:, n % 2, :], sh[:, n % 4, :]).then_inc(hH_ready, 1)

            def scaled_high(f, e, first=False):
                act.wait_ge(xsT_done, E * f + e + 1)
                if not first:
                    act.wait_ge(up_done, NCH * f + FC * (e - 1))
                sc.copy(xsH[:, e % 2, :], xs_ps[:, :]).then_inc(xsH_ready, 1)

            def tokens_high(g, first=False):
                act.wait_ge(x2T_ready, g + 1)
                if not first:
                    act.wait_ge(gate_done, NCH * g)
                sc.copy(x2H[:, :], x2T).then_inc(x2H_ready, 1)

            def take_y(f):
                act.wait_ge(down_done, NCH * f + NCH)
                act.wait_ge(out_stored, 16 * (f + 1))
                sc.copy(yo[:, :, :].rearrange("p b d -> p (b d)"), y_ps[:, :]).then_inc(yT_ready, 1)

            def run_ffn(f, before, after):
                def chunk(n, place):
                    if place:
                        return
                    if n % FC == 2:
                        if n // FC + 1 < E:
                            scaled_high(f, n // FC + 1)
                        elif after is not None:
                            scaled_high(after, 0)
                    if n == 2 and before is not None:
                        take_y(before)
                    act.wait_ge(gate_done, NCH * f + n + 1)
                    if n == NCH - 1 and after is not None:
                        tokens_high(after)
                    if n >= 4 or before is not None:
                        act.wait_ge(hL_ready, NCH * f + n - 3)
                    sc.activation(sh[:, n % 4, :], ring[GATE_BANK[n % FC]][:, :], ACT.Silu).then_inc(silu_ready, 1)
                    if n == 0 and before is not None:
                        high(before, NCH - 1)
                    if n >= 1:
                        high(f, n - 1, first=before is None)
                    if n == 4:
                        act.wait_ge(r3_ready, f)
                        act.wait_ge(x2_ready, f + 1)
                        sc.copy(x2r[:, :, :], x2[:, :, :]).then_inc(x2r_ready, 1)
                return chunk

            act.wait_ge(pe_bias, 1)
            sc.copy(bias_o[:, :], xs_ps[:, 0:P])
            sc.copy(bias_x[:, :], xs_ps[:, P:2 * P]).then_inc(bias_ready, 1)
            walk(None, run_att(0, first=True))
            tokens_high(0, first=True)
            scaled_high(0, 0, first=True)
            walk(run_ffn(0, None, 1), run_att(1))
            with act.Fori(2, G) as i:
                walk(run_ffn(i - 1, i - 2, i), run_att(i))
            walk(run_ffn(G - 1, G - 2, None), None)
            high(G - 1, NCH - 1)
            take_y(G - 1)

        @block.vector
        def _(dve):
            ve = nc.vector
            links = [0, 0]

            def link(ins, s, base):
                which = 1 if s is ffn_link else 0
                links[which] += 1
                ins.then_inc(s, 1)
                dve.wait_ge(s, base + links[which])

            ve.memset(xT[:, :, P:PADT], 0.0)
            ve.memset(qv[:, :], 0.0)
            ve.memset(ones[:, :], 1.0)
            ve.memset(minus_half[:, :], -0.5)
            dve.wait_ge(params_in, 16 * 18)
            ve.tensor_copy(mrow[:, :], cst_in[:, C_MROW - C_KEEP:C_MROW - C_KEEP + P])
            ve.tensor_copy(mcol[:, :], cst_in[:, C_MCOL - C_KEEP:C_MCOL - C_KEEP + BANK])
            ve.tensor_copy(sel[:, :, :], cst_in[:, C_SEL - C_KEEP:].rearrange("p (j m) -> p j m", j=NBLK))
            ve.tensor_scalar(bv2[:, :], cols[:, 2:3], 2.0, None, ALU.mult)
            ve.tensor_scalar(bkq[:, :], headv[:, 0:NQ], cols[:, 1:2], None, ALU.mult)
            for s in range(2):
                ve.tensor_copy(Vbd[0][:, s, :, VW - 1], headv)
            ve.tensor_copy(V5[:, :, :, HD], headv.unsqueeze(1).broadcast_to([P, T, HEADS])).then_inc(dve_setup, 1)

            def stats(r, st, m, ve_out, do_link, base, s):
                for b in range(T):
                    ins = ve.bn_stats(st[:, b, :], r[:, b, :])
                do_link(ins, s, base)
                ve.memset(pause[:, :], 0.0)
                for b in range(T):
                    ins = ve.bn_aggr(m[:, b, :], st[:, b, :])
                do_link(ins, s, base)
                return ve.tensor_scalar(ve_out[:, :], m[:, :, 1], EPS, None, ALU.add)

            def normalise(dst, r, m, rs):
                for b in range(T):
                    ins = ve.tensor_scalar(dst[:, b, :], r[:, b, :], m[:, b, 0:1], rs[:, b:b + 1],
                                           ALU.subtract, ALU.mult)
                return ins

            def run_att(g, first=False):
                base = g * DVE_ATT_LINKS

                def lk(ins):
                    link(ins, att_link, base)

                def step(name, args):
                    if name == "qk":
                        dve.wait_ge(pair_done[PAIR["qk"]], done_at("qk", g))
                        if not first:
                            dve.wait_ge(pair_done[PAIR["av35"]], done_at("av35", g - 1))
                        for q in range(2):
                            ve.tensor_scalar(Kq[:, q, :, 0:P],
                                             pair[PAIR["qk"]][:, 1, :].rearrange("p (b t) -> p b t", b=T),
                                             headv[:, q:q + 1], bkq[:, q:q + 1], ALU.mult, ALU.add)
                    elif name == "k2":
                        for q in range(2, NQ):
                            ve.tensor_scalar(Kq[:, q, :, 0:P],
                                             pair[PAIR["qk"]][:, 1, :].rearrange("p (b t) -> p b t", b=T),
                                             headv[:, q:q + 1], bkq[:, q:q + 1], ALU.mult, ALU.add)
                        ve.tensor_copy(Kq[:, :, :, P:PADT],
                                       bkq[:, :].unsqueeze(2).unsqueeze(3).broadcast_to([P, NQ, T, PADT - P]))\
                            .then_inc(k_ready, 1)
                    elif name == "vn":
                        dve.wait_ge(vH_ready, g + 1)
                        ve.tensor_tensor(vL[:, :], pair[PAIR["vn"]][:, 0, :], vH[:, :].bitcast(F32), ALU.subtract)\
                            .then_inc(vL_ready, 1)
                    elif name == "sc" and args[1] == 1:
                        b, _ = args
                        nm = f"sc{b}"
                        dve.wait_ge(pair_done[PAIR[nm]], done_at(nm, g))
                        v = pair[PAIR[nm]][:, :, :].rearrange("p a (j q k) -> p (a j) q k", q=NQ, k=BLK)
                        m = smax[:, :].rearrange("p (j q) -> p j q", q=NQ)
                        dve.wait_ge(s_ready, (T + 1) * g + b + 1)
                        lk(ve.tensor_reduce(m, v, AX, ALU.max))
                        ve.tensor_tensor(S[:, b].rearrange("p q j k -> p j q k")[:, 0:SBLK], v,
                                         m.unsqueeze(3).broadcast_to([P, SBLK, NQ, BLK]), ALU.subtract)\
                            .then_inc(s_ready, 1)
                    elif name == "sc_last":
                        dve.wait_ge(pair_done[PAIR["sc_last"]], done_at("sc_last", g))
                        v = pair[PAIR["sc_last"]][:, 0, :].rearrange("p (b q k) -> p b q k", b=T, q=NQ)
                        m = smax[:, 0:T * NQ].rearrange("p (b q) -> p b q", b=T)
                        dve.wait_ge(av_read, AV_PER * g)
                        lk(ve.tensor_reduce(m, v, AX, ALU.max))
                        dve.wait_ge(x2L_ready, g)
                        ve.tensor_tensor(S[:, :, :, NBLK - 1, :], v, m.unsqueeze(3).broadcast_to([P, T, NQ, BLK]),
                                         ALU.subtract).then_inc(s_ready, 1)
                    elif name == "vr":
                        b, which = args
                        nm, s = f"vr{b}{which}", "LA".index(which)
                        dve.wait_ge(pair_done[PAIR[nm]], done_at(nm, g))
                        if b:
                            dve.wait_ge(pair_done[PAIR[f"av1{which}"]], done_at(f"av1{which}", g))
                        elif not first:
                            dve.wait_ge(pair_done[PAIR[f"av3{which}"]], done_at(f"av3{which}", g - 1))
                        if (b, which) == (0, "L"):
                            dve.wait_ge(qbd_ready, T * g + T)
                            dve.wait_ge(qlast_ready, g + 1)
                            ve.tensor_copy(Vbd[1][:, :, :, VW - 1], headv.unsqueeze(1).broadcast_to([P, 2, HEADS]))
                        src = pair[PAIR[nm]][:, :, :].rearrange("p a (k b h d) -> p (a k) b h d", k=2, b=2, h=HEADS)
                        for half in range(2):
                            dst = Vbd[half][:, s, :, 0:VW - 1].rearrange("p h (k d) -> p k h d", k=NLOC)
                            ins = ve.tensor_tensor(dst, src[:, :, half],
                                                   headv.unsqueeze(1).unsqueeze(3).broadcast_to([P, NLOC, HEADS, HD]),
                                                   ALU.mult)
                        ins.then_inc(v_ready, 1)
                    elif name == "v5":
                        dve.wait_ge(pair_done[PAIR["v5"]], done_at("v5", g))
                        if not first:
                            dve.wait_ge(pair_done[PAIR["av35"]], done_at("av35", g - 1))
                        src = pair[PAIR["v5"]][:, 0, :].rearrange("p (b h d) -> p b h d", b=T, h=HEADS)
                        ve.tensor_tensor(V5[:, :, :, 0:HD], src,
                                         headv.unsqueeze(1).unsqueeze(3).broadcast_to([P, T, HEADS, HD]),
                                         ALU.mult).then_inc(v5_ready, 1)
                    elif name == "tr":
                        b, = args
                        dve.wait_ge(p_ready, T * g + b + 1)
                        if b == 0:
                            dve.wait_ge(pair_done[PAIR["sc3"]], done_at("sc3", g))
                        if b >= 2:
                            dve.wait_ge(pair_done[PAIR[f"av{b - 2}5"]], done_at(f"av{b - 2}5", g))
                        ve.transpose(Pt[:, b % 2].rearrange("p g j k -> p (g j k)"),
                                     S[:, b].rearrange("p g j k -> p (g j k)")).then_inc(pt_ready, 1)
                    elif name == "av":
                        b, which = args
                        nm = f"av{b}{which}"
                        dve.wait_ge(pair_done[PAIR[nm]], done_at(nm, g))
                        v = pair[PAIR[nm]][:, :, 0:2 * QUAD * VW].rearrange("p a (h c) -> p a h c", c=VW)
                        s = "LA".index(which)
                        rs = rsum[:, s, :].rearrange("p (a h) -> p a h", a=2)
                        if b == 0:
                            dve.wait_ge(s_ready, (T + 1) * g + T + 1)
                        dve.wait_ge(av_read, AV_PER * g + 3 * b)
                        lk(ve.reciprocal(rs, v[:, :, :, VW - 1]))
                        o = (oL if which == "L" else oA)[:, b, :].rearrange("p (a h d) -> p a h d", a=2, d=HD)
                        for k in range(NLOC):
                            q = slice(BLK * k, BLK * (k + 1))
                            ins = ve.tensor_tensor(o[q], v[q, :, :, HD * k:HD * (k + 1)],
                                                   rs[q].unsqueeze(3).broadcast_to([BLK, 2, HEADS // 2, HD]), ALU.mult)
                        ins.then_inc(av_read, 1)
                    elif name == "av5":
                        b, = args
                        nm = f"av{b}5"
                        dve.wait_ge(pair_done[PAIR[nm]], done_at(nm, g))
                        v = pair[PAIR[nm]][0:BLK, 0, 0:HEADS * (HD + 1)].rearrange("p (h c) -> p h c", c=HD + 1)
                        dve.wait_ge(av_read, AV_PER * g + 3 * b + 1)
                        lk(ve.reciprocal(rsum[0:BLK, 0, :], v[:, :, HD]))
                        ve.tensor_tensor(o5[0:BLK, b, :].rearrange("p (h d) -> p h d", d=HD), v[:, :, 0:HD],
                                         rsum[0:BLK, 0, :].unsqueeze(2).broadcast_to([BLK, HEADS, HD]), ALU.mult)\
                            .then_inc(av_read, 1)
                    elif name == "ot":
                        dve.wait_ge(oTl_ready, g + 1)
                        src = pair[PAIR["ot"]][:, 1, :].rearrange("p (b t) -> p b t", b=T)
                        dst = oT[:, :, :].rearrange("p b (i r) -> p b r i", r=DIL)
                        for r in range(DIL):
                            d = dst[:, :, r, 0:BLK]
                            ve.tensor_tensor(d, d, src[:, :, r * BLK:(r + 1) * BLK], ALU.add)
                        n_last = -(-(P - DIL * BLK - 1) // DIL)
                        for r in range(2):
                            d = dst[:, :, r, BLK:BLK + n_last]
                            ve.tensor_tensor(d, d, src[:, :, DIL * BLK + r * CHUNK:DIL * BLK + r * CHUNK + n_last],
                                             ALU.add)
                    elif name == "ot5":
                        dve.wait_ge(pair_done[PAIR["ot5"]], done_at("ot5", g))
                        src = pair[PAIR["ot5"]][:, 0, :].rearrange("p (b t) -> p b t", b=T)
                        n_last = (P - DIL * BLK - 2 + DIL - 1) // DIL
                        d = oT[:, :, :].rearrange("p b (i r) -> p b r i", r=DIL)[:, :, 2, BLK:BLK + n_last]
                        ve.tensor_tensor(d, d, src[:, :, CHUNK:CHUNK + n_last], ALU.add).then_inc(oT_ready, 1)
                    elif name == "wo":
                        dve.wait_ge(pair_done[PAIR["wo"]], done_at("wo", g))
                        dve.wait_ge(xb_ready, 2 * g + 1)
                        lk(ve.tensor_tensor(r1, pair[PAIR["wo"]][:, 0, :].rearrange("p (b d) -> p b d", b=T),
                                            xb[:, :, :], ALU.add))
                        stats(r1, bst, mv, vareps, link, base, att_link).then_inc(var_ready, 1)
                    elif name == "ln1":
                        dve.wait_ge(rstd_ready, 2 * g + 1)
                        normalise(x1, r1, mv, rstd).then_inc(x1_ready, 1)
                    elif name == "sx":
                        dve.wait_ge(pair_done[PAIR["sx"]], done_at("sx", g))
                        v = pair[PAIR["sx"]][:, 0, 0:T * LC].rearrange("p (b k) -> p b k", b=T)
                        lk(ve.tensor_reduce(xmax[:, :], v, AX, ALU.max))
                        ve.tensor_tensor(Px, v, xmax[:, :].unsqueeze(2).broadcast_to([P, T, LC]), ALU.subtract)\
                            .then_inc(sx_ready, 1)
                    elif name == "pt":
                        dve.wait_ge(ex_ready, g + 1)
                        lk(ve.tensor_reduce(xsum[:, :], Px, AX, ALU.add))
                        lk(ve.reciprocal(xrec[:, :], xsum[:, :]))
                    elif name == "ax":
                        dve.wait_ge(pair_done[PAIR["ax"]], done_at("ax", g))
                        dve.wait_ge(x1b_ready, g + 1)
                        for b in range(T):
                            ins = ve.scalar_tensor_tensor(r2[:, b, :], pair[PAIR["ax"]][:, 0, b * P:(b + 1) * P],
                                                          xrec[:, b:b + 1], xb[:, b, :], ALU.mult, ALU.add)
                        lk(ins)
                        stats(r2, bst, mv, vareps, link, base, att_link).then_inc(var_ready, 1)
                    elif name == "ln2":
                        dve.wait_ge(rstd_ready, 2 * g + 2)
                        if not first:
                            dve.wait_ge(pair_done[PAIR["x2t"]], done_at("x2t", g - 1))
                        dve.wait_ge(xs_ready, E * g)
                        dve.wait_ge(x2r_ready, g)
                        normalise(x2, r2, mv, rstd).then_inc(x2_ready, 1)
                    elif name == "rt":
                        dve.wait_ge(pair_done[PAIR["rt"]], done_at("rt", g))
                        v = pair[PAIR["rt"]][:, 0, 0:T * 2 * E].rearrange("p (s e) -> p s e", e=E)
                        lk(ve.tensor_reduce(lmax[:, :], v, AX, ALU.max))
                        ve.tensor_tensor(lg[:, :, :], v, lmax[:, :].unsqueeze(2).broadcast_to([P, 2 * T, E]),
                                         ALU.subtract).then_inc(lg_ready, 1)
                    elif name == "cw2":
                        dve.wait_ge(elg_ready, g + 1)
                        lk(ve.tensor_reduce(lsum[:, :], lg[:, :, :], AX, ALU.add))
                        lk(ve.reciprocal(lrec[:, :], lsum[:, :]))
                        lk(ve.tensor_tensor(lg[:, :, :], lg[:, :, :],
                                            lrec[:, :].unsqueeze(2).broadcast_to([P, 2 * T, E]), ALU.mult))
                        v = lg[:, :, :].rearrange("p (b s) e -> p b s e", s=2)
                        lk(ve.tensor_tensor(v[:, :, 0, :], v[:, :, 0, :], v[:, :, 1, :], ALU.mult))
                        lk(ve.tensor_reduce(csum[:, :], v[:, :, 0, :], AX, ALU.add))
                        lk(ve.tensor_scalar(csum[:, :], csum[:, :], 1e-9, None, ALU.add))
                        lk(ve.reciprocal(crec[:, :], csum[:, :]))
                        ve.tensor_tensor(cw[:, :, :], v[:, :, 0, :],
                                         crec[:, :].unsqueeze(2).broadcast_to([P, T, E]), ALU.mult).then_inc(cw_ready, 1)
                return step

            def scaled_low(f, e):
                dve.wait_ge(xsH_ready, E * f + e + 1)
                ve.tensor_tensor(xsL[:, e % 2, :], xs_ps[:, :], xsH[:, e % 2, :].bitcast(F32), ALU.subtract)\
                    .then_inc(xsL_ready, 1)

            def tokens_low(g):
                dve.wait_ge(x2H_ready, g + 1)
                ve.tensor_tensor(x2L[:, :], x2T, x2H[:, :].bitcast(F32), ALU.subtract).then_inc(x2L_ready, 1)

            def add_y(f):
                fb = f * DVE_FFN_LINKS
                links[1] = 0
                dve.wait_ge(yt_done, f + 1)
                dve.wait_ge(x2r_ready, f + 1)
                link(ve.tensor_tensor(yo[:, :, :], y_ps[:, :].rearrange("p (b d) -> p b d", b=T),
                                      x2r[:, :, :], ALU.add), ffn_link, fb)
                dve.sem_inc(r3_ready, 1)
                stats(yo, bst3, mv3, vareps3, link, fb, ffn_link).then_inc(var3_ready, 1)
                assert links[1] == DVE_FFN_LINKS, links

            def finish_y(f):
                dve.wait_ge(rstd3_ready, f + 1)
                normalise(yo, yo, mv3, rstd3).then_inc(out_ready, 1)

            def run_ffn(f, before, after):
                def chunk(n, place):
                    if n % FC == 2 and place == 0:
                        if n // FC + 1 < E:
                            scaled_low(f, n // FC + 1)
                        elif after is not None:
                            scaled_low(after, 0)
                    if place != 1:
                        return
                    if n == NCH - 1 and after is not None:
                        tokens_low(after)
                    dve.wait_ge(silu_ready, NCH * f + n + 1)
                    dve.wait_ge(up_done, NCH * f + n + 1)
                    ve.tensor_tensor(sh[:, n % 4, :], sh[:, n % 4, :], ring[UP_BANK[n % FC]][:, :], ALU.mult)\
                        .then_inc(h_ready, 1)
                    if n == 2 and before is not None:
                        add_y(before)
                    if n == 3 and before is not None:
                        finish_y(before)
                return chunk

            links[0] = 0
            walk(None, run_att(0, first=True))
            tokens_low(0)
            scaled_low(0, 0)
            assert links[0] == DVE_ATT_LINKS, links
            links[0] = 0
            walk(run_ffn(0, None, 1), run_att(1))
            links[0] = 0
            with dve.Fori(2, G) as i:
                walk(run_ffn(i - 1, i - 2, i), run_att(i))
            walk(run_ffn(G - 1, G - 2, None), None)
            add_y(G - 1)
            finish_y(G - 1)

        @block.gpsimd
        def _(pool):
            po = nc.gpsimd
            pool.wait_ge(bias_ready, 1)

            def run_att(g, first=False):
                def step(name, args):
                    if name == "xt":
                        pool.wait_ge(x_loaded, 16 * g + 16)
                        pool.wait_ge(x2_ready, g)
                        po.tensor_tensor(xb[:, :, :], x_in[:, :, :],
                                         bias_o[:, :].unsqueeze(1).broadcast_to([P, T, P]), ALU.add)\
                            .then_inc(xb_ready, 1)
                    elif name == "qe":
                        b, = args
                        pool.wait_ge(q_ready, g + 1)
                        if b >= 2:
                            pool.wait_ge(pair_done[PAIR[f"sc{b - 2}"]], done_at(f"sc{b - 2}", g))
                        else:
                            if not first:
                                pool.wait_ge(pair_done[PAIR["wo"]], done_at("wo", g - 1))
                        po.tensor_tensor(Qbd[:, b % 2], Qr[:, b, 0:SBLK].unsqueeze(2).broadcast_to([P, SBLK, QUAD, BLK]),
                                         headq.unsqueeze(1).unsqueeze(3).broadcast_to([P, SBLK, QUAD, BLK]),
                                         ALU.mult).then_inc(qbd_ready, 1)
                    elif name == "qe_last":
                        pool.wait_ge(q_ready, g + 1)
                        if not first:
                            pool.wait_ge(pair_done[PAIR["wo"]], done_at("wo", g - 1))
                        po.tensor_tensor(Qbd_last, Qr[:, :, NBLK - 1].unsqueeze(2).broadcast_to([P, T, QUAD, BLK]),
                                         headq.unsqueeze(1).unsqueeze(3).broadcast_to([P, T, QUAD, BLK]),
                                         ALU.mult).then_inc(qlast_ready, 1)
                    elif name == "pow1":
                        pool.wait_ge(var_ready, 2 * g + 1)
                        po.tensor_tensor(rstd[:, :], vareps[:, :], minus_half[:, :], ALU.pow).then_inc(rstd_ready, 1)
                    elif name == "x1t":
                        pool.wait_ge(x1_ready, g + 1)
                        po.tensor_tensor(xb[:, :, :], x1, bias_x[:, :].unsqueeze(1).broadcast_to([P, T, P]), ALU.add)\
                            .then_inc(x1b_ready, 1)
                        pool.wait_ge(x1b_ready, g + 1)
                        pool.sem_inc(xb_ready, 1)
                    elif name == "pow2":
                        pool.wait_ge(var_ready, 2 * g + 2)
                        po.tensor_tensor(rstd[:, :], vareps[:, :], minus_half[:, :], ALU.pow).then_inc(rstd_ready, 1)
                    elif name == "piece":
                        n, = args
                        pool.wait_ge(piece_hi, n + 1)
                        po.tensor_tensor(wL[:, n // E, n % E, :], sh[:, n % 4, :],
                                         wH[:, n // E, n % E, :].bitcast(F32), ALU.subtract).then_inc(piece_lo, 1)
                return step

            def scaled(f, e):
                pool.wait_ge(xsT_done, E * f + e)
                po.tensor_tensor(xs[:, :, :], x2[:, :, :], cw[:, :, e:e + 1].broadcast_to([P, T, P]), ALU.mult)\
                    .then_inc(xs_ready, 1)

            def low(f, n):
                pool.wait_ge(hH_ready, NCH * f + n + 1)
                po.tensor_tensor(hL[:, n % 2, :], sh[:, n % 4, :], hH[:, n % 2, :].bitcast(F32), ALU.subtract)\
                    .then_inc(hL_ready, 1)

            def raise_variance(f):
                pool.wait_ge(var3_ready, f + 1)
                po.tensor_tensor(rstd3[:, :], vareps3[:, :], minus_half[:, :], ALU.pow).then_inc(rstd3_ready, 1)

            def run_ffn(f, before, after):
                def chunk(n, place):
                    if place != (2 if 1 <= n <= 6 else 0):
                        return
                    if n == 0 and before is not None:
                        low(before, NCH - 1)
                    if n == NCH - 3 and after is not None:
                        pool.wait_ge(cw_ready, after + 1)
                        scaled(after, 0)
                    if n >= 1:
                        low(f, n - 1)
                    if n == 2 and before is not None:
                        raise_variance(before)
                    if n % FC == 2:
                        if n // FC + 2 < E:
                            scaled(f, n // FC + 2)
                        elif n // FC + 1 == E and after is not None:
                            scaled(after, 1)
                return chunk

            walk(None, run_att(0, first=True))
            pool.wait_ge(cw_ready, 1)
            scaled(0, 0)
            scaled(0, 1)
            walk(run_ffn(0, None, 1), run_att(1))
            with pool.Fori(2, G) as i:
                walk(run_ffn(i - 1, i - 2, i), run_att(i))
            walk(run_ffn(G - 1, G - 2, None), None)
            low(G - 1, NCH - 1)
            raise_variance(G - 1)


def kernel(**inputs):
    import concourse.bacc as bacc
    from concourse.bass_utils import run_bass_kernel_spmd

    names = {"x": "x", "ctx": "ctx_768", "bq": "L0_attn_bq", "bk": "L0_attn_bk", "bv": "L0_attn_bv",
             "bo": "L0_attn_bo", "Wxq": "L0_xattn_Wq", "Wxk": "L0_xattn_Wk", "Wxv": "L0_xattn_Wv",
             "bxq": "L0_xattn_bq", "bxk": "L0_xattn_bk", "bxv": "L0_xattn_bv",
             "w_router": "L0_ffn_w_router", "w_gating": "L0_ffn_w_gating", "w_gate": "L0_ffn_w_gate",
             "w_up": "L0_ffn_w_up", "w_down": "L0_ffn_w_down"}
    arrays = {k: np.ascontiguousarray(inputs[v]) for k, v in names.items()}
    for k in ("q", "k", "v", "o"):
        arrays[f"W{k}T"] = np.ascontiguousarray(np.asarray(inputs[f"L0_attn_W{k}"]).T)
    arrays["cst"] = constants()

    nc = bacc.Bacc("TRN2", target_bir_lowering=False, num_devices=1)
    aps = {k: nc.dram_tensor(f"in_{k}", a.shape, mybir.dt.from_np(a.dtype), kind="ExternalInput").ap()
           for k, a in arrays.items()}
    out = nc.dram_tensor("out", arrays["x"].shape, F32, kind="ExternalOutput").ap()
    build_decoder(nc, out=out, **aps)
    r = run_bass_kernel_spmd(nc, [{f"in_{k}": a for k, a in arrays.items()}], core_ids=[0])
    return r.results[0]["out"]
```
